# Optimizing a Trainium2 kernel written in Bass

```python
import numpy as np
import jax
import jax.numpy as jnp

def _softmax(x, axis=-1):
    return jax.nn.softmax(x, axis=axis)

def _gelu(x):
    return jax.nn.gelu(x, approximate=True)

def _silu(x):
    return jax.nn.silu(x)

def _sigmoid(x):
    return jax.nn.sigmoid(x)

def _layernorm(x, axis=-1, eps=1e-05):
    m = jnp.mean(x, axis=axis, keepdims=True)
    v = jnp.var(x, axis=axis, keepdims=True)
    return (x - m) / jnp.sqrt(v + eps)

def _scatter_add(tgt, idx, src, axis=0):
    return tgt.at[idx].add(src)

def _segment_sum(src, seg, n):
    return jax.ops.segment_sum(src, seg, n)
kernel_name = 'mk_perceiver_d2_seqx_r8_edbd39'

def setup_inputs(seed: int=0):
    np.random.seed(seed)
    _w = jnp.asarray

    def _rec_inputs():
        import jax
        import jax.numpy as jnp
        _rk = jax.random.key(seed)
        x = 7.22e-05 + 1 * jax.random.normal(jax.random.fold_in(_rk, 1), (2, 128, 128), jnp.float32)
        _lenS = 128 - jax.random.randint(jax.random.fold_in(_rk, 7), (2,), 0, max(1, 128 // 4) + 1, jnp.int32)
        _lenS2 = 2048 - jax.random.randint(jax.random.fold_in(_rk, 8), (2,), 0, max(1, 2048 // 4) + 1, jnp.int32)
        _ctx_1024P = jax.random.normal(jax.random.fold_in(_rk, 11), (2, 16, 128), jnp.float32)
        _ctx_1024c = jax.random.dirichlet(jax.random.fold_in(_rk, 511), 0.3 * jnp.ones((16,), jnp.float32), (2, 2048))
        _ctx_1024t = jnp.einsum('bsk,bkd->bsd', _ctx_1024c, _ctx_1024P)
        _ctx_1024t = _ctx_1024t * jax.lax.rsqrt(jnp.mean(jnp.square(_ctx_1024t)) + 1e-12) * 0.953939
        ctx_1024 = 4.13588e-05 + 0.999923 * (_ctx_1024t + 0.3 * jax.random.normal(jax.random.fold_in(_rk, 611), (2, 2048, 128), jnp.float32))
        _validS = jnp.arange(128)[None, :] < _lenS[:, None]
        _validS2 = jnp.arange(2048)[None, :] < _lenS2[:, None]
        _causal = jnp.tril(jnp.ones((128, 128), dtype=bool))
        mask_BxSxS2_bk0 = jnp.logical_not(jnp.broadcast_to(_validS2[:, None, :], (2, 128, 2048)))
        return (x, ctx_1024, mask_BxSxS2_bk0)
    x, ctx_1024, mask_BxSxS2_bk0 = _rec_inputs()

    def _L0_xattn_setup():
        import jax, jax.numpy as jnp
        import numpy as np
        HEADS = 16
        DIM_HEAD = 64
        SCALE = DIM_HEAD ** (-0.5)

        def _split_heads(x):
            b, l, n = x.shape
            return x.reshape(b, l, HEADS, DIM_HEAD).transpose(0, 2, 1, 3)
        key = jax.random.key(seed)
        ks = jax.random.split(key, 6)
        B, L, D = (4, 256, 128)
        inner = HEADS * DIM_HEAD
        s = lambda fan_in: 1.0 / np.sqrt(fan_in)
        return {'x1': jax.random.normal(ks[0], (B, L, D), jnp.float32), 'x2': jax.random.normal(ks[1], (B, L, D), jnp.float32), 'Wq': jax.random.normal(ks[2], (D, inner), jnp.float32) * s(D), 'Wkv': jax.random.normal(ks[3], (D, 2 * inner), jnp.float32) * s(D), 'Wo': jax.random.normal(ks[4], (inner, D), jnp.float32) * s(inner), 'bo': jax.random.normal(ks[5], (D,), jnp.float32) * 0.02}
    _L0_xattn_all = _L0_xattn_setup()
    _L0_xattn_in = {k: v for k, v in _L0_xattn_all.items() if k in ('Wq', 'Wkv', 'Wo', 'bo')}
    del _L0_xattn_all

    def _L0_attn_setup():
        import jax, jax.numpy as jnp
        import numpy as np
        D_MODEL, N_HEADS = (128, 16)
        D_H = D_MODEL // N_HEADS
        D_HR = D_H // 2
        D_LATENT = 32
        THETA = 10000.0

        def rope(x, theta=THETA):
            S, d = (x.shape[-2], x.shape[-1])
            inv = theta ** (-jnp.arange(0, d, 2, dtype=jnp.float32) / d)
            ang = jnp.arange(S, dtype=jnp.float32)[:, None] * inv
            cos, sin = (jnp.cos(ang), jnp.sin(ang))
            x1, x2 = (x[..., 0::2], x[..., 1::2])
            r1 = x1 * cos - x2 * sin
            r2 = x1 * sin + x2 * cos
            return jnp.stack([r1, r2], axis=-1).reshape(x.shape)
        key = jax.random.key(seed)
        ks = jax.random.split(key, 9)
        s = lambda fan_in: 1.0 / np.sqrt(fan_in)
        return {'x': jax.random.normal(ks[0], (4, 256, D_MODEL), jnp.float32), 'W_DQ': jax.random.normal(ks[1], (D_MODEL, D_LATENT), jnp.float32) * s(D_MODEL), 'W_UQ': jax.random.normal(ks[2], (D_LATENT, N_HEADS * D_H), jnp.float32) * s(D_LATENT), 'W_QR': jax.random.normal(ks[3], (D_LATENT, N_HEADS * D_HR), jnp.float32) * s(D_LATENT), 'W_DKV': jax.random.normal(ks[4], (D_MODEL, D_LATENT), jnp.float32) * s(D_MODEL), 'W_UK': jax.random.normal(ks[5], (D_LATENT, N_HEADS * D_H), jnp.float32) * s(D_LATENT), 'W_UV': jax.random.normal(ks[6], (D_LATENT, N_HEADS * D_H), jnp.float32) * s(D_LATENT), 'W_KR': jax.random.normal(ks[7], (D_MODEL, D_HR), jnp.float32) * s(D_MODEL), 'W_O': jax.random.normal(ks[8], (N_HEADS * D_H, D_MODEL), jnp.float32) * s(N_HEADS * D_H)}
    _L0_attn_all = _L0_attn_setup()
    _L0_attn_in = {k: v for k, v in _L0_attn_all.items() if k in ('W_DQ', 'W_UQ', 'W_QR', 'W_DKV', 'W_UK', 'W_UV', 'W_KR', 'W_O')}
    del _L0_attn_all

    def _L0_ffn_setup():
        import jax, jax.numpy as jnp
        import numpy as np
        B, S, H, FFN, E = (2, 256, 128, 512, 8)
        key = jax.random.key(seed)
        k0, k1, k2, k3 = jax.random.split(key, 4)
        return {'hidden_states': jax.random.normal(k0, (B, S, H), dtype=jnp.float32), 'Wr': jax.random.normal(k1, (H, E), dtype=jnp.float32) * 0.02, 'br': jnp.zeros((E,), dtype=jnp.float32), 'W1': jax.random.normal(k2, (E, H, FFN), dtype=jnp.float32) * 0.02, 'W2': jax.random.normal(k3, (E, FFN, H), dtype=jnp.float32) * 0.02}
    _L0_ffn_all = _L0_ffn_setup()
    _L0_ffn_in = {k: v for k, v in _L0_ffn_all.items() if k in ('Wr', 'br', 'W1', 'W2')}
    del _L0_ffn_all

    def _L1_xattn_setup():
        import jax, jax.numpy as jnp
        import numpy as np
        from math import sqrt
        B, Q, S, D, H = (2, 256, 256, 128, 16)
        ADIM = D // H
        IEPS = 1e-32

        def sparse_norm(scores, nbias):
            t = jax.nn.relu(scores + nbias[0])
            t = t * t
            return t / (t.sum(-1, keepdims=True) + IEPS)
        key = jax.random.key(seed)
        ks = jax.random.split(key, 7)
        sc = 0.02
        return {'iQ': jax.random.normal(ks[0], (B, Q, D), jnp.float32), 'iK': jax.random.normal(ks[1], (B, S, D), jnp.float32), 'mask': jax.random.randint(ks[2], (B, Q, S), 0, 2) > 0, 'Wq': jax.random.normal(ks[3], (D, D), jnp.float32) * sc, 'Wkv': jax.random.normal(ks[4], (2 * D, D), jnp.float32) * sc, 'Wo': jax.random.normal(ks[5], (D, D), jnp.float32) * sc, 'nbias': jnp.zeros((1,), jnp.float32)}
    _L1_xattn_all = _L1_xattn_setup()
    _L1_xattn_in = {k: v for k, v in _L1_xattn_all.items() if k in ('Wq', 'Wkv', 'Wo', 'nbias')}
    del _L1_xattn_all

    def _L1_attn_setup():
        import math
        import jax, jax.numpy as jnp
        import numpy as np
        D, DK, DV = (128, 128, 128)
        B, S = (4, 256)
        key = jax.random.key(seed)
        ks = jax.random.split(key, 4)
        std_qk = math.sqrt(2.0 / (D + DK))
        std_v = math.sqrt(2.0 / (D + DV))
        return {'X': jax.random.normal(ks[0], (B, S, D), dtype=jnp.float32), 'W_q': jax.random.normal(ks[1], (D, DK), dtype=jnp.float32) * std_qk, 'W_k': jax.random.normal(ks[2], (D, DK), dtype=jnp.float32) * std_qk, 'W_v': jax.random.normal(ks[3], (D, DV), dtype=jnp.float32) * std_v, 'b_q': jnp.zeros((DK,), dtype=jnp.float32), 'b_k': jnp.zeros((DK,), dtype=jnp.float32), 'b_v': jnp.zeros((DV,), dtype=jnp.float32)}
    _L1_attn_all = _L1_attn_setup()
    _L1_attn_in = {k: v for k, v in _L1_attn_all.items() if k in ('W_q', 'W_k', 'W_v', 'b_q', 'b_k', 'b_v')}
    del _L1_attn_all

    def _L1_ffn_setup():
        import jax, jax.numpy as jnp
        import numpy as np
        B, S, D = (2, 64, 128)
        E, K, I = (16, 8, 128)
        I_SH = 128
        ROUTE_SCALE = 2.826
        key = jax.random.key(seed)
        ks = jax.random.split(key, 8)
        s = 0.02
        return {'x': jax.random.normal(ks[0], (B, S, D), dtype=jnp.float32), 'gate_w': jax.random.normal(ks[1], (E, D), dtype=jnp.float32) * s, 'expert_bias': jnp.zeros((E,), dtype=jnp.float32), 'w_gate': jax.random.normal(ks[2], (E, I, D), dtype=jnp.float32) * s, 'w_up': jax.random.normal(ks[3], (E, I, D), dtype=jnp.float32) * s, 'w_down': jax.random.normal(ks[4], (E, D, I), dtype=jnp.float32) * s, 'shared_gate_w': jax.random.normal(ks[5], (I_SH, D), dtype=jnp.float32) * s, 'shared_up_w': jax.random.normal(ks[6], (I_SH, D), dtype=jnp.float32) * s, 'shared_down_w': jax.random.normal(ks[7], (D, I_SH), dtype=jnp.float32) * s}
    _L1_ffn_all = _L1_ffn_setup()
    _L1_ffn_in = {k: v for k, v in _L1_ffn_all.items() if k in ('gate_w', 'expert_bias', 'w_gate', 'w_up', 'w_down', 'shared_gate_w', 'shared_up_w', 'shared_down_w')}
    del _L1_ffn_all
    return {'x': x, 'ctx_1024': ctx_1024, 'mask_BxSxS2_bk0': mask_BxSxS2_bk0, 'L0_xattn_Wq': _L0_xattn_in['Wq'], 'L0_xattn_Wkv': _L0_xattn_in['Wkv'], 'L0_xattn_Wo': _L0_xattn_in['Wo'], 'L0_xattn_bo': _L0_xattn_in['bo'], 'L0_attn_W_DQ': _L0_attn_in['W_DQ'], 'L0_attn_W_UQ': _L0_attn_in['W_UQ'], 'L0_attn_W_QR': _L0_attn_in['W_QR'], 'L0_attn_W_DKV': _L0_attn_in['W_DKV'], 'L0_attn_W_UK': _L0_attn_in['W_UK'], 'L0_attn_W_UV': _L0_attn_in['W_UV'], 'L0_attn_W_KR': _L0_attn_in['W_KR'], 'L0_attn_W_O': _L0_attn_in['W_O'], 'L0_ffn_Wr': _L0_ffn_in['Wr'], 'L0_ffn_br': _L0_ffn_in['br'], 'L0_ffn_W1': _L0_ffn_in['W1'], 'L0_ffn_W2': _L0_ffn_in['W2'], 'L1_xattn_Wq': _L1_xattn_in['Wq'], 'L1_xattn_Wkv': _L1_xattn_in['Wkv'], 'L1_xattn_Wo': _L1_xattn_in['Wo'], 'L1_xattn_nbias': _L1_xattn_in['nbias'], 'L1_attn_W_q': _L1_attn_in['W_q'], 'L1_attn_W_k': _L1_attn_in['W_k'], 'L1_attn_W_v': _L1_attn_in['W_v'], 'L1_attn_b_q': _L1_attn_in['b_q'], 'L1_attn_b_k': _L1_attn_in['b_k'], 'L1_attn_b_v': _L1_attn_in['b_v'], 'L1_ffn_gate_w': _L1_ffn_in['gate_w'], 'L1_ffn_expert_bias': _L1_ffn_in['expert_bias'], 'L1_ffn_w_gate': _L1_ffn_in['w_gate'], 'L1_ffn_w_up': _L1_ffn_in['w_up'], 'L1_ffn_w_down': _L1_ffn_in['w_down'], 'L1_ffn_shared_gate_w': _L1_ffn_in['shared_gate_w'], 'L1_ffn_shared_up_w': _L1_ffn_in['shared_up_w'], 'L1_ffn_shared_down_w': _L1_ffn_in['shared_down_w']}

def reference(x, ctx_1024, mask_BxSxS2_bk0, L0_xattn_Wq, L0_xattn_Wkv, L0_xattn_Wo, L0_xattn_bo, L0_attn_W_DQ, L0_attn_W_UQ, L0_attn_W_QR, L0_attn_W_DKV, L0_attn_W_UK, L0_attn_W_UV, L0_attn_W_KR, L0_attn_W_O, L0_ffn_Wr, L0_ffn_br, L0_ffn_W1, L0_ffn_W2, L1_xattn_Wq, L1_xattn_Wkv, L1_xattn_Wo, L1_xattn_nbias, L1_attn_W_q, L1_attn_W_k, L1_attn_W_v, L1_attn_b_q, L1_attn_b_k, L1_attn_b_v, L1_ffn_gate_w, L1_ffn_expert_bias, L1_ffn_w_gate, L1_ffn_w_up, L1_ffn_w_down, L1_ffn_shared_gate_w, L1_ffn_shared_up_w, L1_ffn_shared_down_w):
    import jax
    import jax.numpy as jnp

    def _L0_xattn_ref(x1, x2, Wq, Wkv, Wo, bo):
        import jax, jax.numpy as jnp
        import numpy as np
        HEADS = 16
        DIM_HEAD = 64
        SCALE = DIM_HEAD ** (-0.5)

        def _split_heads(x):
            b, l, n = x.shape
            return x.reshape(b, l, HEADS, DIM_HEAD).transpose(0, 2, 1, 3)
        q = x1 @ Wq
        kv = x2 @ Wkv
        k, v = jnp.split(kv, 2, axis=-1)
        q, k, v = map(_split_heads, (q, k, v))
        attn = jnp.einsum('bhid,bhjd->bhij', q, k) * SCALE
        attn = jax.nn.softmax(attn, axis=-1)
        out = jnp.einsum('bhij,bhjd->bhid', attn, v)
        b, h, l, d = out.shape
        out = out.transpose(0, 2, 1, 3).reshape(b, l, h * d)
        return out @ Wo + bo

    def _L0_attn_ref(x, W_DQ, W_UQ, W_QR, W_DKV, W_UK, W_UV, W_KR, W_O):
        import jax, jax.numpy as jnp
        import numpy as np
        D_MODEL, N_HEADS = (128, 16)
        D_H = D_MODEL // N_HEADS
        D_HR = D_H // 2
        D_LATENT = 32
        THETA = 10000.0

        def rope(x, theta=THETA):
            S, d = (x.shape[-2], x.shape[-1])
            inv = theta ** (-jnp.arange(0, d, 2, dtype=jnp.float32) / d)
            ang = jnp.arange(S, dtype=jnp.float32)[:, None] * inv
            cos, sin = (jnp.cos(ang), jnp.sin(ang))
            x1, x2 = (x[..., 0::2], x[..., 1::2])
            r1 = x1 * cos - x2 * sin
            r2 = x1 * sin + x2 * cos
            return jnp.stack([r1, r2], axis=-1).reshape(x.shape)
        B, S, _ = x.shape
        d_qk = D_H + D_HR
        c_q = x @ W_DQ
        Qc = (c_q @ W_UQ).reshape(B, S, N_HEADS, D_H).transpose(0, 2, 1, 3)
        Qr = (c_q @ W_QR).reshape(B, S, N_HEADS, D_HR).transpose(0, 2, 1, 3)
        Qr = rope(Qr)
        c_kv = x @ W_DKV
        Kc = (c_kv @ W_UK).reshape(B, S, N_HEADS, D_H).transpose(0, 2, 1, 3)
        Kr = rope((x @ W_KR)[:, None, :, :])
        Kr = jnp.broadcast_to(Kr, (B, N_HEADS, S, D_HR))
        V = (c_kv @ W_UV).reshape(B, S, N_HEADS, D_H).transpose(0, 2, 1, 3)
        Q = jnp.concatenate([Qc, Qr], axis=-1)
        K = jnp.concatenate([Kc, Kr], axis=-1)
        scores = jnp.einsum('bhqd,bhkd->bhqk', Q, K)
        scores = jnp.clip(scores, -80.0, 80.0)
        causal = jnp.tril(jnp.ones((S, S), dtype=bool))
        scores = jnp.where(causal, scores, -jnp.inf)
        weights = jax.nn.softmax(scores / jnp.sqrt(jnp.float32(d_qk)), axis=-1)
        attn = jnp.einsum('bhqk,bhkd->bhqd', weights, V)
        attn = attn.transpose(0, 2, 1, 3).reshape(B, S, N_HEADS * D_H)
        return attn @ W_O

    def _L0_ffn_ref(hidden_states, Wr, br, W1, W2):
        import jax, jax.numpy as jnp
        import numpy as np
        B, S, H, FFN, E = (2, 256, 128, 512, 8)
        b, s, h = hidden_states.shape
        x = hidden_states.reshape(-1, h)
        route = jax.nn.sigmoid(x @ Wr + br)
        max_prob = jnp.max(route, axis=1, keepdims=True)
        max_ind = jnp.argmax(route, axis=1)
        out = jnp.zeros_like(x)
        n_experts = Wr.shape[1]
        for e in range(n_experts):
            mask = (max_ind == e)[:, None].astype(x.dtype)
            y = jax.nn.gelu(x @ W1[e], approximate=False) @ W2[e]
            out = out + mask * y
        out = out * max_prob
        return out.reshape(b, s, h)

    def _L1_xattn_ref(iQ, iK, mask, Wq, Wkv, Wo, nbias):
        import jax, jax.numpy as jnp
        import numpy as np
        from math import sqrt
        B, Q, S, D, H = (2, 256, 256, 128, 16)
        ADIM = D // H
        IEPS = 1e-32

        def sparse_norm(scores, nbias):
            t = jax.nn.relu(scores + nbias[0])
            t = t * t
            return t / (t.sum(-1, keepdims=True) + IEPS)
        b, q, _ = iQ.shape
        s = iK.shape[1]
        rq = (iQ @ Wq.T).reshape(b, q, H, ADIM)
        kv = (iK @ Wkv.T).reshape(b, s, 2, H, ADIM)
        rk, rv = (kv[:, :, 0], kv[:, :, 1])
        scores = jnp.einsum('bqhd,bshd->bhqs', rq, rk) / sqrt(ADIM)
        scores = jnp.where(mask[:, None, :, :], jnp.float32(-1e+32), scores)
        attn = sparse_norm(scores, nbias)
        o = jnp.einsum('bhqs,bshd->bqhd', attn, rv).reshape(b, q, H * ADIM)
        return o @ Wo.T

    def _L1_attn_ref(X, W_q, W_k, W_v, b_q, b_k, b_v):
        import math
        import jax, jax.numpy as jnp
        import numpy as np
        D, DK, DV = (128, 128, 128)
        B, S = (4, 256)
        scale = 1.0 / math.sqrt(DK)
        Q = X @ W_q + b_q
        K = X @ W_k + b_k
        V = X @ W_v + b_v
        A = jnp.einsum('bsd,btd->bst', Q, K) * scale
        A = jax.nn.softmax(A, axis=2)
        return jnp.einsum('bst,btv->bsv', A, V)

    def _L1_ffn_ref(x, gate_w, expert_bias, w_gate, w_up, w_down, shared_gate_w, shared_up_w, shared_down_w):
        import jax, jax.numpy as jnp
        import numpy as np
        B, S, D = (2, 64, 128)
        E, K, I = (16, 8, 128)
        I_SH = 128
        ROUTE_SCALE = 2.826
        gates = jnp.einsum('bsd,ed->bse', x, gate_w)
        scores = jax.nn.sigmoid(gates.astype(jnp.float32))
        sel_scores = scores + expert_bias
        _, inds = jax.lax.top_k(sel_scores, K)
        selected = jnp.take_along_axis(scores, inds, axis=-1)
        selected = selected / selected.sum(axis=-1, keepdims=True)
        selected = selected * ROUTE_SCALE
        onehot = jax.nn.one_hot(inds, E, dtype=selected.dtype)
        combine = jnp.einsum('bske,bsk->bse', onehot, selected)
        hg = jnp.einsum('bsd,eid->bsei', x, w_gate)
        hu = jnp.einsum('bsd,eid->bsei', x, w_up)
        h = jax.nn.silu(hg) * hu
        ye = jnp.einsum('bsei,edi->bsed', h, w_down)
        y = jnp.einsum('bsed,bse->bsd', ye, combine).astype(x.dtype)
        g = jnp.einsum('bsd,id->bsi', x, shared_gate_w)
        u = jnp.einsum('bsd,id->bsi', x, shared_up_w)
        y = y + jnp.einsum('bsi,di->bsd', jax.nn.silu(g) * u, shared_down_w)
        return y
    x = x + _L0_xattn_ref(_layernorm(x, axis=-1), ctx_1024, L0_xattn_Wq, L0_xattn_Wkv, L0_xattn_Wo, L0_xattn_bo)
    x = x + _L0_attn_ref(_layernorm(x, axis=-1), L0_attn_W_DQ, L0_attn_W_UQ, L0_attn_W_QR, L0_attn_W_DKV, L0_attn_W_UK, L0_attn_W_UV, L0_attn_W_KR, L0_attn_W_O)
    x = x + _L0_ffn_ref(_layernorm(x, axis=-1), L0_ffn_Wr, L0_ffn_br, L0_ffn_W1, L0_ffn_W2)
    x = x + _L1_xattn_ref(_layernorm(x, axis=-1), ctx_1024, mask_BxSxS2_bk0, L1_xattn_Wq, L1_xattn_Wkv, L1_xattn_Wo, L1_xattn_nbias)
    x = x + _L1_attn_ref(_layernorm(x, axis=-1), L1_attn_W_q, L1_attn_W_k, L1_attn_W_v, L1_attn_b_q, L1_attn_b_k, L1_attn_b_v)
    x = x + _L1_ffn_ref(_layernorm(x, axis=-1), L1_ffn_gate_w, L1_ffn_expert_bias, L1_ffn_w_gate, L1_ffn_w_up, L1_ffn_w_down, L1_ffn_shared_gate_w, L1_ffn_shared_up_w, L1_ffn_shared_down_w)
    return x

_drawn_inputs = setup_inputs


def setup_inputs(seed=0):
    import zlib

    import numpy as np

    out = dict(_drawn_inputs(seed))
    spreads = {'L0_ffn_br': (0.0, 0.353),
     'L1_attn_b_q': (0.0, 0.658),
     'L1_attn_b_k': (0.0, 0.8),
     'L1_attn_b_v': (0.0, 0.1),
     'L1_ffn_expert_bias': (0.0, 0.8)}
    factors = {'L0_ffn_Wr': 2.741,
     'L1_xattn_Wq': 3.47,
     'L1_ffn_gate_w': 8.0,
     'L1_ffn_w_gate': 8.0,
     'L1_ffn_w_up': 8.0,
     'L1_ffn_w_down': 8.0,
     'L1_ffn_shared_gate_w': 8.0,
     'L1_ffn_shared_up_w': 8.0,
     'L1_ffn_shared_down_w': 8.0}
    for name, (base, spread) in spreads.items():
        noise = np.random.default_rng([zlib.crc32(name.encode()), seed]).standard_normal(out[name].shape)
        drawn = base * np.exp(spread * noise) if base else spread * noise
        out[name] = jnp.asarray(drawn.astype(out[name].dtype))
    for name, factor in factors.items():
        out[name] = (out[name] * factor).astype(out[name].dtype)
    return out
```

```python
from contextlib import ExitStack
import math

import numpy as np
import concourse.bass as bass
from concourse import mybir

F32 = mybir.dt.float32
F32R = mybir.dt.float32r
I32 = mybir.dt.int32
U8 = mybir.dt.uint8
ALU = mybir.AluOpType
ACT = mybir.ActivationFunctionType
AX = mybir.AxisListType

P = 128
B = 2
S = 128
T = B * S
D = 128
CTX = 2048
NBLK = CTX // P
H = 16
DH = 64
QUAD = 4
NQ = B * H // QUAD
CH = CTX // 512
SCALE0 = DH ** -0.5
LAT = 32
DC = D // H
DR = DC // 2
HR = 32
CLIP = 80.0
SCALE_MLA = 1.0 / math.sqrt(DC + DR)
E0 = 8
FF = 512
NF = FF // P
DA = D // H
SCALE1 = 1.0 / math.sqrt(DA)
BIG = 3.0e38
TINY = 1e-32
SCALE_SA = 1.0 / math.sqrt(D)
E1 = 16
TOPK = 8
ROUTE_SCALE = 2.826
EPS = 1e-5
RSQRT_SEED = 0x5F3759DF

INPUTS = {
    "x_tok": (S, B, D), "ctx_nat": (P, B * NBLK, D), "ctx_t": (D, B * CTX),
    "mask_t": (P, B * NBLK, S),
    "wq0": (D, H * DH), "wk0_t": (P, H // 2, D), "wv0": (D, H * DH), "wo0": (P, H // 2, D), "bo0": (P, D),
    "w_lat": (D, 2 * LAT), "wq_mla": (LAT, 2, 4, P), "wk_mla": (LAT, 4, P), "wkr_mla": (D, 2, P),
    "wuv": (LAT, D), "wo_mla": (D, D), "rope": (P, 2, S),
    "wr": (D, E0), "br": (P, E0), "w1": (D, E0, FF), "w2": (P, NF, E0, D), "rank": (P, E0),
    "wq1": (D, 4, P), "wk1": (D, D), "wv1": (D, D), "wo1": (D, D), "nbias": (P, 1), "headsel": (P, 4),
    "wqkv_sa": (D, 3, D), "bqk_sa": (D, 2), "bv_sa": (P, D),
    "gate_w": (D, E1), "gate_b": (P, E1), "below": (P, E1, E1),
    "wg": (D, E1 + 1, P), "wu": (D, E1 + 1, P), "wd": (P, E1 + 1, D),
    "ident": (P, P),
}


class Arena:

    def __init__(self, nc, start, end):
        self.nc, self.at, self.end = nc, start, end

    def take(self, name, shape, dt=F32):
        size = int(np.prod(shape[1:])) * (1 if dt == U8 else 4)
        t = self.nc.alloc_sbuf_tensor_at(name, list(shape), dt, offset=self.at)
        self.at += -(-size // 32) * 32
        assert self.at <= self.end, (name, self.at - self.end)
        return t


def build(nc, ins, out):
    with ExitStack() as ctx:
        def sem(name):
            return ctx.enter_context(nc.semaphore(name))

        def bc(ap, axis, n):
            ap = ap.unsqueeze(axis)
            shape = list(ap.shape)
            shape[axis] = n
            return ap.to_broadcast(shape)

        start = -(-nc.sbuf_base // 32) * 32
        end = nc.sbuf_usable_end
        A = Arena(nc, start, end)
        x = A.take("x", (P, B, D))
        xn = A.take("xn", (P, B, D))
        xnT = A.take("xnT", (P, T))
        ident = A.take("ident_sb", (P, P))
        headsel = A.take("headsel_sb", (P, 4))
        nbias = A.take("nbias_sb", (P, 1))
        neg_nbias = A.take("neg_nbias", (P, 1))
        bias_rows = A.take("bias_rows", (P, 2 * D))
        br_sb = A.take("br_sb", (P, E0))
        rank_sb = A.take("rank_sb", (P, E0))
        wr_sb = A.take("wr_sb", (P, E0))
        w_lat = A.take("w_lat_sb", (P, 2 * LAT))
        wkr_mla = A.take("wkr_mla_sb", (P, 2, P))
        wuv = A.take("wuv_sb", (LAT, D))
        wo_mla = A.take("wo_mla_sb", (P, D))
        rope = A.take("rope_sb", (P, 2, S))
        stats = A.take("stats", (P, B, 6))
        mv = A.take("mv", (P, B, 2))
        nwt = A.take("nwt", (P, 4, B))
        seed = A.take("seed", (P, 2, B), I32)
        max2 = A.take("max2", (P, 2 * 2))
        nmax = A.take("nmax", (P, 2))
        rowsum = A.take("rowsum", (P, B * H, 2))
        rden = A.take("rden", (P, 2, QUAD))
        xb = A.take("xb", (P, B, D))
        attn0 = A.take("attn0", (P, B, H * DH))
        attn0_at = A.at - B * H * DH * 4
        wv0 = A.take("wv0_sb", (P, H * DH))
        wo0 = A.take("wo0_sb", (P, H // 2, D))
        wo0_at = A.at - H // 2 * D * 4
        stage = A.at

        A = Arena(nc, stage, end)
        ctxT_hi = A.take("ctxT_hi", (P, B * CTX), F32R)
        ctxT_lo = A.take("ctxT_lo", (P, B * CTX), F32R)
        probs_at = A.at
        probs = A.take("probs", (P, 2, QUAD, CTX))
        qk_at = A.at
        qk_hi = A.take("qk_hi", (P, H, B, S), F32R)
        qk_lo = A.take("qk_lo", (P, H, B, S), F32R)
        ctx_at = A.at
        ctx_hi = A.take("ctx_hi", (P, B * NBLK, D), F32R)
        ctx_lo = A.take("ctx_lo", (P, B * NBLK, D), F32R)
        pT_hi = A.take("pT_hi", (P, 3, 512), F32R)
        pT_lo = A.take("pT_lo", (P, 3, 512), F32R)
        u_sb = A.take("u_sb", (P, 512))
        A = Arena(nc, probs_at, qk_at)
        ctxT_raw = A.take("ctxT_raw", (P, B * CTX))
        ctx_raw = A.take("ctx_raw", (P, B * NBLK, D))
        wq0 = A.take("wq0_sb", (P, H * DH))
        wk0_t = A.take("wk0_t_sb", (P, H // 2, D))
        q0T = A.take("q0T", (P, H // 2, T))

        A = Arena(nc, stage, probs_at)
        w1 = A.take("w1_sb", (P, E0, FF))
        w2 = A.take("w2_sb", (P, NF, E0, D))
        A = Arena(nc, stage, probs_at)
        wg = A.take("wg_sb", (P, E1 + 1, P))
        wu = A.take("wu_sb", (P, E1 + 1, P))
        wd = A.take("wd_sb", (P, E1 + 1, D))
        oT1 = A.take("oT1", (P, 2 * 4, S))
        A = Arena(nc, probs_at, qk_at)
        attn0T = A.take("attn0T", (P, B, H // 2, S))
        lat_sb = A.take("lat_sb", (LAT, 2, T))
        qr = A.take("qr", (P, 4, T))
        kr = A.take("kr", (P, 4, T))
        ropet = A.take("ropet", (P, 4, T))
        ropek = A.take("ropek", (P, T))
        vx = A.take("vx", (P, B, H, DC + 1))
        clipped = A.take("clipped", (P, H, S))
        pm = A.take("pm", (P, B, H, S))
        attn_m = A.take("attn_m", (P, B, H, DC))
        rl_m = A.take("rl_m", (P, B * H))
        attn_mT = A.take("attn_mT", (P, T))
        wq_mla = A.take("wq_mla_sb", (LAT, 2, 4, P))
        wk_mla = A.take("wk_mla_sb", (LAT, 4, P))
        A = Arena(nc, probs_at, qk_at)
        kstack = A.take("kstack", (P, 4, B * CTX), F32R)
        A = Arena(nc, probs_at, qk_at)
        qk_sa = A.take("qk_sa", (P, 2, T))
        v_sa = A.take("v_sa", (P, B, D))
        p_sa = A.take("p_sa", (P, B, S))
        pT_sa = A.take("pT_sa", (P, T))
        mx_sa = A.take("mx_sa", (P, 4, B))
        wqkv = A.take("wqkv_sb", (P, 3, D))
        bqk = A.take("bqk_sb", (P, 2))
        gate_w = A.take("gate_w_sb", (P, E1))
        gate_b = A.take("gate_b_sb", (P, E1))
        below = A.take("below_sb", (P, E1, E1))
        sc1 = A.take("sc1", (P, 4, B, E1))
        cmp1 = A.take("cmp1", (P, 3, B, E1, E1))
        comb = A.take("comb", (P, B, E1))
        csum = A.take("csum", (P, 2, B))
        silu_g = A.take("silu_g", (P, 2, 512))
        hT1 = A.take("hT1", (P, E1 + 1, T))
        A = Arena(nc, qk_at, ctx_at)
        ctxT_raw2 = A.take("ctxT_raw2", (P, B * CTX))
        cap = A.take("cap", (P, B * NBLK, S))
        A = Arena(nc, qk_at, ctx_at)
        xm = A.take("xm", (P, B, E0, S))
        g0 = A.take("g0", (P, NF, T))
        yw = A.take("yw", (P, E0, D))
        A = Arena(nc, qk_at, ctx_at)
        qbd = A.take("qbd", (P, B, 4, 4, S), F32R)
        A = Arena(nc, ctx_at, end)
        k1_hi = A.take("k1_hi", (P, B * CTX), F32R)
        k1_lo = A.take("k1_lo", (P, B * CTX), F32R)
        v1 = A.take("v1", (P, B * NBLK, H, DA + 1))
        A = Arena(nc, ctx_at, end)
        w_ring = A.take("w_ring", (P, 3, 1024))
        p_ring = A.take("p_ring", (P, 3, 1024))
        attn1 = A.take("attn1", (P, B, H, DA))
        attn1T = A.take("attn1T", (P, T))
        rl1 = A.take("rl1", (P, 2 * 4, 4))
        A = Arena(nc, attn0_at, attn0_at + B * H * DH * 4)
        mask_sb = A.take("mask_sb", (P, B * NBLK, S), U8)
        A2 = Arena(nc, attn0_at, attn0_at + B * H * DH * 4)
        diag = A2.take("diag", (P, B, E0, S))
        A2 = Arena(nc, attn0_at, attn0_at + B * H * DH * 4)
        q1 = A2.take("q1", (P, 4, T))
        q1s = A2.take("q1s", (P, 4, T), F32R)
        A = Arena(nc, attn0_at + B * H * DH * 4, stage)
        rt = A.take("rt", (P, 5, B, E0))
        rtm = A.take("rtm", (P, 2, B))
        A = Arena(nc, wo0_at, stage)
        wq1 = A.take("wq1_sb", (P, 4, P))
        wkvo1 = A.take("wkvo1_sb", (P, 3, D))

        ps = ctx.enter_context(nc.psum_tensor("ps", [P, 8, 512], F32))

        load = {n: sem("ld_" + n) for n in (
            "x", "wq0", "wk0", "ctxT0", "ctxT1", "ctx0", "ctx1", "vo0", "small", "mla",
            "w1", "w2", "ctxT2", "mask", "l1w", "kstack", "exp1", "sa")}
        xn_ready, xnT_psum, xnT_ready = sem("xn_ready"), sem("xnT_psum"), sem("xnT_ready")
        chain = sem("dve_chain")
        q0_psum, q0_sb = sem("q0_psum"), sem("q0_sb")
        qk_psum, qk_hi_done, qk_lo_done = sem("qk_psum"), sem("qk_hi_done"), sem("qk_lo_done")
        split_hi, split_lo = sem("split_hi"), sem("split_lo")
        scored, maxed, exped = sem("scored"), sem("maxed"), sem("exped")
        turned, hi_done, lo_done, pv_done = sem("turned"), sem("hi_done"), sem("lo_done"), sem("pv_done")
        u_copied, o_psum, o_copied = sem("u_copied"), sem("o_psum"), sem("o_copied")
        a0_turned, a0T_act, a0T_dve, proj0 = sem("a0_turned"), sem("a0T_act"), sem("a0T_dve"), sem("proj0")
        xb_done = sem("xb_done")
        lat_psum, lat_copied = sem("lat_psum"), sem("lat_copied")
        qkr_psum, qr_done, kr_done = sem("qkr_psum"), sem("qr_done"), sem("kr_done")
        vm_psum, vm_done, ones_done = sem("vm_psum"), sem("vm_done"), sem("ones_done")
        ms_psum, ms_clip, ms_exp, ms_masked = sem("ms_psum"), sem("ms_clip"), sem("ms_exp"), sem("ms_masked")
        mo_psum, mo_norm, mo_turned, mo_T, mo_proj = (sem("mo_psum"), sem("mo_norm"), sem("mo_turned"),
                                                      sem("mo_T"), sem("mo_proj"))
        rt_psum, rt_z, rt_e, diag_done = sem("rt_psum"), sem("rt_z"), sem("rt_e"), sem("diag_done")
        xm_psum, xm_act, xm_dve = sem("xm_psum"), sem("xm_act"), sem("xm_dve")
        h0_psum, g0_done, y0_psum = sem("h0_psum"), sem("g0_done"), sem("y0_psum")
        kv_psum, kv_act, k1_split = sem("kv_psum"), sem("kv_act"), sem("k1_split")
        cap_done = sem("cap_done")
        q1_psum, q1_done, qbd_done = sem("q1_psum"), sem("q1_done"), sem("qbd_done")
        s1_psum, w1_done, sq_done, pv1_done = sem("s1_psum"), sem("w1_done"), sem("sq_done"), sem("pv1_done")
        acc_zero, o1_copied = sem("acc_zero"), sem("o1_copied")
        o1_turned, o1_norm, o1_turned2, o1_T, o1_proj = (sem("o1_turned"), sem("o1_norm"), sem("o1_turned2"),
                                                         sem("o1_T"), sem("o1_proj"))
        sa_psum, sa_qk, sa_v, sa_score, sa_max, sa_exp, sa_turned, sa_T, sa_out = (
            sem("sa_psum"), sem("sa_qk"), sem("sa_v"), sem("sa_score"), sem("sa_max"), sem("sa_exp"),
            sem("sa_turned"), sem("sa_T"), sem("sa_out"))
        gt_psum, gt_z, gt_e = sem("gt_psum"), sem("gt_z"), sem("gt_e")
        gu_psum, silu_done, h1_done, y1_psum = sem("gu_psum"), sem("silu_done"), sem("h1_done"), sem("y1_psum")
        y1_added, stored = sem("y1_added"), sem("stored")

        def qk_pair(t, i):
            h = 4 * (i // 2) + i % 2
            return t[:, h:h + 3:2, :, :].rearrange("p h b s -> p h (b s)")

        def qk_bank(i):
            return ps[:, 4 + 2 * ((i // 2) % 2) + i % 2, :].rearrange("p (h t) -> p h t", h=2)

        NHS = B * H
        NB0 = NQ * NBLK
        UNITS = NBLK // 2
        COMBOS = B * 4
        NU = COMBOS * UNITS
        EP = (E1 + 2) // 2

        block = ctx.enter_context(nc.Block())

        @block.sync
        def _(sp):
            def get(dst, name, s, src=None):
                sp.dma_start(dst, ins[name] if src is None else src).then_inc(load[s], 16)

            half = CTX
            get(x[:], "x_tok", "x")
            get(ident[:], "ident", "x")
            get(wq0[:], "wq0", "wq0")
            get(wk0_t[:], "wk0_t", "wk0")
            for b in range(B):
                get(ctxT_raw[:, b * half:(b + 1) * half], "ctx_t", f"ctxT{b}",
                    ins["ctx_t"][:, b * half:(b + 1) * half])
            for b in range(B):
                get(ctx_raw[:, b * NBLK:(b + 1) * NBLK, :], "ctx_nat", f"ctx{b}",
                    ins["ctx_nat"][:, b * NBLK:(b + 1) * NBLK, :])
            get(wv0[:], "wv0", "vo0")
            get(wo0[:], "wo0", "vo0")
            small = [(bias_rows[:, 0:D], "bo0"), (bias_rows[:, D:2 * D], "bv_sa"), (w_lat[:], "w_lat"), (wkr_mla[:], "wkr_mla"), (wuv[:], "wuv"),
                     (wo_mla[:], "wo_mla"), (rope[:], "rope"), (wr_sb[:], "wr"), (br_sb[:], "br"),
                     (rank_sb[:], "rank"), (headsel[:], "headsel"), (nbias[:], "nbias")]
            assert len(small) == N_SMALL
            for dst, name in small:
                get(dst, name, "small")
            sp.wait_ge(scored, 2 * NHS)
            get(ctxT_raw2[:], "ctx_t", "ctxT2")
            get(w1[:], "w1", "w1")
            get(w2[:], "w2", "w2")
            sp.wait_ge(turned, NB0)
            get(wq_mla[:], "wq_mla", "mla")
            get(wk_mla[:], "wk_mla", "mla")
            sp.wait_ge(proj0, 1)
            get(wq1[:], "wq1", "l1w")
            for i, name in enumerate(("wk1", "wv1", "wo1")):
                get(wkvo1[:, i, :], name, "l1w")
            get(mask_sb[:], "mask_t", "mask")
            sp.wait_ge(kv_act, 2 * B * CTX // 512)
            sp.wait_ge(k1_split, B * CTX // 512)
            for t in range(4):
                part = k1_lo if t % 2 else k1_hi
                for g in range(4):
                    sp.dma_start(kstack[32 * t:32 * t + 32, g, :].bitcast(F32),
                                 part[32 * g:32 * g + 32, :].bitcast(F32)).then_inc(load["kstack"], 16)
            sp.wait_ge(y0_psum, 2 * B)
            get(wg[:], "wg", "exp1")
            get(wu[:], "wu", "exp1")
            get(wd[:], "wd", "exp1")
            sp.wait_ge(s1_psum, NU)
            get(wqkv[:], "wqkv_sa", "sa")
            get(bqk[:], "bqk_sa", "sa")
            get(gate_w[:], "gate_w", "sa")
            get(gate_b[:], "gate_b", "sa")
            get(below[:], "below", "sa")
            sp.wait_ge(y1_added, E1 + 1)
            sp.dma_start(out.rearrange("b s d -> s b d"), x[:]).then_inc(stored, 16)
            sp.wait_ge(stored, 16)

        @block.tensor
        def _(pe):
            mm = nc.tensor.matmul

            def turn_xn(layer):
                pe.wait_ge(xn_ready, layer + 1)
                for b in range(B):
                    last = nc.tensor.transpose(ps[:, 5, b * S:(b + 1) * S], xn[:, b, :], ident[:])
                last.then_inc(xnT_psum, 1)
                pe.wait_ge(xnT_ready, layer + 1)

            pe.wait_ge(load["x"], 32)
            turn_xn(0)
            pe.wait_ge(load["wq0"], 16)
            for t in range(H // 2):
                last = mm(ps[:, t // 2, (t % 2) * T:(t % 2 + 1) * T], wq0[:, t * P:(t + 1) * P], xnT[:],
                          start=True, stop=True)
                if t % 2:
                    last.then_inc(q0_psum, 1)
            pe.wait_ge(load["wk0"], 16)
            for h in range(H):
                i, t, r = h // 4, h // 2, (h % 2) * DH
                if h % 4 == 0:
                    pe.wait_ge(q0_sb, i + 1)
                    if i >= 2:
                        pe.wait_ge(qk_lo_done, 2 * (i - 1))
                last = mm(ps[:, 4 + 2 * (i % 2) + h % 2, (t % 2) * T:(t % 2 + 1) * T], wk0_t[r:r + DH, t, :],
                          q0T[r:r + DH, t, :], start=True, stop=True)
                if h % 4 == 3:
                    last.then_inc(qk_psum, 1)

            def scores(hs, c):
                b, h = hs // H, hs % H
                if hs >= 1:
                    pe.wait_ge(exped, 2 * (hs - 1) + c // 2 + 1)
                cols = slice(b * CTX + c * 512, b * CTX + (c + 1) * 512)
                mm(ps[:, c, :], qk_hi[:, h, b, :], ctxT_hi[:, cols], start=True, stop=False)
                mm(ps[:, c, :], qk_lo[:, h, b, :], ctxT_hi[:, cols], start=False, stop=False)
                last = mm(ps[:, c, :], qk_hi[:, h, b, :], ctxT_lo[:, cols], start=False, stop=True)
                if c % 2:
                    last.then_inc(scored, 1)

            def turn_probs(n):
                q, k = n // NBLK, n % NBLK
                if k == 0:
                    pe.wait_ge(exped, 2 * QUAD * (q + 1))
                if n >= 2:
                    pe.wait_ge(lo_done, n - 1)
                for j in range(QUAD):
                    last = nc.tensor.transpose(ps[:, 4 + n % 2, j * S:(j + 1) * S],
                                               probs[:, q % 2, j, k * P:(k + 1) * P], ident[:])
                last.then_inc(turned, 1)

            def weigh_ctx(n):
                q, k = n // NBLK, n % NBLK
                row = (q // QUAD) * NBLK + k
                if k == 0 and q >= 2:
                    pe.wait_ge(o_copied, q - 1)
                pe.wait_ge(lo_done, n + 1)
                acc = ps[:, 6 + q % 2, :]
                mm(acc, ctx_hi[:, row, :], pT_hi[:, n % 3, :], start=(k == 0), stop=False)
                mm(acc, ctx_hi[:, row, :], pT_lo[:, n % 3, :], start=False, stop=False)
                mm(acc, ctx_lo[:, row, :], pT_hi[:, n % 3, :], start=False,
                   stop=(k == NBLK - 1)).then_inc(pv_done, 1)

            def project_v(q):
                pe.wait_ge(u_copied, q + 1)
                if q == 0:
                    pe.wait_ge(load["vo0"], 32)
                for j in range(QUAD):
                    h = (q % QUAD) * QUAD + j
                    last = mm(ps[:, 6 + q % 2, j * DH:(j + 1) * DH], u_sb[:, j * S:(j + 1) * S],
                              wv0[:, h * DH:(h + 1) * DH], start=True, stop=True)
                last.then_inc(o_psum, 1)

            pe.wait_ge(qk_lo_done, H // 2)
            pe.wait_ge(qk_hi_done, H // 2)
            pe.wait_ge(split_lo, 1)
            for step in range(NHS + QUAD):
                n0 = (step - QUAD) * QUAD
                for slot in range(4):
                    if step < NHS and slot < 2:
                        if step == H and slot == 0:
                            pe.wait_ge(split_lo, 3)
                        scores(step, 2 * slot)
                        scores(step, 2 * slot + 1)
                    if n0 >= 0:
                        if n0 == 0 and slot == 0:
                            pe.wait_ge(split_lo, 2)
                        if n0 == QUAD * NBLK and slot == 0:
                            pe.wait_ge(split_lo, 4)
                        n = n0 + slot
                        if n >= 2:
                            weigh_ctx(n - 2)
                        if n >= 2 + NBLK and (n - 2) % NBLK == 2:
                            project_v((n - 2) // NBLK - 1)
                        turn_probs(n)
            weigh_ctx(NB0 - 2)
            weigh_ctx(NB0 - 1)
            project_v(NQ - 1)
            pe.wait_ge(o_copied, NQ)
            for b in range(B):
                for t in range(H // 2):
                    last = nc.tensor.transpose(ps[:, 2 * b + t // 4, (t % 4) * S:(t % 4 + 1) * S],
                                               attn0[:, b, t * P:(t + 1) * P], ident[:])
            last.then_inc(a0_turned, 1)
            for b in range(B):
                pe.wait_ge((a0T_act, a0T_dve)[b], 1)
                for t in range(H // 2):
                    last = mm(ps[:, 4, b * D:(b + 1) * D], attn0T[:, b, t, :], wo0[:, t, :],
                              start=(t == 0), stop=(t == H // 2 - 1))
            last.then_inc(proj0, 1)

            turn_xn(1)
            pe.wait_ge(load["small"], 16 * N_SMALL)
            mm(ps[0:LAT, 5, T:2 * T], w_lat[:, 0:LAT], xnT[:], start=True, stop=True)
            mm(ps[0:LAT, 4, T:2 * T], w_lat[:, LAT:2 * LAT], xnT[:], start=True, stop=True).then_inc(lat_psum, 1)
            pe.wait_ge(lat_copied, 1)
            pe.wait_ge(load["mla"], 32)
            for g in range(4):
                mm(ps[:, g // 2, (g % 2) * T:(g % 2 + 1) * T], wq_mla[:, 0, g, :], lat_sb[:, 0, :],
                   start=True, stop=True)
            for g in range(4):
                last = mm(ps[:, 2 + g // 2, (g % 2) * T:(g % 2 + 1) * T], wq_mla[:, 1, g, :], lat_sb[:, 0, :],
                          start=True, stop=True)
            last.then_inc(qkr_psum, 1)
            mm(ps[:, 4, 0:T], wkr_mla[:, 1, :], xnT[:], start=True, stop=True)
            for g in range(4):
                dst = ps[:, 6 + g // 2, (g % 2) * T:(g % 2 + 1) * T]
                mm(dst, wk_mla[:, g, :], lat_sb[:, 1, :], start=True, stop=False)
                last = mm(dst, wkr_mla[:, 0, :], xnT[:], start=False, stop=True)
            last.then_inc(qkr_psum, 1)
            for b in range(B):
                last = mm(ps[:, 5, b * D:(b + 1) * D], lat_sb[:, 1, b * S:(b + 1) * S], wuv[:],
                          start=True, stop=True)
            last.then_inc(vm_psum, 1)
            pe.wait_ge(qr_done, 1)
            pe.wait_ge(kr_done, 1)
            for b in range(B):
                if b == 1:
                    pe.wait_ge(vm_done, 1)
                for g in range(4):
                    for j in range(4):
                        rows = slice(HR * j, HR * j + HR)
                        last = mm(ps[:, 4 * b + j, g * S:(g + 1) * S], kr[rows, g, b * S:(b + 1) * S],
                                  qr[rows, g, b * S:(b + 1) * S], start=True, stop=True)
                last.then_inc(ms_psum, 1)
            pe.wait_ge(ms_clip, 2 * B)
            pe.wait_ge(ones_done, 3)
            for b in range(B):
                pe.wait_ge(ms_masked, b + 1)
                for h in range(H):
                    at = (b * H + h) * (DC + 1)
                    last = mm(ps[:, 0, at:at + DC + 1], pm[:, b, (h % 4) * 4 + h // 4, :], vx[:, b, h, :],
                              start=True, stop=True)
            last.then_inc(mo_psum, 1)
            pe.wait_ge(mo_norm, 1)
            for b in range(B):
                last = nc.tensor.transpose(ps[:, 1, b * S:(b + 1) * S],
                                           attn_m[:, b, :, :].rearrange("p h d -> p (h d)"), ident[:])
            last.then_inc(mo_turned, 1)
            pe.wait_ge(mo_T, 1)
            for b in range(B):
                last = mm(ps[:, 2, b * D:(b + 1) * D], attn_mT[:, b * S:(b + 1) * S], wo_mla[:],
                          start=True, stop=True)
            last.then_inc(mo_proj, 1)

            turn_xn(2)
            for b in range(B):
                last = mm(ps[:, 6, b * E0:(b + 1) * E0], xnT[:, b * S:(b + 1) * S], wr_sb[:],
                          start=True, stop=True)
            last.then_inc(rt_psum, 1)
            pe.wait_ge(load["ctxT2"], 16)
            pe.wait_ge(load["l1w"], 64)
            for i in range(B * CTX // 512):
                for v in range(2):
                    n = 2 * i + v
                    if n >= 2:
                        pe.wait_ge(kv_act, n - 1)
                        if v == 0:
                            pe.wait_ge(k1_split, i)
                    dst = ps[:, (4, 7)[v], :]
                    if v == 0:
                        last = mm(dst, wkvo1[:, 0, :], ctxT_raw2[:, i * 512:(i + 1) * 512], start=True, stop=True)
                    else:
                        for r in range(4):
                            at = (4 * i + r) * P
                            last = mm(dst[:, r * P:(r + 1) * P], ctxT_raw2[:, at:at + P], wkvo1[:, 1, :],
                                      start=True, stop=True)
                    last.then_inc(kv_psum, 1)
            pe.wait_ge(diag_done, 1)
            for b in range(B):
                for eh in range(2):
                    mm(ps[:, 2 * b + eh, :], xn[:, b, :],
                       diag[:, b, 4 * eh:4 * eh + 4, :].rearrange("p e s -> p (e s)"),
                       start=True, stop=True).then_inc(xm_psum, 1)
            pe.wait_ge(load["w1"], 16)
            pe.wait_ge(xm_act, 2)
            pe.wait_ge(xm_dve, 2)
            pe.wait_ge(kv_act, 2 * B * CTX // 512)
            for f in range(NF):
                for e in range(E0):
                    last = mm(ps[:, 6 + f // 2, (f % 2) * T:(f % 2 + 1) * T], w1[:, e, f * P:(f + 1) * P],
                              xm[:, :, e, :], start=(e == 0), stop=(e == E0 - 1))
                last.then_inc(h0_psum, 1)
            pe.wait_ge(load["w2"], 16)
            pe.wait_ge(g0_done, NF)
            for b in range(B):
                for eh in range(2):
                    for f in range(NF):
                        last = mm(ps[:, 2 * b + eh, :], g0[:, f, b * S:(b + 1) * S],
                                  w2[:, f, 4 * eh:4 * eh + 4, :].rearrange("p e d -> p (e d)"),
                                  start=(f == 0), stop=(f == NF - 1))
                    last.then_inc(y0_psum, 1)

            turn_xn(3)
            for g in range(4):
                last = mm(ps[:, g // 2, (g % 2) * T:(g % 2 + 1) * T], wq1[:, g, :], xnT[:], start=True, stop=True)
            last.then_inc(q1_psum, 1)
            pe.wait_ge(load["kstack"], 16 * 16)

            def scores1(m):
                c, u = m // UNITS, m % UNITS
                b, g = c // 4, c % 4
                if m >= 3:
                    pe.wait_ge(w1_done, m - 2)
                if u == 0:
                    pe.wait_ge(qbd_done, c + 1)
                for i in range(2):
                    at = b * CTX + (2 * u + i) * P
                    last = mm(ps[:, 2 * (m % 3) + i, :], kstack[:, g, at:at + P],
                              qbd[:, b, g, :, :].rearrange("p h s -> p (h s)"), start=True, stop=True)
                last.then_inc(s1_psum, 1)

            def weigh_v(m):
                c, u = m // UNITS, m % UNITS
                b, g = c // 4, c % 4
                if u == 0 and c >= 2:
                    pe.wait_ge(o1_copied, c - 1)
                pe.wait_ge(sq_done, m + 1)
                for i in range(2):
                    k = 2 * u + i
                    for j in range(4):
                        last = mm(ps[HR * j:HR * j + DA + 1, 6 + c % 2, 0:S], v1[:, b * NBLK + k, 4 * g + j, :],
                                  p_ring[:, m % 3, i * 512 + j * S:i * 512 + (j + 1) * S],
                                  start=(k == 0), stop=(k == NBLK - 1))
                last.then_inc(pv1_done, 1)

            pe.wait_ge(acc_zero, 1)
            for m in range(NU + 2):
                if m < NU:
                    scores1(m)
                if m >= 2:
                    weigh_v(m - 2)
            for c in range(COMBOS):
                if c % 4 == 0:
                    pe.wait_ge(o1_copied, c + 4)
                last = nc.tensor.transpose(ps[:, c // 4, (c % 4) * P:(c % 4 + 1) * P], oT1[:, c, :], ident[:])
            last.then_inc(o1_turned, 1)
            pe.wait_ge(o1_norm, 1)
            for b in range(B):
                last = nc.tensor.transpose(ps[:, 2, b * S:(b + 1) * S],
                                           attn1[:, b, :, :].rearrange("p h d -> p (h d)"), ident[:])
            last.then_inc(o1_turned2, 1)
            pe.wait_ge(o1_T, 1)
            for b in range(B):
                last = mm(ps[:, 3, b * D:(b + 1) * D], attn1T[:, b * S:(b + 1) * S], wkvo1[:, 2, :],
                          start=True, stop=True)
            last.then_inc(o1_proj, 1)

            turn_xn(4)
            pe.wait_ge(load["sa"], 16 * 5)
            for i in range(2):
                mm(ps[:, 0, i * T:(i + 1) * T], wqkv[:, i, :], xnT[:], start=True, stop=True)
            for b in range(B):
                last = mm(ps[:, 1, b * D:(b + 1) * D], xnT[:, b * S:(b + 1) * S], wqkv[:, 2, :],
                          start=True, stop=True)
            last.then_inc(sa_psum, 1)
            pe.wait_ge(sa_qk, 2)
            for b in range(B):
                last = mm(ps[:, 2, b * S:(b + 1) * S], qk_sa[:, 0, b * S:(b + 1) * S],
                          qk_sa[:, 1, b * S:(b + 1) * S], start=True, stop=True)
            last.then_inc(sa_score, 1)
            pe.wait_ge(sa_exp, B)
            for b in range(B):
                last = nc.tensor.transpose(ps[:, 3, b * S:(b + 1) * S], p_sa[:, b, :], ident[:])
            last.then_inc(sa_turned, 1)
            pe.wait_ge(sa_T, 1)
            pe.wait_ge(sa_v, 1)
            for b in range(B):
                last = mm(ps[:, 4, b * D:(b + 1) * D], pT_sa[:, b * S:(b + 1) * S], v_sa[:, b, :],
                          start=True, stop=True)
            last.then_inc(sa_out, 1)

            turn_xn(5)
            for b in range(B):
                last = mm(ps[:, 6, b * E1:(b + 1) * E1], xnT[:, b * S:(b + 1) * S], gate_w[:],
                          start=True, stop=True)
            last.then_inc(gt_psum, 1)
            pe.wait_ge(load["exp1"], 48)
            for i in range(EP):
                if i >= 2:
                    pe.wait_ge(h1_done, i - 1)
                for w, weights in enumerate((wg, wu)):
                    for r in range(2):
                        e = 2 * i + r
                        if e <= E1:
                            last = mm(ps[:, 2 * (i % 2) + w, r * T:(r + 1) * T], weights[:, e, :], xnT[:],
                                      start=True, stop=True)
                last.then_inc(gu_psum, 1)
            for i in range(E1 + 1):
                e = (i + E1) % (E1 + 1)
                if i >= 3:
                    pe.wait_ge(y1_added, i - 2)
                if i == 0:
                    pe.wait_ge(h1_done, EP)
                for b in range(B):
                    last = mm(ps[:, (4, 5, 7)[i % 3], b * D:(b + 1) * D], hT1[:, e, b * S:(b + 1) * S],
                              wd[:, e, :], start=True, stop=True)
                last.then_inc(y1_psum, 1)

        @block.scalar
        def _(act):
            def copy(dst, src):
                return nc.scalar.activation(dst, src, ACT.Copy)

            def copy_xnT(layer):
                act.wait_ge(xnT_psum, layer + 1)
                copy(xnT[:], ps[:, 5, 0:T]).then_inc(xnT_ready, 1)

            copy_xnT(0)
            for i in range(4):
                act.wait_ge(q0_psum, i + 1)
                copy(q0T[:, 2 * i:2 * i + 2, :].rearrange("p a t -> p (a t)"), ps[:, i, :]).then_inc(q0_sb, 1)
            for i in range(H // 2):
                act.wait_ge(qk_psum, i // 2 + 1)
                copy(qk_pair(qk_hi, i), qk_bank(i)).then_inc(qk_hi_done, 1)

            def hi(n):
                act.wait_ge(turned, n + 1)
                if n >= 3:
                    act.wait_ge(pv_done, n - 2)
                copy(pT_hi[:, n % 3, :], ps[:, 4 + n % 2, :]).then_inc(hi_done, 1)

            def exp_half(hs, p):
                q, j = hs // QUAD, hs % QUAD
                act.wait_ge(maxed, hs + 1)
                if hs == 0 and p == 0:
                    act.wait_ge(split_lo, 4)
                if q >= 2 and j == 0 and p == 0:
                    act.wait_ge(turned, NBLK * (q - 1))
                nc.scalar.activation(
                    probs[:, q % 2, j, p * 1024:(p + 1) * 1024].rearrange("p (a n) -> p a n", a=2),
                    ps[:, 2 * p:2 * p + 2, :], ACT.Exp, bias=nmax[:, hs % 2:hs % 2 + 1], scale=SCALE0,
                    accum_out=rowsum[:, hs, p:p + 1]).then_inc(exped, 1)

            def copy_u(q):
                act.wait_ge(pv_done, NBLK * (q + 1))
                if q >= 1:
                    act.wait_ge(o_psum, q)
                copy(u_sb[:], ps[:, 6 + q % 2, :]).then_inc(u_copied, 1)

            for step in range(NHS + QUAD):
                n0 = (step - QUAD) * QUAD
                if n0 >= 1:
                    hi(n0 - 1)
                if n0 >= 0:
                    hi(n0)
                    if n0 >= NBLK and n0 % NBLK == 0:
                        copy_u(n0 // NBLK - 1)
                    hi(n0 + 1)
                if step < NHS:
                    exp_half(step, 0)
                if n0 >= 0:
                    hi(n0 + 2)
                if step < NHS:
                    exp_half(step, 1)
            hi(NB0 - 1)
            copy_u(NQ - 1)
            act.wait_ge(a0_turned, 1)
            copy(attn0T[:, 0, :, :].rearrange("p (a t) s -> p a (t s)", a=2), ps[:, 0:2, :]).then_inc(a0T_act, 1)

            copy_xnT(1)
            act.wait_ge(lat_psum, 1)
            copy(lat_sb[:, 0, :], ps[0:LAT, 5, T:2 * T])
            copy(lat_sb[:, 1, :], ps[0:LAT, 4, T:2 * T]).then_inc(lat_copied, 1)
            act.wait_ge(vm_psum, 1)
            copy(vx[:, :, :, 0:DC], ps[:, 5, 0:T].rearrange("p (b h d) -> p b h d", b=B, h=H)).then_inc(vm_done, 1)
            for b in range(B):
                act.wait_ge(ms_clip, 2 * b + 2)
                nc.scalar.activation(pm[:, b, :, :].rearrange("p h s -> p (h s)"),
                                     clipped[:].rearrange("p h s -> p (h s)"), ACT.Exp,
                                     scale=SCALE_MLA).then_inc(ms_exp, 1)
            act.wait_ge(mo_turned, 1)
            copy(attn_mT[:], ps[:, 1, 0:T]).then_inc(mo_T, 1)

            copy_xnT(2)
            act.wait_ge(rt_z, 1)
            nc.scalar.activation(rt[:, 1, :, :], rt[:, 0, :, :], ACT.Exp, scale=-1.0).then_inc(rt_e, 1)
            for i in range(B * CTX // 512):
                act.wait_ge(kv_psum, 2 * i + 1)
                copy(k1_hi[:, i * 512:(i + 1) * 512], ps[:, 4, :]).then_inc(kv_act, 1)
                act.wait_ge(kv_psum, 2 * i + 2)
                copy(v1[:, 4 * i:4 * i + 4, :, 0:DA],
                     ps[:, 7, :].rearrange("p (k h d) -> p k h d", k=4, h=H)).then_inc(kv_act, 1)
            for i in range(2):
                act.wait_ge(xm_psum, i + 1)
                copy(xm[:, 0, 4 * i:4 * i + 4, :].rearrange("p e s -> p (e s)"), ps[:, i, :]).then_inc(xm_act, 1)
            for f in range(NF):
                act.wait_ge(h0_psum, 2 * (f // 2) + 2)
                nc.scalar.activation(g0[:, f, :], ps[:, 6 + f // 2, (f % 2) * T:(f % 2 + 1) * T],
                                     ACT.Gelu).then_inc(g0_done, 1)

            copy_xnT(3)
            act.wait_ge(q1_psum, 1)
            nc.scalar.activation(q1[:].rearrange("p (a g) t -> p a (g t)", a=2), ps[:, 0:2, :], ACT.Copy,
                                 scale=SCALE1).then_inc(q1_done, 1)

            def copy_o1(c):
                act.wait_ge(pv1_done, UNITS * (c + 1))
                copy(oT1[:, c, :], ps[:, 6 + c % 2, 0:S]).then_inc(o1_copied, 1)

            for m in range(NU):
                if m % UNITS == 2 and m >= UNITS:
                    copy_o1(m // UNITS - 1)
                act.wait_ge(w1_done, m + 1)
                if m >= 3:
                    act.wait_ge(pv1_done, m - 2)
                nc.scalar.activation(p_ring[:, m % 3, :], w_ring[:, m % 3, :], ACT.Square,
                                     bias=nbias[:]).then_inc(sq_done, 1)
            copy_o1(COMBOS - 1)
            act.wait_ge(o1_turned2, 1)
            copy(attn1T[:], ps[:, 2, 0:T]).then_inc(o1_T, 1)

            copy_xnT(4)
            act.wait_ge(sa_psum, 1)
            for i in range(2):
                nc.scalar.activation(qk_sa[:, i, :], ps[:, 0, i * T:(i + 1) * T], ACT.Identity,
                                     bias=bqk[:, i:i + 1]).then_inc(sa_qk, 1)
            act.wait_ge(sa_max, 1)
            for b in range(B):
                nc.scalar.activation(p_sa[:, b, :], ps[:, 2, b * S:(b + 1) * S], ACT.Exp,
                                     bias=mx_sa[:, 1, b:b + 1], scale=SCALE_SA,
                                     accum_out=mx_sa[:, 2, b:b + 1]).then_inc(sa_exp, 1)
            act.wait_ge(sa_turned, 1)
            copy(pT_sa[:], ps[:, 3, 0:T]).then_inc(sa_T, 1)

            copy_xnT(5)
            act.wait_ge(gt_z, 1)
            nc.scalar.activation(sc1[:, 1, :, :], sc1[:, 0, :, :], ACT.Exp, scale=-1.0).then_inc(gt_e, 1)
            for i in range(EP):
                n = T * (2 if 2 * i + 1 <= E1 else 1)
                act.wait_ge(gu_psum, i + 1)
                if i >= 2:
                    act.wait_ge(h1_done, i - 1)
                nc.scalar.activation(silu_g[:, i % 2, 0:n], ps[:, 2 * (i % 2), 0:n], ACT.Silu)\
                    .then_inc(silu_done, 1)

        @block.gpsimd
        def _(pool):
            pool.wait_ge(load["small"], 16 * N_SMALL)
            pool.wait_ge(load["x"], 32)
            nc.gpsimd.tensor_tensor(xb[:], x[:], bc(bias_rows[:, 0:D], 1, B), ALU.add).then_inc(xb_done, 1)
            pool.wait_ge(a0_turned, 1)
            nc.gpsimd.memset(vx[:, :, :, DC:DC + 1], 1.0).then_inc(ones_done, 1)
            nc.gpsimd.memset(v1[:, :, :, DA:DA + 1], 1.0).then_inc(ones_done, 1)
            nc.gpsimd.tensor_scalar(neg_nbias[:], nbias[:], -1.0, None, ALU.mult).then_inc(ones_done, 1)
            pool.wait_ge(ones_done, 3)
            pool.wait_ge(load["mask"], 16)
            for b in range(B):
                pool.wait_ge(ms_exp, b + 1)
                nc.gpsimd.affine_select(out=pm[:, b, :, :], in_=pm[:, b, :, :], compare_op=ALU.is_ge, fill=0.0,
                                        base=0, pattern=[[0, H], [1, S]], channel_multiplier=-1)\
                    .then_inc(ms_masked, 1)

        @block.vector
        def _(dve):
            v = nc.vector
            links = [0]

            def link(ins_):
                links[0] += 1
                ins_.then_inc(chain, 1)
                dve.wait_ge(chain, links[0])

            def layer_norm(layer):
                for b in range(B):
                    s = v.bn_stats(stats[:, b, :], x[:, b, :])
                link(s)
                for b in range(B):
                    s = v.bn_aggr(mv[:, b, :], stats[:, b, :])
                link(s)
                var, y, t = nwt[:, 0, :], nwt[:, 1, :], nwt[:, 2, :]
                link(v.tensor_scalar(var, mv[:, :, 1], EPS, None, ALU.add))
                link(v.tensor_scalar(seed[:, 0, :], var.bitcast(I32), 1, None, ALU.logical_shift_right))
                link(v.tensor_scalar(y.bitcast(I32), seed[:, 0, :], -1.0, float(RSQRT_SEED), ALU.mult, ALU.add))
                for _ in range(3):
                    link(v.tensor_tensor(t, y, y, ALU.mult))
                    link(v.scalar_tensor_tensor(t, t, -0.5, var, ALU.mult, ALU.mult))
                    link(v.scalar_tensor_tensor(y, t, 1.5, y, ALU.add, ALU.mult))
                for b in range(B):
                    s = v.tensor_scalar(xn[:, b, :], x[:, b, :], mv[:, b, 0:1], nwt[:, 1, b:b + 1],
                                        ALU.subtract, ALU.mult)
                s.then_inc(xn_ready, 1)

            dve.wait_ge(load["x"], 32)
            layer_norm(0)

            def split(hi_t, lo_t, raw, which):
                dve.wait_ge(load[which], 16)
                link(v.tensor_copy(hi_t, raw))
                v.tensor_tensor(lo_t, raw, hi_t, ALU.subtract).then_inc(split_lo, 1)

            def qk_rest(i):
                dve.wait_ge(qk_hi_done, i + 1)
                v.tensor_tensor(qk_pair(qk_lo, i), qk_bank(i), qk_pair(qk_hi, i),
                                ALU.subtract).then_inc(qk_lo_done, 1)

            half = slice(0, CTX), slice(CTX, 2 * CTX)
            rows = slice(0, NBLK), slice(NBLK, 2 * NBLK)
            split(ctxT_hi[:, half[0]], ctxT_lo[:, half[0]], ctxT_raw[:, half[0]], "ctxT0")
            for i in range(H // 2):
                qk_rest(i)
            split(ctx_hi[:, rows[0], :], ctx_lo[:, rows[0], :], ctx_raw[:, rows[0], :], "ctx0")
            split(ctxT_hi[:, half[1]], ctxT_lo[:, half[1]], ctxT_raw[:, half[1]], "ctxT1")
            split(ctx_hi[:, rows[1], :], ctx_lo[:, rows[1], :], ctx_raw[:, rows[1], :], "ctx1")

            def lo(n):
                dve.wait_ge(hi_done, n + 1)
                v.tensor_tensor(pT_lo[:, n % 3, :], ps[:, 4 + n % 2, :], pT_hi[:, n % 3, :],
                                ALU.subtract).then_inc(lo_done, 1)

            def half_max(hs, p):
                dve.wait_ge(scored, 2 * hs + p + 1)
                return v.tensor_reduce(max2[:, p:p + 1], ps[:, 2 * p:2 * p + 2, :], AX.XY, ALU.max)

            def copy_o(q):
                hs = q * QUAD
                b, h = hs // H, hs % H
                r = rden[:, q % 2, :]
                dve.wait_ge(exped, 2 * QUAD * (q + 1))
                link(v.tensor_tensor(r, rowsum[:, hs:hs + QUAD, 0], rowsum[:, hs:hs + QUAD, 1], ALU.add))
                link(v.reciprocal(r, r))
                dve.wait_ge(o_psum, q + 1)
                v.tensor_tensor(attn0[:, b, h * DH:(h + QUAD) * DH].rearrange("p (j d) -> p j d", j=QUAD),
                                ps[:, 6 + q % 2, 0:QUAD * DH].rearrange("p (j d) -> p j d", j=QUAD),
                                bc(r, 2, DH), ALU.mult).then_inc(o_copied, 1)

            for step in range(NHS + QUAD):
                n0 = (step - QUAD) * QUAD
                if n0 >= 1:
                    lo(n0 - 1)
                if step < NHS:
                    half_max(step, 0)
                if n0 >= 0:
                    lo(n0)
                if step < NHS:
                    link(half_max(step, 1))
                    v.tensor_scalar(nmax[:, step % 2:step % 2 + 1], max2[:, 0:1], max2[:, 1:2], -SCALE0,
                                    ALU.max, ALU.mult).then_inc(maxed, 1)
                if n0 >= 0:
                    lo(n0 + 1)
                    if n0 > NBLK and n0 % NBLK == QUAD:
                        copy_o(n0 // NBLK - 1)
                    lo(n0 + 2)
            lo(NB0 - 1)
            copy_o(NQ - 1)
            dve.wait_ge(a0_turned, 1)
            v.tensor_copy(attn0T[:, 1, :, :].rearrange("p (a t) s -> p a (t s)", a=2), ps[:, 2:4, :])\
                .then_inc(a0T_dve, 1)
            dve.wait_ge(proj0, 1)
            dve.wait_ge(xb_done, 1)
            link(v.tensor_tensor(x[:].rearrange("p b d -> p (b d)"), ps[:, 4, 0:T],
                                 xb[:].rearrange("p b d -> p (b d)"), ALU.add))

            layer_norm(1)
            cos, sin = rope[:, 0, :], rope[:, 1, :]
            rows_gb = "p g (b s) -> p (g b) s"

            def banks(a):
                return ps[:, a:a + 2, :].rearrange("p a (g s) -> p (a g) s", s=S)

            dve.wait_ge(qkr_psum, 1)
            v.tensor_tensor(ropet[:].rearrange(rows_gb, b=B), banks(2), bc(sin, 1, 8), ALU.mult)
            link(v.tensor_tensor(qr[:].rearrange(rows_gb, b=B), banks(0), bc(cos, 1, 8), ALU.mult))
            v.tensor_tensor(qr[:], qr[:], ropet[:], ALU.add).then_inc(qr_done, 1)
            dve.wait_ge(qkr_psum, 2)
            v.tensor_tensor(ropek[:].rearrange("p (b s) -> p b s", b=B),
                            ps[:, 4, 0:T].rearrange("p (b s) -> p b s", b=B), bc(sin, 1, B), ALU.mult)
            link(v.tensor_tensor(kr[:].rearrange(rows_gb, b=B), banks(6), bc(cos, 1, 8), ALU.mult))
            v.tensor_tensor(kr[:], kr[:], bc(ropek[:], 1, 4), ALU.add).then_inc(kr_done, 1)
            for b in range(B):
                dve.wait_ge(ms_psum, b + 1)
                if b:
                    dve.wait_ge(ms_exp, b)
                for i in range(2):
                    v.tensor_scalar(clipped[:, 8 * i:8 * i + 8, :].rearrange("p (a g) s -> p a (g s)", a=2),
                                    ps[:, 4 * b + 2 * i:4 * b + 2 * i + 2, :], CLIP, -CLIP,
                                    ALU.min, ALU.max).then_inc(ms_clip, 1)
            dve.wait_ge(mo_psum, 1)
            heads = ps[:, 0, 0:B * H * (DC + 1)].rearrange("p (h d) -> p h d", d=DC + 1)
            link(v.reciprocal(rl_m[:], heads[:, :, DC]))
            v.tensor_tensor(attn_m[:].rearrange("p b h d -> p (b h) d"), heads[:, :, 0:DC],
                            bc(rl_m[:], 2, DC), ALU.mult).then_inc(mo_norm, 1)
            dve.wait_ge(mo_proj, 1)
            xf = x[:].rearrange("p b d -> p (b d)")
            link(v.tensor_tensor(xf, ps[:, 2, 0:T], xf, ALU.add))

            layer_norm(2)
            z, ez, r, eq, onehot = (rt[:, i, :, :] for i in range(5))
            dve.wait_ge(rt_psum, 1)
            v.tensor_tensor(z, ps[:, 6, 0:B * E0].rearrange("p (b e) -> p b e", b=B),
                            bc(br_sb[:], 1, B), ALU.add).then_inc(rt_z, 1)
            dve.wait_ge(rt_e, 1)
            link(v.tensor_scalar(ez, ez, 1.0, None, ALU.add))
            link(v.reciprocal(r, ez))
            link(v.tensor_reduce(rtm[:, 0, :], r, AX.X, ALU.max))
            link(v.tensor_tensor(eq, r, bc(rtm[:, 0, :], 2, E0), ALU.is_equal))
            link(v.tensor_tensor(eq, eq, bc(rank_sb[:], 1, B), ALU.mult))
            link(v.tensor_reduce(rtm[:, 1, :], eq, AX.X, ALU.max))
            link(v.tensor_tensor(onehot, eq, bc(rtm[:, 1, :], 2, E0), ALU.is_equal))
            dve.wait_ge(load["mask"], 16)
            dve.wait_ge(ones_done, 3)
            link(v.tensor_scalar(cap[:], mask_sb[:], 0.0, BIG, ALU.is_equal, ALU.mult))
            v.scalar_tensor_tensor(cap[:], mask_sb[:], neg_nbias[:], cap[:], ALU.mult, ALU.add)\
                .then_inc(cap_done, 1)
            dve.wait_ge(cap_done, 1)
            for b in range(B):
                s = v.tensor_tensor(diag[:, b, :, :], bc(ident[:], 1, E0), bc(onehot[:, b, :], 2, S), ALU.mult)
            s.then_inc(diag_done, 1)
            link(v.tensor_tensor(eq, onehot, bc(rtm[:, 0, :], 2, E0), ALU.mult))
            for i in range(B * CTX // 512):
                dve.wait_ge(kv_act, 2 * i + 1)
                v.tensor_tensor(k1_lo[:, i * 512:(i + 1) * 512], ps[:, 4, :], k1_hi[:, i * 512:(i + 1) * 512],
                                ALU.subtract).then_inc(k1_split, 1)
            for i in range(2):
                dve.wait_ge(xm_psum, 3 + i)
                v.tensor_copy(xm[:, 1, 4 * i:4 * i + 4, :].rearrange("p e s -> p (e s)"), ps[:, 2 + i, :])\
                    .then_inc(xm_dve, 1)
            for b in range(B):
                dve.wait_ge(y0_psum, 2 * b + 2)
                link(v.tensor_tensor(yw[:], ps[:, 2 * b:2 * b + 2, :].rearrange("p a (e d) -> p (a e) d", d=D),
                                     bc(eq[:, b, :], 2, D), ALU.mult))
                link(v.tensor_reduce(xb[:, b, :], yw[:].rearrange("p e d -> p d e"), AX.X, ALU.add))
            link(v.tensor_tensor(x[:], x[:], xb[:], ALU.add))

            layer_norm(3)
            dve.wait_ge(q1_done, 1)
            link(v.tensor_copy(q1s[:], q1[:]))
            link(v.tensor_tensor(q1s[64:128], q1[64:128], q1s[64:128], ALU.subtract))

            def spread_q(c):
                b, g = c // 4, c % 4
                v.tensor_tensor(qbd[:, b, g, :, :], bc(q1s[:, g, b * S:(b + 1) * S], 1, 4),
                                bc(headsel[:], 2, S), ALU.mult).then_inc(qbd_done, 1)

            spread_q(0)
            v.memset(ps[:, 6:8, :], 0.0).then_inc(acc_zero, 1)
            dve.wait_ge(load["kstack"], 256)
            for m in range(NU):
                c, u = m // UNITS, m % UNITS
                if u == 1 and c + 1 < COMBOS:
                    spread_q(c + 1)
                dve.wait_ge(s1_psum, m + 1)
                if m >= 3:
                    dve.wait_ge(sq_done, m - 2)
                k = (c // 4) * NBLK + 2 * u
                for i in range(2):
                    s = v.scalar_tensor_tensor(
                        w_ring[:, m % 3, i * 512:(i + 1) * 512].rearrange("p (h s) -> p h s", h=4),
                        ps[:, 2 * (m % 3) + i, :].rearrange("p (h s) -> p h s", h=4), neg_nbias[:],
                        bc(cap[:, k + i, :], 1, 4), ALU.max, ALU.min)
                s.then_inc(w1_done, 1)
            dve.wait_ge(o1_turned, 1)
            for b in range(B):
                o4 = ps[:, b, :].rearrange("p (h d) -> p h d", d=HR)
                r4 = rl1[:, 4 * b:4 * b + 4, :].rearrange("p g j -> p (g j)")
                link(v.tensor_scalar(r4, o4[:, :, DA], TINY, None, ALU.add))
                link(v.reciprocal(r4, r4))
                s = v.tensor_tensor(attn1[:, b, :, :], o4[:, :, 0:DA], bc(r4, 2, DA), ALU.mult)
            s.then_inc(o1_norm, 1)
            dve.wait_ge(o1_proj, 1)
            link(v.tensor_tensor(xf, ps[:, 3, 0:T], xf, ALU.add))

            layer_norm(4)
            dve.wait_ge(sa_psum, 1)
            v.tensor_tensor(v_sa[:], ps[:, 1, 0:T].rearrange("p (b d) -> p b d", b=B),
                            bc(bias_rows[:, D:2 * D], 1, B), ALU.add).then_inc(sa_v, 1)
            dve.wait_ge(sa_score, 1)
            link(v.tensor_reduce(mx_sa[:, 0, :], ps[:, 2, 0:T].rearrange("p (b s) -> p b s", b=B), AX.X, ALU.max))
            v.tensor_scalar(mx_sa[:, 1, :], mx_sa[:, 0, :], -SCALE_SA, None, ALU.mult).then_inc(sa_max, 1)
            dve.wait_ge(sa_exp, B)
            link(v.reciprocal(mx_sa[:, 3, :], mx_sa[:, 2, :]))
            dve.wait_ge(sa_out, 1)
            for b in range(B):
                s = v.scalar_tensor_tensor(x[:, b, :], ps[:, 4, b * D:(b + 1) * D], mx_sa[:, 3, b:b + 1],
                                           x[:, b, :], ALU.mult, ALU.add)
            link(s)

            layer_norm(5)
            z, ez, score, sel = (sc1[:, i, :, :] for i in range(4))
            dve.wait_ge(gt_psum, 1)
            v.tensor_copy(z, ps[:, 6, 0:B * E1].rearrange("p (b e) -> p b e", b=B)).then_inc(gt_z, 1)
            dve.wait_ge(gt_e, 1)
            link(v.tensor_scalar(ez, ez, 1.0, None, ALU.add))
            link(v.reciprocal(score, ez))
            link(v.tensor_tensor(sel, score, bc(gate_b[:], 1, B), ALU.add))
            for b in range(B):
                ge, gt = cmp1[:, 0, b, :, :], cmp1[:, 1, b, :, :]
                mine, other = bc(sel[:, b, :], 2, E1), bc(sel[:, b, :], 1, E1)
                v.tensor_tensor(gt, other, mine, ALU.is_gt)
                link(v.tensor_tensor(ge, other, mine, ALU.is_ge))
                link(v.tensor_tensor(ge, ge, below[:], ALU.mult))
                link(v.tensor_tensor(gt, gt, ge, ALU.max))
                link(v.tensor_reduce(comb[:, b, :], gt, AX.X, ALU.add))
            link(v.scalar_tensor_tensor(comb[:], comb[:], TOPK - 0.5, score, ALU.is_lt, ALU.mult))
            link(v.tensor_reduce(csum[:, 0, :], comb[:], AX.X, ALU.add))
            link(v.reciprocal(csum[:, 1, :], csum[:, 0, :]))
            for b in range(B):
                s = v.tensor_scalar(comb[:, b, :], comb[:, b, :], csum[:, 1, b:b + 1], ROUTE_SCALE,
                                    ALU.mult, ALU.mult)
            link(s)
            for i in range(EP):
                n = T * (2 if 2 * i + 1 <= E1 else 1)
                dve.wait_ge(silu_done, i + 1)
                v.tensor_tensor(hT1[:, 2 * i:2 * i + n // T, :].rearrange("p e t -> p (e t)"),
                                ps[:, 2 * (i % 2) + 1, 0:n], silu_g[:, i % 2, 0:n], ALU.mult).then_inc(h1_done, 1)
            for i in range(E1 + 1):
                dve.wait_ge(y1_psum, i + 1)
                for b in range(B):
                    y = ps[:, (4, 5, 7)[i % 3], b * D:(b + 1) * D]
                    if i == 0:
                        s = v.tensor_tensor(x[:, b, :], y, x[:, b, :], ALU.add)
                    else:
                        s = v.scalar_tensor_tensor(x[:, b, :], y, comb[:, b, i - 1:i], x[:, b, :],
                                                   ALU.mult, ALU.add)
                s.then_inc(y1_added, 1)
                dve.wait_ge(y1_added, i + 1)


N_SMALL = 12


def _rope_tables():
    inv = np.float32(10000.0) ** (-np.arange(0, DR, 2, dtype=np.float32) / np.float32(DR))
    ang = np.arange(S, dtype=np.float32)[:, None] * inv
    table = np.zeros((4, HR, 2, S), np.float32)
    table[:, :DC, 0] = 1.0
    for r in range(DR):
        table[:, DC + r, 0] = np.cos(ang[:, r // 2])
        table[:, DC + r, 1] = np.sin(ang[:, r // 2]) * (-1.0 if r % 2 == 0 else 1.0)
    return table.reshape(P, 2, S)


def _layout(a):
    ctx = a["ctx_1024"]
    swap = [1, 0, 3, 2]
    uq = a["L0_attn_W_UQ"].reshape(LAT, 4, 4, DC)
    qr = a["L0_attn_W_QR"].reshape(LAT, 4, 4, DR)
    wq_mla = np.zeros((LAT, 2, 4, 4, HR), np.float32)
    wq_mla[:, 0, :, :, :DC] = uq
    wq_mla[:, 0, :, :, DC:DC + DR] = qr
    wq_mla[:, 1, :, :, DC:DC + DR] = qr[..., swap]
    wk_mla = np.zeros((LAT, 4, 4, HR), np.float32)
    wk_mla[..., :DC] = a["L0_attn_W_UK"].reshape(LAT, 4, 4, DC)
    wkr = np.zeros((D, 2, 4, HR), np.float32)
    wkr[:, 0, :, DC:DC + DR] = a["L0_attn_W_KR"][:, None, :]
    wkr[:, 1, :, DC:DC + DR] = a["L0_attn_W_KR"][:, None, swap]
    wq1 = a["L1_xattn_Wq"].T.reshape(D, 4, 1, 4 * DA)
    e = np.arange(E1)
    rows = lambda v, n: np.broadcast_to(v[None, :], (P, n))
    return {
        "x_tok": a["x"].transpose(1, 0, 2),
        "ctx_nat": ctx.reshape(B * NBLK, P, D).transpose(1, 0, 2),
        "ctx_t": ctx.reshape(B * CTX, D).T,
        "mask_t": a["mask_BxSxS2_bk0"].reshape(B, S, NBLK, P).transpose(3, 0, 2, 1).reshape(P, B * NBLK, S),
        "wq0": a["L0_xattn_Wq"],
        "wk0_t": a["L0_xattn_Wkv"][:, :H * DH].T.reshape(H // 2, P, D).transpose(1, 0, 2),
        "wv0": a["L0_xattn_Wkv"][:, H * DH:],
        "wo0": a["L0_xattn_Wo"].reshape(H // 2, P, D).transpose(1, 0, 2),
        "bo0": rows(a["L0_xattn_bo"], D),
        "w_lat": np.concatenate([a["L0_attn_W_DQ"], a["L0_attn_W_DKV"]], 1),
        "wq_mla": wq_mla.reshape(LAT, 2, 4, P), "wk_mla": wk_mla.reshape(LAT, 4, P),
        "wkr_mla": wkr.reshape(D, 2, P),
        "wuv": a["L0_attn_W_UV"], "wo_mla": a["L0_attn_W_O"], "rope": _rope_tables(),
        "wr": a["L0_ffn_Wr"], "br": rows(a["L0_ffn_br"], E0),
        "w1": a["L0_ffn_W1"].transpose(1, 0, 2),
        "w2": a["L0_ffn_W2"].reshape(E0, NF, P, D).transpose(2, 1, 0, 3),
        "rank": rows(np.arange(E0, 0, -1, dtype=np.float32), E0),
        "wq1": np.broadcast_to(wq1, (D, 4, 4, 4 * DA)).reshape(D, 4, P),
        "wk1": a["L1_xattn_Wkv"][:D].T, "wv1": a["L1_xattn_Wkv"][D:].T, "wo1": a["L1_xattn_Wo"].T,
        "nbias": np.broadcast_to(a["L1_xattn_nbias"][None, :], (P, 1)),
        "headsel": ((np.arange(P)[:, None] % HR) // DA == np.arange(4)).astype(np.float32),
        "wqkv_sa": np.stack([a["L1_attn_W_q"], a["L1_attn_W_k"], a["L1_attn_W_v"]], 1),
        "bqk_sa": np.stack([a["L1_attn_b_q"], a["L1_attn_b_k"]], 1),
        "bv_sa": rows(a["L1_attn_b_v"], D),
        "gate_w": a["L1_ffn_gate_w"].T, "gate_b": rows(a["L1_ffn_expert_bias"], E1),
        "below": np.broadcast_to((e[None, :] < e[:, None]).astype(np.float32), (P, E1, E1)),
        "wg": np.concatenate([a["L1_ffn_w_gate"], a["L1_ffn_shared_gate_w"][None]]).transpose(2, 0, 1),
        "wu": np.concatenate([a["L1_ffn_w_up"], a["L1_ffn_shared_up_w"][None]]).transpose(2, 0, 1),
        "wd": np.concatenate([a["L1_ffn_w_down"], a["L1_ffn_shared_down_w"][None]]).transpose(2, 0, 1),
        "ident": np.eye(P, dtype=np.float32),
    }


def kernel(**inputs):
    import concourse.bacc as bacc
    from concourse.bass_utils import run_bass_kernel_spmd

    nc = bacc.Bacc("TRN2", target_bir_lowering=False, num_devices=1)
    arrays = {k: np.ascontiguousarray(v) for k, v in
              _layout({k: np.asarray(v) for k, v in inputs.items()}).items()}
    ins = {}
    for name, shape in INPUTS.items():
        a = arrays[name]
        assert a.shape == shape, (name, a.shape, shape)
        ins[name] = nc.dram_tensor(f"in_{name}", shape, mybir.dt.from_np(a.dtype), kind="ExternalInput").ap()
    out = nc.dram_tensor("out_x", (B, S, D), F32, kind="ExternalOutput").ap()
    build(nc, ins, out)
    r = run_bass_kernel_spmd(nc, [{f"in_{k}": arrays[k] for k in INPUTS}], core_ids=[0])
    return r.results[0]["out_x"]
```

```python
from contextlib import ExitStack
import math

import numpy as np
import concourse.bass as bass
from concourse import mybir

F32 = mybir.dt.float32
F32R = mybir.dt.float32r
I32 = mybir.dt.int32
U8 = mybir.dt.uint8
ALU = mybir.AluOpType
ACT = mybir.ActivationFunctionType
AX = mybir.AxisListType

P = 128
B = 2
S = 128
T = B * S
D = 128
CTX = 2048
NBLK = CTX // P
H = 16
DH = 64
QUAD = 4
NQ = B * H // QUAD
CH = CTX // 512
SCALE0 = DH ** -0.5
LAT = 32
DC = D // H
DR = DC // 2
HR = 32
CLIP = 80.0
SCALE_MLA = 1.0 / math.sqrt(DC + DR)
E0 = 8
FF = 512
NF = FF // P
DA = D // H
SCALE1 = 1.0 / math.sqrt(DA)
BIG = 1.0e38
TINY = 1e-32
SCALE_SA = 1.0 / math.sqrt(D)
E1 = 16
TOPK = 8
ROUTE_SCALE = 2.826
EPS = 1e-5
RSQRT_SEED = 0x5F3759DF

FILLS = (3, 5, 4, 4)

WARM = 8

INPUTS = {
    "x_tok": (S, B, D), "ctx_nat": (P, B * NBLK, D), "ctx_t": (D, B * CTX),
    "mask_t": (P, B * NBLK, S),
    "wq0": (D, H * DH), "wk0_t": (P, H, D), "wv0": (D, H * DH), "wo0": (P, H // 2, D), "bo0": (P, D),
    "w_lat": (D, P), "wq_mla": (P, 2, 4, P), "wk_mla": (P, 5, P), "wuv": (P, D), "wo_mla": (D, D), "rope": (P, 2, S),
    "wr": (D, E0), "br": (P, E0), "w1": (D, E0, FF), "w2": (P, NF, E0, D), "rank": (P, E0),
    "wq1": (D, 4, P), "wkvo1": (D, 3, D), "nbias": (P, 1), "headsel": (P, 4),
    "wqkv_sa": (D, 3, D), "bqk_sa": (D, 2), "bv_sa": (P, D),
    "gate_w": (D, E1), "gate_b": (P, E1), "below": (P, E1, E1),
    "wg": (D, E1 + 1, P), "wu": (D, E1 + 1, P), "wd": (P, E1 + 1, D),
    "ident": (P, P),
}


class Arena:

    def __init__(self, nc, start, end):
        self.nc, self.at, self.end = nc, start, end

    def take(self, name, shape, dt=F32):
        size = int(np.prod(shape[1:])) * (1 if dt == U8 else 4)
        t = self.nc.alloc_sbuf_tensor_at(name, list(shape), dt, offset=self.at)
        self.at += -(-size // 32) * 32
        assert self.at <= self.end, (name, self.at - self.end)
        return t


def build(nc, ins, out):
    with ExitStack() as ctx:
        def sem(name):
            return ctx.enter_context(nc.semaphore(name))

        def bc(ap, axis, n):
            ap = ap.unsqueeze(axis)
            shape = list(ap.shape)
            shape[axis] = n
            return ap.to_broadcast(shape)

        start = -(-nc.sbuf_base // 32) * 32
        end = nc.sbuf_usable_end
        A = Arena(nc, start, end)
        x = A.take("x", (P, B, D))
        xn = A.take("xn", (P, B, D))
        xnT = A.take("xnT", (P, T))
        ident = A.take("ident_sb", (P, P))
        headsel = A.take("headsel_sb", (P, 4))
        nbias = A.take("nbias_sb", (P, 1))
        neg_nbias = A.take("neg_nbias", (P, 1))
        bias_rows = A.take("bias_rows", (P, 2 * D))
        br_sb = A.take("br_sb", (P, E0))
        rank_sb = A.take("rank_sb", (P, E0))
        wr_sb = A.take("wr_sb", (P, E0))
        w_lat = A.take("w_lat_sb", (P, P))
        wuv = A.take("wuv_sb", (P, D))
        wo_mla = A.take("wo_mla_sb", (P, D))
        rope = A.take("rope_sb", (P, 2, S))
        stats = A.take("stats", (P, B, 6))
        mv = A.take("mv", (P, B, 2))
        nwt = A.take("nwt", (P, 4, B))
        seed = A.take("seed", (P, 2, B), I32)
        max2 = A.take("max2", (P, 2 * 2))
        nmax = A.take("nmax", (P, 2))
        rowsum = A.take("rowsum", (P, B * H, 2))
        rden = A.take("rden", (P, 2, QUAD))
        xb = A.take("xb", (P, B, D))
        zeros = A.take("zeros", (P, T))
        attn0 = A.take("attn0", (P, B, H * DH))
        attn0_at = A.at - B * H * DH * 4
        wv0 = A.take("wv0_sb", (P, H * DH))
        wo0 = A.take("wo0_sb", (P, H // 2, D))
        wo0_at = A.at - H // 2 * D * 4
        stage = A.at

        A = Arena(nc, stage, end)
        ctxT_hi = A.take("ctxT_hi", (P, B * CTX), F32R)
        ctxT_lo = A.take("ctxT_lo", (P, B * CTX), F32R)
        probs_at = A.at
        probs = A.take("probs", (P, 2, QUAD, CTX))
        qk_at = A.at
        qk_hi = A.take("qk_hi", (P, H, B, S), F32R)
        qk_lo = A.take("qk_lo", (P, H, B, S), F32R)
        ctx_at = A.at
        ctx_hi = A.take("ctx_hi", (P, B * NBLK, D), F32R)
        ctx_lo = A.take("ctx_lo", (P, B * NBLK, D), F32R)
        pT_at = A.at
        pT_hi = A.take("pT_hi", (P, 3, 512), F32R)
        pT_lo = A.take("pT_lo", (P, 3, 512), F32R)
        u_sb = A.take("u_sb", (P, 512))
        A = Arena(nc, probs_at + QUAD * CTX * 4, qk_at)
        ctx_raw1 = A.take("ctx_raw1", (P, 2, CTX))
        wq0 = A.take("wq0_sb", (P, H * DH))
        wk0_t = A.take("wk0_t_sb", (P, H, D))
        q0T = A.take("q0T", (P, 2, 2, T))
        ctxT_raw0 = Arena(nc, pT_at, end).take("ctxT_raw0", (P, CTX))
        ctx_raw0 = Arena(nc, attn0_at, stage).take("ctx_raw0", (P, CTX))

        A = Arena(nc, stage, probs_at)
        w1 = A.take("w1_sb", (P, E0, FF))
        w2 = A.take("w2_sb", (P, NF, E0, D))
        A = Arena(nc, stage, probs_at)
        wg = A.take("wg_sb", (P, E1 + 1, P))
        wu = A.take("wu_sb", (P, E1 + 1, P))
        wd = A.take("wd_sb", (P, E1 + 1, D))
        oT1 = A.take("oT1", (P, 2 * 4, S))
        keep = A.take("keep", (P, B, 2 * S))
        A = Arena(nc, probs_at, qk_at)
        attn0T = A.take("attn0T", (P, B, H // 2, S))
        lat_at = A.at
        lat_sb = A.take("lat_sb", (P, T))
        qr_at = A.at
        qr = A.take("qr", (P, 4, T))
        kr_at = A.at
        kr = A.take("kr", (P, 4, T))
        ropet_at = A.at
        ropet = A.take("ropet", (P, 4, T))
        ropek = A.take("ropek", (P, T))
        vx = A.take("vx", (P, B, H, HR))
        qbd_m = A.take("qbd_m", (P, B, 4, 4, S))
        pm = A.take("pm", (P, B, 4, 4, S))
        rl_m = A.take("rl_m", (P, B, H))
        wq_mla = A.take("wq_mla_sb", (P, 2, 4, P))
        clipped = Arena(nc, probs_at, lat_at).take("clipped", (P, 2, 1024))
        A = Arena(nc, qr_at, kr_at)
        oTm = A.take("oTm", (P, B, 4, S))
        A = Arena(nc, ropet_at, qk_at)
        attn_m = A.take("attn_m", (P, B, H, DC))
        attn_mT = A.take("attn_mT", (P, T))
        A = Arena(nc, probs_at, qk_at)
        kstack = A.take("kstack", (P, 4, B * CTX), F32R)
        A = Arena(nc, probs_at, qk_at)
        qk_sa = A.take("qk_sa", (P, 2, T))
        v_sa = A.take("v_sa", (P, B, D))
        p_sa = A.take("p_sa", (P, B, S))
        pT_sa = A.take("pT_sa", (P, T))
        mx_sa = A.take("mx_sa", (P, 4, B))
        wqkv = A.take("wqkv_sb", (P, 3, D))
        bqk = A.take("bqk_sb", (P, 2))
        gate_w = A.take("gate_w_sb", (P, E1))
        gate_b = A.take("gate_b_sb", (P, E1))
        below = A.take("below_sb", (P, E1, E1))
        sc1 = A.take("sc1", (P, 4, B, E1))
        cmp1 = A.take("cmp1", (P, 3, B, E1, E1))
        comb = A.take("comb", (P, B, E1))
        csum = A.take("csum", (P, 2, B))
        silu_g = A.take("silu_g", (P, 2, 512))
        hT1 = A.take("hT1", (P, E1 + 1, T))
        A = Arena(nc, qk_at, ctx_at)
        ctxT_raw2 = A.take("ctxT_raw2", (P, B * CTX))
        cap = A.take("cap", (P, B * NBLK, S))
        A = Arena(nc, qk_at, ctx_at)
        xm = A.take("xm", (P, B, E0, S))
        g0 = A.take("g0", (P, NF, T))
        yw = A.take("yw", (P, E0, D))
        A = Arena(nc, qk_at, ctx_at)
        qbd = A.take("qbd", (P, B, 4, 4, S), F32R)
        A = Arena(nc, ctx_at, end)
        k1_hi = A.take("k1_hi", (P, B * CTX), F32R)
        k1_lo = A.take("k1_lo", (P, B * CTX), F32R)
        v1_at = A.at
        v1 = A.take("v1", (P, B * NBLK, H, DA + 1))
        k1_raw = Arena(nc, v1_at, end).take("k1_raw", (P, B * CTX))
        A = Arena(nc, ctx_at, end)
        w_ring = A.take("w_ring", (P, 3, 1024))
        p_ring = A.take("p_ring", (P, 3, 1024))
        w_first = A.take("w_first", (P, 1024))
        attn1 = A.take("attn1", (P, B, H, DA))
        attn1T = A.take("attn1T", (P, T))
        rl1 = A.take("rl1", (P, 2 * 4, 4))
        A = Arena(nc, attn0_at, attn0_at + B * H * DH * 4)
        wk_mla = A.take("wk_mla_sb", (P, 5, P))
        A2 = Arena(nc, attn0_at, attn0_at + B * H * DH * 4)
        diag = A2.take("diag", (P, B, E0, S))
        A2 = Arena(nc, attn0_at, attn0_at + B * H * DH * 4)
        q1 = A2.take("q1", (P, 4, T))
        q1s = A2.take("q1s", (P, 4, T), F32R)
        p_first = Arena(nc, attn0_at, stage).take("p_first", (P, 1024))
        A = Arena(nc, attn0_at + B * H * DH * 4, wo0_at)
        rt = A.take("rt", (P, 5, B, E0))
        rtm = A.take("rtm", (P, 2, B))
        wq1 = A.take("wq1_sb", (P, 4, P))
        wkvo1 = A.take("wkvo1_sb", (P, 3, D))
        mask_sb = Arena(nc, wo0_at, stage).take("mask_sb", (P, B * NBLK, S), U8)

        ps = ctx.enter_context(nc.psum_tensor("ps", [P, 8, 512], F32))

        load = {n: sem("ld_" + n) for n in (
            "x", "wqk0", "wqk1", "ctxT0", "ctxT1", "ctx0", "ctx1", "vo0", "small", "mla",
            "w1", "w2", "ctxT2", "mask", "l1w", "kstack", "exp1", "sa")}
        xn_ready, xnT_psum, xnT_ready = sem("xn_ready"), sem("xnT_psum"), sem("xnT_ready")
        chain = sem("dve_chain")
        q0_psum, q0_sb = sem("q0_psum"), sem("q0_sb")
        qk_psum, qk_hi_done, qk_lo_done = sem("qk_psum"), sem("qk_hi_done"), sem("qk_lo_done")
        splitT_hi, splitT_lo = sem("splitT_hi"), sem("splitT_lo")
        split_hi, split_lo = sem("split_hi"), sem("split_lo")
        scored, maxed, exped = sem("scored"), sem("maxed"), sem("exped")
        turned, hi_done, lo_done, pv_done = sem("turned"), sem("hi_done"), sem("lo_done"), sem("pv_done")
        u_copied, o_psum, o_copied = sem("u_copied"), sem("o_psum"), sem("o_copied")
        a0_turned, a0T_act, a0T_dve, proj0 = sem("a0_turned"), sem("a0T_act"), sem("a0T_dve"), sem("proj0")
        xb_done = sem("xb_done")
        lat_psum, lat_copied = sem("lat_psum"), sem("lat_copied")
        k_psum, vm_psum, q_psum, qsw_psum = sem("k_psum"), sem("vm_psum"), sem("q_psum"), sem("qsw_psum")
        kc_read, kr_done, q_terms, qbd_m_dve, qbd_m_pool = (
            sem("kc_read"), sem("kr_done"), sem("q_terms"), sem("qbd_m_dve"), sem("qbd_m_pool"))
        vm_done, zeroed = sem("vm_done"), sem("zeroed")
        ms_psum, ms_clip, ms_exp, ms_masked = sem("ms_psum"), sem("ms_clip"), sem("ms_exp"), sem("ms_masked")
        mo_psum, mo_T, mo_turned, mo_norm, mo_turned2, mo_T2, mo_proj = (
            sem("mo_psum"), sem("mo_T"), sem("mo_turned"), sem("mo_norm"), sem("mo_turned2"), sem("mo_T2"),
            sem("mo_proj"))
        rt_psum, rt_z, rt_e, diag_done = sem("rt_psum"), sem("rt_z"), sem("rt_e"), sem("diag_done")
        xm_psum, xm_act, xm_dve = sem("xm_psum"), sem("xm_act"), sem("xm_dve")
        h0_psum, g0_done, y0_psum = sem("h0_psum"), sem("g0_done"), sem("y0_psum")
        kv_psum, kv_act, k1_split = sem("kv_psum"), sem("kv_act"), sem("k1_split")
        q1s_done, qbd_pool = sem("q1s_done"), sem("qbd_pool")
        cap_big, cap_done = sem("cap_big"), sem("cap_done")
        q1_psum, q1_done, qbd_done = sem("q1_psum"), sem("q1_done"), sem("qbd_done")
        s1_psum, w1_done, sq_done, pv1_done = sem("s1_psum"), sem("w1_done"), sem("sq_done"), sem("pv1_done")
        keep_done, relu_done, kept, sq_pool = sem("keep_done"), sem("relu_done"), sem("kept"), sem("sq_pool")
        warm, acc_zero, o1_copied = sem("warm"), sem("acc_zero"), sem("o1_copied")
        o1_turned, o1_norm, o1_turned2, o1_T, o1_proj = (sem("o1_turned"), sem("o1_norm"), sem("o1_turned2"),
                                                         sem("o1_T"), sem("o1_proj"))
        sa_psum, sa_qk, sa_v, sa_score, sa_max, sa_exp, sa_turned, sa_T, sa_out = (
            sem("sa_psum"), sem("sa_qk"), sem("sa_v"), sem("sa_score"), sem("sa_max"), sem("sa_exp"),
            sem("sa_turned"), sem("sa_T"), sem("sa_out"))
        gt_psum, gt_z, gt_e = sem("gt_psum"), sem("gt_z"), sem("gt_e")
        gu_psum, silu_done, h1_done, y1_psum = sem("gu_psum"), sem("silu_done"), sem("h1_done"), sem("y1_psum")
        y1_added, stored = sem("y1_added"), sem("stored")

        def qk_pair(t, n):
            return t[:, 2 * n:2 * n + 2, :, :].rearrange("p h b s -> p (h b s)")

        def ctx_chunk(i):
            part, c = i // 4, i % 4
            b, nat = part // 2, part % 2
            cols = slice(c * 512, (c + 1) * 512)
            raw = (ctxT_raw0, ctx_raw0)[nat][:, cols] if b == 0 else ctx_raw1[:, nat, cols]
            if nat:
                rows = slice(b * NBLK + 4 * c, b * NBLK + 4 * c + 4)
                hi_t, lo_t = (t[:, rows, :].rearrange("p k d -> p (k d)") for t in (ctx_hi, ctx_lo))
            else:
                hi_t, lo_t = (t[:, b * CTX + c * 512:b * CTX + (c + 1) * 512] for t in (ctxT_hi, ctxT_lo))
            return hi_t, lo_t, raw, load[("ctxT0", "ctx0", "ctxT1", "ctx1")[part]]

        def place_q(engine, j):
            rows = slice(HR * j, HR * j + HR)
            view = "p g (b s) -> p b g s"
            return engine.tensor_tensor(qbd_m[rows, :, :, j, :], qr[rows, :, :].rearrange(view, b=B),
                                        ropet[rows, :, :].rearrange(view, b=B), ALU.add)

        def spread_q(engine, c):
            b, g = c // 4, c % 4
            return engine.tensor_tensor(qbd[:, b, g, :, :], bc(q1s[:, g, b * S:(b + 1) * S], 1, 4),
                                        bc(headsel[:], 2, S), ALU.mult)

        NHS = B * H
        NB0 = NQ * NBLK
        UNITS = NBLK // 2
        COMBOS = B * 4
        NU = COMBOS * UNITS
        NKV = B * CTX // 512
        EP = (E1 + 2) // 2

        def c_of(m):
            return m // UNITS

        def is_first(m):
            return m % UNITS == 0

        def nth(m):
            return m - m // UNITS

        block = ctx.enter_context(nc.Block())

        @block.sync
        def _(sp):
            def get(dst, name, s, src=None):
                sp.dma_start(dst, ins[name] if src is None else src).then_inc(load[s], 16)

            get(x[:], "x_tok", "x")
            get(ident[:], "ident", "x")
            get(wq0[:, 0:2 * P], "wq0", "wqk0", ins["wq0"][:, 0:2 * P])
            get(wk0_t[:, 0:QUAD, :], "wk0_t", "wqk0", ins["wk0_t"][:, 0:QUAD, :])
            get(ctxT_raw0[:], "ctx_t", "ctxT0", ins["ctx_t"][:, 0:CTX])
            get(wq0[:, 2 * P:], "wq0", "wqk1", ins["wq0"][:, 2 * P:])
            get(wk0_t[:, QUAD:, :], "wk0_t", "wqk1", ins["wk0_t"][:, QUAD:, :])
            get(ctx_raw0[:], "ctx_nat", "ctx0", ins["ctx_nat"][:, 0:NBLK, :].rearrange("p k d -> p (k d)"))
            get(ctx_raw1[:, 0, :], "ctx_t", "ctxT1", ins["ctx_t"][:, CTX:])
            get(ctx_raw1[:, 1, :], "ctx_nat", "ctx1", ins["ctx_nat"][:, NBLK:, :].rearrange("p k d -> p (k d)"))
            get(wv0[:], "wv0", "vo0")
            get(wo0[:], "wo0", "vo0")
            small = [(bias_rows[:, 0:D], "bo0"), (bias_rows[:, D:2 * D], "bv_sa"), (w_lat[:], "w_lat"),
                     (wuv[:], "wuv"), (wo_mla[:], "wo_mla"), (rope[:], "rope"), (wr_sb[:], "wr"),
                     (br_sb[:], "br"), (rank_sb[:], "rank"), (headsel[:], "headsel"), (nbias[:], "nbias")]
            assert len(small) == N_SMALL
            for dst, name in small:
                get(dst, name, "small")
            sp.wait_ge(scored, 2 * NHS)
            get(ctxT_raw2[:], "ctx_t", "ctxT2")
            get(w1[:], "w1", "w1")
            get(w2[:], "w2", "w2")
            sp.wait_ge(turned, NB0)
            get(wq_mla[:], "wq_mla", "mla")
            sp.wait_ge(o_psum, NQ)
            get(wkvo1[:], "wkvo1", "l1w")
            get(wq1[:], "wq1", "l1w")
            sp.wait_ge(a0_turned, 1)
            get(wk_mla[:], "wk_mla", "mla")
            sp.wait_ge(proj0, 1)
            get(mask_sb[:], "mask_t", "mask")
            sp.wait_ge(mo_proj, 1)
            sp.wait_ge(kv_act, 2 * NKV)
            sp.wait_ge(k1_split, NKV)
            for t in range(4):
                part = k1_lo if t % 2 else k1_hi
                for g in range(4):
                    sp.dma_start(kstack[32 * t:32 * t + 32, g, :].bitcast(F32),
                                 part[32 * g:32 * g + 32, :].bitcast(F32)).then_inc(load["kstack"], 16)
            sp.wait_ge(y0_psum, 2 * B)
            get(wg[:], "wg", "exp1")
            get(wu[:], "wu", "exp1")
            get(wd[:], "wd", "exp1")
            sp.wait_ge(s1_psum, NU)
            get(wqkv[:], "wqkv_sa", "sa")
            get(bqk[:], "bqk_sa", "sa")
            get(gate_w[:], "gate_w", "sa")
            get(gate_b[:], "gate_b", "sa")
            get(below[:], "below", "sa")
            sp.wait_ge(y1_added, E1 + 1)
            sp.dma_start(out.rearrange("b s d -> s b d"), x[:]).then_inc(stored, 16)
            sp.wait_ge(stored, 16)

        @block.tensor
        def _(pe):
            mm = nc.tensor.matmul

            def turn_xn(layer):
                pe.wait_ge(xn_ready, layer + 1)
                for b in range(B):
                    last = nc.tensor.transpose(ps[:, 5, b * S:(b + 1) * S], xn[:, b, :], ident[:])
                last.then_inc(xnT_psum, 1)
                pe.wait_ge(xnT_ready, layer + 1)

            pe.wait_ge(warm, 1)
            for _ in range(WARM):
                mm(ps[:, 0, 0:T], zeros[:, 0:P], zeros[:], start=True, stop=True)
            pe.wait_ge(load["x"], 32)
            turn_xn(0)

            def make_qk(i):
                pe.wait_ge(load[f"wqk{min(i, 1)}"], 32)
                for t in range(2):
                    last = mm(ps[:, 4, t * T:(t + 1) * T], wq0[:, (2 * i + t) * P:(2 * i + t + 1) * P], xnT[:],
                              start=True, stop=True)
                last.then_inc(q0_psum, 1)
                pe.wait_ge(q0_sb, i + 1)
                if i:
                    pe.wait_ge(qk_lo_done, 2 * i)
                for j in range(QUAD):
                    last = mm(ps[:, 6 + j // 2, (j % 2) * T:(j % 2 + 1) * T], wk0_t[:, 4 * i + j, :],
                              q0T[:, i % 2, j // 2, :], start=True, stop=True)
                    if j % 2:
                        last.then_inc(qk_psum, 1)

            def scores(hs, c):
                b, h = hs // H, hs % H
                if hs >= 1:
                    pe.wait_ge(exped, 2 * (hs - 1) + c // 2 + 1)
                if hs == 0:
                    pe.wait_ge(splitT_lo, c + 1)
                if hs == H:
                    pe.wait_ge(split_lo, 4 + c + 1)
                cols = slice(b * CTX + c * 512, b * CTX + (c + 1) * 512)
                mm(ps[:, c, :], qk_hi[:, h, b, :], ctxT_hi[:, cols], start=True, stop=False)
                mm(ps[:, c, :], qk_lo[:, h, b, :], ctxT_hi[:, cols], start=False, stop=False)
                last = mm(ps[:, c, :], qk_hi[:, h, b, :], ctxT_lo[:, cols], start=False, stop=True)
                if c % 2:
                    last.then_inc(scored, 1)

            def turn_probs(n):
                q, k = n // NBLK, n % NBLK
                if k == 0:
                    pe.wait_ge(exped, 2 * QUAD * (q + 1))
                if n >= 2:
                    pe.wait_ge(lo_done, n - 1)
                for j in range(QUAD):
                    last = nc.tensor.transpose(ps[:, 4 + n % 2, j * S:(j + 1) * S],
                                               probs[:, q % 2, j, k * P:(k + 1) * P], ident[:])
                last.then_inc(turned, 1)

            def weigh_ctx(n):
                q, k = n // NBLK, n % NBLK
                row = (q // QUAD) * NBLK + k
                if k == 0 and q >= 2:
                    pe.wait_ge(o_copied, q - 1)
                if q % QUAD == 0 and k % 4 == 0:
                    pe.wait_ge(split_lo, (0, 8)[q // QUAD] + k // 4 + 1)
                pe.wait_ge(lo_done, n + 1)
                acc = ps[:, 6 + q % 2, :]
                mm(acc, ctx_hi[:, row, :], pT_hi[:, n % 3, :], start=(k == 0), stop=False)
                mm(acc, ctx_hi[:, row, :], pT_lo[:, n % 3, :], start=False, stop=False)
                mm(acc, ctx_lo[:, row, :], pT_hi[:, n % 3, :], start=False,
                   stop=(k == NBLK - 1)).then_inc(pv_done, 1)

            def project_v(q):
                pe.wait_ge(u_copied, q + 1)
                if q == 0:
                    pe.wait_ge(load["vo0"], 32)
                for j in range(QUAD):
                    h = (q % QUAD) * QUAD + j // 2 * 2
                    last = mm(ps[:, 6 + q % 2, j * P:(j + 1) * P], u_sb[:, j * S:(j + 1) * S],
                              wv0[:, h * DH:(h + 2) * DH], start=True, stop=True)
                last.then_inc(o_psum, 1)

            make_qk(0)
            for step in range(NHS + QUAD):
                n0 = (step - QUAD) * QUAD
                if step < H and step % 2 == 0:
                    pe.wait_ge(qk_lo_done, step // 2 + 1)
                for slot in range(4):
                    if step < NHS and slot < 2:
                        scores(step, 2 * slot)
                        scores(step, 2 * slot + 1)
                    if n0 >= 0:
                        n = n0 + slot
                        if n >= 2:
                            weigh_ctx(n - 2)
                        if n >= 2 + NBLK and (n - 2) % NBLK == 2:
                            project_v((n - 2) // NBLK - 1)
                        turn_probs(n)
                if step < 3:
                    make_qk(step + 1)
            weigh_ctx(NB0 - 2)
            weigh_ctx(NB0 - 1)
            project_v(NQ - 1)
            pe.wait_ge(o_copied, NQ)
            for b in range(B):
                for t in range(H // 2):
                    last = nc.tensor.transpose(ps[:, 2 * b + t // 4, (t % 4) * S:(t % 4 + 1) * S],
                                               attn0[:, b, t * P:(t + 1) * P], ident[:])
            last.then_inc(a0_turned, 1)
            for b in range(B):
                pe.wait_ge((a0T_act, a0T_dve)[b], 1)
                for t in range(H // 2):
                    last = mm(ps[:, 4, b * D:(b + 1) * D], attn0T[:, b, t, :], wo0[:, t, :],
                              start=(t == 0), stop=(t == H // 2 - 1))
            last.then_inc(proj0, 1)

            made = [0]

            def fill(count):
                for n in range(made[0], made[0] + count):
                    if n == 0:
                        pe.wait_ge(load["ctxT2"], 16)
                        pe.wait_ge(load["l1w"], 32)
                    if n >= 2:
                        pe.wait_ge(kv_act, n - 1)
                    i = n % NKV
                    if n < NKV:
                        last = mm(ps[:, 6 + n % 2, :], wkvo1[:, 0, :], ctxT_raw2[:, i * 512:(i + 1) * 512],
                                  start=True, stop=True)
                    else:
                        for r in range(4):
                            at = (4 * i + r) * P
                            last = mm(ps[:, 6 + n % 2, r * P:(r + 1) * P], ctxT_raw2[:, at:at + P],
                                      wkvo1[:, 1, :], start=True, stop=True)
                    last.then_inc(kv_psum, 1)
                made[0] += count

            fill(FILLS[0])
            turn_xn(1)
            pe.wait_ge(load["small"], 16 * N_SMALL)
            mm(ps[:, 5, T:2 * T], w_lat[:], xnT[:], start=True, stop=True).then_inc(lat_psum, 1)
            pe.wait_ge(lat_copied, 1)
            pe.wait_ge(load["mla"], 32)
            mm(ps[:, 4, 0:T], wk_mla[:, 4, :], lat_sb[:], start=True, stop=True)
            for g in range(4):
                last = mm(ps[:, g // 2, (g % 2) * T:(g % 2 + 1) * T], wk_mla[:, g, :], lat_sb[:],
                          start=True, stop=True)
            last.then_inc(k_psum, 1)
            for g in range(4):
                last = mm(ps[:, 2 + g // 2, (g % 2) * T:(g % 2 + 1) * T], wq_mla[:, 0, g, :], lat_sb[:],
                          start=True, stop=True)
            last.then_inc(q_psum, 1)
            for b in range(B):
                last = mm(ps[:, 5, b * D:(b + 1) * D], lat_sb[:, b * S:(b + 1) * S], wuv[:],
                          start=True, stop=True)
            last.then_inc(vm_psum, 1)
            pe.wait_ge(kc_read, 1)
            for g in range(4):
                last = mm(ps[:, g // 2, (g % 2) * T:(g % 2 + 1) * T], wq_mla[:, 1, g, :], lat_sb[:],
                          start=True, stop=True)
            last.then_inc(qsw_psum, 1)
            fill(FILLS[1])
            pe.wait_ge(kr_done, 1)
            pe.wait_ge(qbd_m_dve, 1)
            pe.wait_ge(qbd_m_pool, 1)
            for b in range(B):
                for g in range(4):
                    if b and g % 2 == 0:
                        pe.wait_ge(ms_clip, g // 2 + 1)
                    last = mm(ps[:, g, :], kr[:, g, b * S:(b + 1) * S],
                              qbd_m[:, b, g, :, :].rearrange("p j s -> p (j s)"), start=True, stop=True)
                    if g % 2:
                        last.then_inc(ms_psum, 1)
            pe.wait_ge(vm_done, 1)
            for b in range(B):
                for g in range(4):
                    if g % 2 == 0:
                        pe.wait_ge(ms_masked, 2 * b + g // 2 + 1)
                    for j in range(4):
                        last = mm(ps[HR * j:HR * j + HR, 4 + b, g * S:(g + 1) * S], vx[:, b, 4 * g + j, :],
                                  pm[:, b, g, j, :], start=True, stop=True)
                last.then_inc(mo_psum, 1)
            for b in range(B):
                pe.wait_ge(mo_T, b + 1)
                if b == 0:
                    pe.wait_ge(ms_clip, 2 * B)
                for g in range(4):
                    last = nc.tensor.transpose(ps[:, b, g * P:(g + 1) * P], oTm[:, b, g, :], ident[:])
                last.then_inc(mo_turned, 1)
            for b in range(B):
                pe.wait_ge(mo_norm, b + 1)
                last = nc.tensor.transpose(ps[:, 2, b * S:(b + 1) * S],
                                           attn_m[:, b, :, :].rearrange("p h d -> p (h d)"), ident[:])
            last.then_inc(mo_turned2, 1)
            pe.wait_ge(mo_T2, 1)
            for b in range(B):
                last = mm(ps[:, 3, b * D:(b + 1) * D], attn_mT[:, b * S:(b + 1) * S], wo_mla[:],
                          start=True, stop=True)
            last.then_inc(mo_proj, 1)

            fill(FILLS[2])
            turn_xn(2)
            for b in range(B):
                last = mm(ps[:, 4, b * E0:(b + 1) * E0], xnT[:, b * S:(b + 1) * S], wr_sb[:],
                          start=True, stop=True)
            last.then_inc(rt_psum, 1)
            fill(FILLS[3])
            assert made[0] == 2 * NKV
            pe.wait_ge(diag_done, 1)
            for b in range(B):
                for eh in range(2):
                    mm(ps[:, 2 * b + eh, :], xn[:, b, :],
                       diag[:, b, 4 * eh:4 * eh + 4, :].rearrange("p e s -> p (e s)"),
                       start=True, stop=True).then_inc(xm_psum, 1)
            pe.wait_ge(load["w1"], 16)
            pe.wait_ge(xm_act, 2)
            pe.wait_ge(xm_dve, 2)
            pe.wait_ge(kv_act, 2 * NKV)
            for f in range(NF):
                for e in range(E0):
                    last = mm(ps[:, 6 + f // 2, (f % 2) * T:(f % 2 + 1) * T], w1[:, e, f * P:(f + 1) * P],
                              xm[:, :, e, :], start=(e == 0), stop=(e == E0 - 1))
                last.then_inc(h0_psum, 1)
            pe.wait_ge(load["w2"], 16)
            pe.wait_ge(g0_done, NF)
            for b in range(B):
                for eh in range(2):
                    for f in range(NF):
                        last = mm(ps[:, 2 * b + eh, :], g0[:, f, b * S:(b + 1) * S],
                                  w2[:, f, 4 * eh:4 * eh + 4, :].rearrange("p e d -> p (e d)"),
                                  start=(f == 0), stop=(f == NF - 1))
                    last.then_inc(y0_psum, 1)

            turn_xn(3)
            for g in range(4):
                last = mm(ps[:, g // 2, (g % 2) * T:(g % 2 + 1) * T], wq1[:, g, :], xnT[:], start=True, stop=True)
            last.then_inc(q1_psum, 1)
            pe.wait_ge(load["kstack"], 16 * 16)

            def scores1(m):
                c, u = m // UNITS, m % UNITS
                b, g = c // 4, c % 4
                if m >= 3:
                    if is_first(m - 3):
                        pe.wait_ge(relu_done, c_of(m - 3) + 1)
                    else:
                        pe.wait_ge(w1_done, nth(m - 3))
                if m == 0:
                    pe.wait_ge(qbd_done, 1)
                elif u == 0:
                    pe.wait_ge(qbd_pool, c)
                for i in range(2):
                    at = b * CTX + (2 * u + i) * P
                    for a in range(2):
                        dst = ps[:, 2 * (m % 3) + a, :].rearrange("p (h i s) -> p h i s", h=2, i=2)[:, :, i, :]
                        last = mm(dst, kstack[:, g, at:at + P], qbd[:, b, g, 2 * a:2 * a + 2, :],
                                  start=True, stop=True)
                last.then_inc(s1_psum, 1)

            def weigh_v(n):
                c, u = n // UNITS, (n + 1) % UNITS
                b, g = c // 4, c % 4
                if u == 1 and c >= 2:
                    pe.wait_ge(o1_copied, c - 1)
                if u == 0:
                    pe.wait_ge(sq_pool, c + 1)
                    p = p_first[:]
                else:
                    at = nth(c * UNITS + u)
                    pe.wait_ge(sq_done, at)
                    p = p_ring[:, (at - 1) % 3, :]
                for i in range(2):
                    k = 2 * u + i
                    for j in range(4):
                        last = mm(ps[HR * j:HR * j + DA + 1, 6 + c % 2, 0:S], v1[:, b * NBLK + k, 4 * g + j, :],
                                  p[:, (2 * j + i) * S:(2 * j + i + 1) * S],
                                  start=(k == 2), stop=(k == 1))
                last.then_inc(pv1_done, 1)

            pe.wait_ge(acc_zero, 1)
            pe.wait_ge(zeroed, 4)
            for m in range(NU + 3):
                if m < NU:
                    scores1(m)
                if m >= 3:
                    weigh_v(m - 3)
            for c in range(COMBOS):
                if c % 4 == 0:
                    pe.wait_ge(o1_copied, c + 4)
                last = nc.tensor.transpose(ps[:, c // 4, (c % 4) * P:(c % 4 + 1) * P], oT1[:, c, :], ident[:])
            last.then_inc(o1_turned, 1)
            pe.wait_ge(o1_norm, 1)
            for b in range(B):
                last = nc.tensor.transpose(ps[:, 2, b * S:(b + 1) * S],
                                           attn1[:, b, :, :].rearrange("p h d -> p (h d)"), ident[:])
            last.then_inc(o1_turned2, 1)
            pe.wait_ge(o1_T, 1)
            for b in range(B):
                last = mm(ps[:, 3, b * D:(b + 1) * D], attn1T[:, b * S:(b + 1) * S], wkvo1[:, 2, :],
                          start=True, stop=True)
            last.then_inc(o1_proj, 1)

            turn_xn(4)
            pe.wait_ge(load["sa"], 16 * 5)
            for i in range(2):
                mm(ps[:, 0, i * T:(i + 1) * T], wqkv[:, i, :], xnT[:], start=True, stop=True)
            for b in range(B):
                last = mm(ps[:, 1, b * D:(b + 1) * D], xnT[:, b * S:(b + 1) * S], wqkv[:, 2, :],
                          start=True, stop=True)
            last.then_inc(sa_psum, 1)
            pe.wait_ge(sa_qk, 2)
            for b in range(B):
                last = mm(ps[:, 2, b * S:(b + 1) * S], qk_sa[:, 0, b * S:(b + 1) * S],
                          qk_sa[:, 1, b * S:(b + 1) * S], start=True, stop=True)
            last.then_inc(sa_score, 1)
            pe.wait_ge(sa_exp, B)
            for b in range(B):
                last = nc.tensor.transpose(ps[:, 3, b * S:(b + 1) * S], p_sa[:, b, :], ident[:])
            last.then_inc(sa_turned, 1)
            pe.wait_ge(sa_T, 1)
            pe.wait_ge(sa_v, 1)
            for b in range(B):
                last = mm(ps[:, 4, b * D:(b + 1) * D], pT_sa[:, b * S:(b + 1) * S], v_sa[:, b, :],
                          start=True, stop=True)
            last.then_inc(sa_out, 1)

            turn_xn(5)
            for b in range(B):
                last = mm(ps[:, 6, b * E1:(b + 1) * E1], xnT[:, b * S:(b + 1) * S], gate_w[:],
                          start=True, stop=True)
            last.then_inc(gt_psum, 1)
            pe.wait_ge(load["exp1"], 48)
            for i in range(EP):
                if i >= 2:
                    pe.wait_ge(h1_done, i - 1)
                for w, weights in enumerate((wg, wu)):
                    for r in range(2):
                        e = 2 * i + r
                        if e <= E1:
                            last = mm(ps[:, 2 * (i % 2) + w, r * T:(r + 1) * T], weights[:, e, :], xnT[:],
                                      start=True, stop=True)
                last.then_inc(gu_psum, 1)
            for i in range(E1 + 1):
                e = (i + E1) % (E1 + 1)
                if i >= 3:
                    pe.wait_ge(y1_added, i - 2)
                if i == 0:
                    pe.wait_ge(h1_done, EP)
                for b in range(B):
                    last = mm(ps[:, (4, 5, 7)[i % 3], b * D:(b + 1) * D], hT1[:, e, b * S:(b + 1) * S],
                              wd[:, e, :], start=True, stop=True)
                last.then_inc(y1_psum, 1)

        @block.scalar
        def _(act):
            def copy(dst, src):
                return nc.scalar.activation(dst, src, ACT.Copy)

            def copy_xnT(layer):
                act.wait_ge(xnT_psum, layer + 1)
                copy(xnT[:], ps[:, 5, 0:T]).then_inc(xnT_ready, 1)


            def split(i):
                hi_t, _, raw, loaded = ctx_chunk(i)
                act.wait_ge(loaded, 16)
                copy(hi_t, raw).then_inc(splitT_hi, 1)

            def copy_q(i):
                act.wait_ge(q0_psum, i + 1)
                copy(q0T[:, i % 2, :, :].rearrange("p a t -> p (a t)"), ps[:, 4, :]).then_inc(q0_sb, 1)

            def make_qk(i):
                for n in range(2 * i, 2 * i + 2):
                    act.wait_ge(qk_psum, n + 1)
                    copy(qk_pair(qk_hi, n), ps[:, 6 + n % 2, :]).then_inc(qk_hi_done, 1)

            copy_xnT(0)
            split(0)
            copy_q(0)
            split(1)
            make_qk(0)
            split(2)
            split(3)

            def hi(n):
                act.wait_ge(turned, n + 1)
                if n >= 3:
                    act.wait_ge(pv_done, n - 2)
                copy(pT_hi[:, n % 3, :], ps[:, 4 + n % 2, :]).then_inc(hi_done, 1)

            def exp_half(hs, p):
                q, j = hs // QUAD, hs % QUAD
                act.wait_ge(maxed, hs + 1)
                if hs == QUAD and p == 0:
                    act.wait_ge(split_lo, 12)
                if q >= 2 and j == 0 and p == 0:
                    act.wait_ge(turned, NBLK * (q - 1))
                nc.scalar.activation(
                    probs[:, q % 2, j, p * 1024:(p + 1) * 1024].rearrange("p (a n) -> p a n", a=2),
                    ps[:, 2 * p:2 * p + 2, :], ACT.Exp, bias=nmax[:, hs % 2:hs % 2 + 1], scale=SCALE0,
                    accum_out=rowsum[:, hs, p:p + 1]).then_inc(exped, 1)

            def copy_u(q):
                act.wait_ge(pv_done, NBLK * (q + 1))
                if q >= 1:
                    act.wait_ge(o_psum, q)
                copy(u_sb[:], ps[:, 6 + q % 2, :]).then_inc(u_copied, 1)

            for step in range(NHS + QUAD):
                n0 = (step - QUAD) * QUAD
                if n0 >= 1:
                    hi(n0 - 1)
                if n0 >= 0:
                    hi(n0)
                    if n0 >= NBLK and n0 % NBLK == 0:
                        copy_u(n0 // NBLK - 1)
                    hi(n0 + 1)
                if step < 3:
                    copy_q(step + 1)
                if step < NHS:
                    exp_half(step, 0)
                if n0 >= 0:
                    hi(n0 + 2)
                if step < NHS:
                    exp_half(step, 1)
                if step < 3:
                    make_qk(step + 1)
            hi(NB0 - 1)
            copy_u(NQ - 1)
            act.wait_ge(a0_turned, 1)
            copy(attn0T[:, 0, :, :].rearrange("p (a t) s -> p a (t s)", a=2), ps[:, 0:2, :]).then_inc(a0T_act, 1)

            made = [0]

            def fill(count):
                for n in range(made[0], made[0] + count):
                    act.wait_ge(kv_psum, n + 1)
                    bank, i = ps[:, 6 + n % 2, :], n % NKV
                    if n < NKV:
                        cols = slice(i * 512, (i + 1) * 512)
                        copy(k1_raw[:, cols], bank)
                        copy(k1_hi[:, cols], bank).then_inc(kv_act, 1)
                    else:
                        if i == 0:
                            act.wait_ge(zeroed, 4)
                        copy(v1[:, 4 * i:4 * i + 4, :, 0:DA],
                             bank.rearrange("p (k h d) -> p k h d", k=4, h=H)).then_inc(kv_act, 1)
                made[0] += count

            fill(FILLS[0])
            copy_xnT(1)
            act.wait_ge(lat_psum, 1)
            copy(lat_sb[:], ps[:, 5, T:2 * T]).then_inc(lat_copied, 1)
            act.wait_ge(vm_psum, 1)
            act.wait_ge(zeroed, 2)
            copy(vx[:, :, :, 0:DC], ps[:, 5, 0:T].rearrange("p (b h d) -> p b h d", b=B, h=H)).then_inc(vm_done, 1)
            fill(FILLS[1])
            for i in range(2 * B):
                act.wait_ge(ms_clip, i + 1)
                nc.scalar.activation(pm[:, i // 2, 2 * (i % 2):2 * (i % 2) + 2, :, :].rearrange("p g j s -> p (g j s)"),
                                     clipped[:, i % 2, :], ACT.Exp, scale=SCALE_MLA).then_inc(ms_exp, 1)
            for b in range(B):
                act.wait_ge(mo_psum, b + 1)
                copy(oTm[:, b, :, :].rearrange("p g s -> p (g s)"), ps[:, 4 + b, :]).then_inc(mo_T, 1)
            act.wait_ge(mo_turned2, 1)
            copy(attn_mT[:], ps[:, 2, 0:T]).then_inc(mo_T2, 1)

            fill(FILLS[2])
            copy_xnT(2)
            act.wait_ge(rt_z, 1)
            nc.scalar.activation(rt[:, 1, :, :], rt[:, 0, :, :], ACT.Exp, scale=-1.0).then_inc(rt_e, 1)
            fill(FILLS[3])
            for i in range(2):
                act.wait_ge(xm_psum, i + 1)
                copy(xm[:, 0, 4 * i:4 * i + 4, :].rearrange("p e s -> p (e s)"), ps[:, i, :]).then_inc(xm_act, 1)
            for f in range(NF):
                act.wait_ge(h0_psum, 2 * (f // 2) + 2)
                nc.scalar.activation(g0[:, f, :], ps[:, 6 + f // 2, (f % 2) * T:(f % 2 + 1) * T],
                                     ACT.Gelu).then_inc(g0_done, 1)

            copy_xnT(3)
            act.wait_ge(q1_psum, 1)
            nc.scalar.activation(q1[:].rearrange("p (a g) t -> p a (g t)", a=2), ps[:, 0:2, :], ACT.Copy,
                                 scale=SCALE1).then_inc(q1_done, 1)

            def copy_o1(c):
                act.wait_ge(pv1_done, UNITS * (c + 1))
                copy(oT1[:, c, :], ps[:, 6 + c % 2, 0:S]).then_inc(o1_copied, 1)

            def relu_first(c):
                m = c * UNITS
                act.wait_ge(s1_psum, m + 1)
                if c:
                    act.wait_ge(sq_pool, c)
                at = 2 * (m % 3)
                nc.scalar.activation(w_first[:].rearrange("p (a n) -> p a n", a=2), ps[:, at:at + 2, :], ACT.Relu,
                                     bias=nbias[:]).then_inc(relu_done, 1)

            def weighed_at(at):
                return (at - 1) // (UNITS - 1) * UNITS + (at - 1) % (UNITS - 1) + 1

            for m in range(NU):
                if m % UNITS == 3 and m >= UNITS:
                    copy_o1(c_of(m) - 1)
                if m == 0:
                    relu_first(0)
                elif m % UNITS == UNITS - 1 and c_of(m) + 1 < COMBOS:
                    relu_first(c_of(m) + 1)
                if is_first(m):
                    continue
                at = nth(m)
                act.wait_ge(w1_done, at)
                if at > 3:
                    act.wait_ge(pv1_done, weighed_at(at - 3))
                nc.scalar.activation(p_ring[:, (at - 1) % 3, :], w_ring[:, (at - 1) % 3, :], ACT.Square,
                                     bias=nbias[:]).then_inc(sq_done, 1)
            copy_o1(COMBOS - 1)
            act.wait_ge(o1_turned2, 1)
            copy(attn1T[:], ps[:, 2, 0:T]).then_inc(o1_T, 1)

            copy_xnT(4)
            act.wait_ge(sa_psum, 1)
            for i in range(2):
                nc.scalar.activation(qk_sa[:, i, :], ps[:, 0, i * T:(i + 1) * T], ACT.Identity,
                                     bias=bqk[:, i:i + 1]).then_inc(sa_qk, 1)
            act.wait_ge(sa_max, 1)
            for b in range(B):
                nc.scalar.activation(p_sa[:, b, :], ps[:, 2, b * S:(b + 1) * S], ACT.Exp,
                                     bias=mx_sa[:, 1, b:b + 1], scale=SCALE_SA,
                                     accum_out=mx_sa[:, 2, b:b + 1]).then_inc(sa_exp, 1)
            act.wait_ge(sa_turned, 1)
            copy(pT_sa[:], ps[:, 3, 0:T]).then_inc(sa_T, 1)

            copy_xnT(5)
            act.wait_ge(gt_z, 1)
            nc.scalar.activation(sc1[:, 1, :, :], sc1[:, 0, :, :], ACT.Exp, scale=-1.0).then_inc(gt_e, 1)
            for i in range(EP):
                n = T * (2 if 2 * i + 1 <= E1 else 1)
                act.wait_ge(gu_psum, i + 1)
                if i >= 2:
                    act.wait_ge(h1_done, i - 1)
                nc.scalar.activation(silu_g[:, i % 2, 0:n], ps[:, 2 * (i % 2), 0:n], ACT.Silu)\
                    .then_inc(silu_done, 1)

        @block.gpsimd
        def _(pool):
            nc.gpsimd.memset(zeros[:], 0.0).then_inc(warm, 1)
            for i in range(4, 16):
                hi_t, lo_t, raw, _ = ctx_chunk(i)
                pool.wait_ge(split_hi, i - 3)
                nc.gpsimd.tensor_tensor(lo_t, raw, hi_t, ALU.subtract).then_inc(split_lo, 1)
            pool.wait_ge(load["small"], 16 * N_SMALL)
            nc.gpsimd.tensor_tensor(xb[:], x[:], bc(bias_rows[:, 0:D], 1, B), ALU.add).then_inc(xb_done, 1)
            nc.gpsimd.tensor_scalar(neg_nbias[:], nbias[:], -1.0, None, ALU.mult).then_inc(zeroed, 1)
            pool.wait_ge(proj0, 1)
            nc.gpsimd.memset(vx[:, :, :, DC:DC + 1], 1.0)
            nc.gpsimd.memset(vx[:, :, :, DC + 1:HR], 0.0).then_inc(zeroed, 1)
            nc.gpsimd.memset(qbd_m[:], 0.0).then_inc(zeroed, 1)
            made = [0]

            def fill(count):
                for i in range(made[0], min(made[0] + count, NKV)):
                    cols = slice(i * 512, (i + 1) * 512)
                    pool.wait_ge(kv_act, i + 1)
                    nc.gpsimd.tensor_tensor(k1_lo[:, cols], k1_raw[:, cols], k1_hi[:, cols],
                                            ALU.subtract).then_inc(k1_split, 1)
                made[0] += count

            fill(FILLS[0])
            pool.wait_ge(q_terms, 1)
            pool.wait_ge(zeroed, 3)
            pool.wait_ge(k1_split, min(FILLS[0], NKV))
            place_q(nc.gpsimd, 3).then_inc(qbd_m_pool, 1)
            pool.wait_ge(qbd_m_pool, 1)
            fill(FILLS[1])
            for i in range(2 * B):
                pool.wait_ge(ms_exp, i + 1)
                part = pm[:, i // 2, 2 * (i % 2):2 * (i % 2) + 2, :, :].rearrange("p g j s -> p (g j) s")
                nc.gpsimd.affine_select(out=part, in_=part, compare_op=ALU.is_ge, fill=0.0, base=0,
                                        pattern=[[0, 8], [1, S]], channel_multiplier=-1).then_inc(ms_masked, 1)
            assert made[0] >= NKV
            pool.wait_ge(k1_split, NKV)
            nc.gpsimd.memset(v1[:, :, :, DA:DA + 1], 1.0).then_inc(zeroed, 1)
            pool.wait_ge(q1s_done, 1)
            pool.wait_ge(keep_done, 1)
            for c in range(COMBOS):
                if c + 1 < COMBOS:
                    spread_q(nc.gpsimd, c + 1).then_inc(qbd_pool, 1)
                pool.wait_ge(relu_done, c + 1)
                heads = w_first[:].rearrange("p (h n) -> p h n", h=4)
                nc.gpsimd.tensor_tensor(heads, heads, bc(keep[:, c // 4, :], 1, 4), ALU.mult).then_inc(kept, 1)
                pool.wait_ge(kept, c + 1)
                if c:
                    pool.wait_ge(pv1_done, UNITS * c)
                nc.gpsimd.tensor_tensor(p_first[:], w_first[:], w_first[:], ALU.mult).then_inc(sq_pool, 1)

        @block.vector
        def _(dve):
            v = nc.vector
            links = [0]

            def link(ins_):
                links[0] += 1
                ins_.then_inc(chain, 1)
                dve.wait_ge(chain, links[0])

            def layer_norm(layer):
                for b in range(B):
                    s = v.bn_stats(stats[:, b, :], x[:, b, :])
                link(s)
                for b in range(B):
                    s = v.bn_aggr(mv[:, b, :], stats[:, b, :])
                link(s)
                var, y, t = nwt[:, 0, :], nwt[:, 1, :], nwt[:, 2, :]
                link(v.tensor_scalar(var, mv[:, :, 1], EPS, None, ALU.add))
                link(v.tensor_scalar(seed[:, 0, :], var.bitcast(I32), 1, None, ALU.logical_shift_right))
                link(v.tensor_scalar(y.bitcast(I32), seed[:, 0, :], -1.0, float(RSQRT_SEED), ALU.mult, ALU.add))
                for _ in range(3):
                    link(v.tensor_tensor(t, y, y, ALU.mult))
                    link(v.scalar_tensor_tensor(t, t, -0.5, var, ALU.mult, ALU.mult))
                    link(v.scalar_tensor_tensor(y, t, 1.5, y, ALU.add, ALU.mult))
                for b in range(B):
                    s = v.tensor_scalar(xn[:, b, :], x[:, b, :], mv[:, b, 0:1], nwt[:, 1, b:b + 1],
                                        ALU.subtract, ALU.mult)
                s.then_inc(xn_ready, 1)

            dve.wait_ge(load["x"], 32)
            layer_norm(0)


            def qk_rest(n):
                dve.wait_ge(qk_hi_done, n + 1)
                v.tensor_tensor(qk_pair(qk_lo, n), ps[:, 6 + n % 2, :], qk_pair(qk_hi, n),
                                ALU.subtract).then_inc(qk_lo_done, 1)

            def split_rest(i):
                hi_t, lo_t, raw, _ = ctx_chunk(i)
                dve.wait_ge(splitT_hi, i + 1)
                v.tensor_tensor(lo_t, raw, hi_t, ALU.subtract).then_inc(splitT_lo, 1)

            def split(i):
                hi_t, _, raw, loaded = ctx_chunk(i)
                dve.wait_ge(loaded, 16)
                v.tensor_copy(hi_t, raw).then_inc(split_hi, 1)

            split_rest(0)
            qk_rest(0)
            split_rest(1)
            qk_rest(1)
            split_rest(2)
            split_rest(3)

            def lo(n):
                dve.wait_ge(hi_done, n + 1)
                v.tensor_tensor(pT_lo[:, n % 3, :], ps[:, 4 + n % 2, :], pT_hi[:, n % 3, :],
                                ALU.subtract).then_inc(lo_done, 1)

            def half_max(hs, p):
                dve.wait_ge(scored, 2 * hs + p + 1)
                return v.tensor_reduce(max2[:, p:p + 1], ps[:, 2 * p:2 * p + 2, :], AX.XY, ALU.max)

            def copy_o(q):
                hs = q * QUAD
                b, h = hs // H, hs % H
                r = rden[:, q % 2, :]
                dve.wait_ge(exped, 2 * QUAD * (q + 1))
                link(v.tensor_tensor(r, rowsum[:, hs:hs + QUAD, 0], rowsum[:, hs:hs + QUAD, 1], ALU.add))
                link(v.reciprocal(r, r))
                dve.wait_ge(o_psum, q + 1)
                for e in range(2):
                    s = v.tensor_tensor(
                        attn0[:, b, h * DH:(h + QUAD) * DH].rearrange("p (a f) -> p a f", a=2)[:, :, e * DH:(e + 1) * DH],
                        ps[:, 6 + q % 2, :].rearrange("p (a f) -> p a f", a=2)[:, :, e * (P + DH):e * (P + DH) + DH],
                        bc(r[:, e::2], 2, DH), ALU.mult)
                s.then_inc(o_copied, 1)

            for step in range(NHS + QUAD):
                n0 = (step - QUAD) * QUAD
                if n0 >= 1:
                    lo(n0 - 1)
                if step < NHS:
                    half_max(step, 0)
                if n0 >= 0:
                    lo(n0)
                if step < NHS:
                    link(half_max(step, 1))
                    v.tensor_scalar(nmax[:, step % 2:step % 2 + 1], max2[:, 0:1], max2[:, 1:2], -SCALE0,
                                    ALU.max, ALU.mult).then_inc(maxed, 1)
                if step < 3:
                    qk_rest(2 * step + 2)
                    qk_rest(2 * step + 3)
                if step < 3:
                    for i in range(4 * step + 4, 4 * step + 8):
                        split(i)
                if n0 >= 0:
                    lo(n0 + 1)
                    if n0 > NBLK and n0 % NBLK == QUAD:
                        copy_o(n0 // NBLK - 1)
                    lo(n0 + 2)
            lo(NB0 - 1)
            copy_o(NQ - 1)
            dve.wait_ge(a0_turned, 1)
            v.tensor_copy(attn0T[:, 1, :, :].rearrange("p (a t) s -> p a (t s)", a=2), ps[:, 2:4, :])\
                .then_inc(a0T_dve, 1)
            dve.wait_ge(proj0, 1)
            dve.wait_ge(xb_done, 1)
            link(v.tensor_tensor(x[:].rearrange("p b d -> p (b d)"), ps[:, 4, 0:T],
                                 xb[:].rearrange("p b d -> p (b d)"), ALU.add))

            layer_norm(1)
            cos, sin = rope[:, 0, :], rope[:, 1, :]
            rows_gb = "p g (b s) -> p (g b) s"

            def banks(a):
                return ps[:, a:a + 2, :].rearrange("p a (g s) -> p (a g) s", s=S)

            dve.wait_ge(k_psum, 1)
            v.tensor_tensor(ropek[:].rearrange("p (b s) -> p b s", b=B),
                            ps[:, 4, 0:T].rearrange("p (b s) -> p b s", b=B), bc(sin, 1, B), ALU.mult)
            v.tensor_tensor(kr[:].rearrange(rows_gb, b=B), banks(0), bc(cos, 1, 8), ALU.mult).then_inc(kc_read, 1)
            dve.wait_ge(kc_read, 1)
            v.tensor_tensor(kr[:], kr[:], bc(ropek[:], 1, 4), ALU.add).then_inc(kr_done, 1)
            dve.wait_ge(q_psum, 1)
            v.tensor_tensor(qr[:].rearrange(rows_gb, b=B), banks(2), bc(cos, 1, 8), ALU.mult)
            dve.wait_ge(qsw_psum, 1)
            v.tensor_tensor(ropet[:].rearrange(rows_gb, b=B), banks(0), bc(sin, 1, 8), ALU.mult)\
                .then_inc(q_terms, 1)
            dve.wait_ge(q_terms, 1)
            dve.wait_ge(zeroed, 3)
            for j in range(3):
                s = place_q(v, j)
            s.then_inc(qbd_m_dve, 1)
            for i in range(2 * B):
                dve.wait_ge(ms_psum, i + 1)
                if i >= 2:
                    dve.wait_ge(ms_exp, i - 1)
                at = 2 * (i % 2)
                v.tensor_scalar(clipped[:, i % 2, :].rearrange("p (a n) -> p a n", a=2), ps[:, at:at + 2, :],
                                CLIP, -CLIP, ALU.min, ALU.max).then_inc(ms_clip, 1)
            for b in range(B):
                dve.wait_ge(mo_turned, b + 1)
                heads = ps[:, b, :].rearrange("p (h d) -> p h d", d=HR)
                link(v.reciprocal(rl_m[:, b, :], heads[:, :, DC]))
                v.tensor_tensor(attn_m[:, b, :, :], heads[:, :, 0:DC], bc(rl_m[:, b, :], 2, DC), ALU.mult)\
                    .then_inc(mo_norm, 1)
            dve.wait_ge(mo_proj, 1)
            xf = x[:].rearrange("p b d -> p (b d)")
            link(v.tensor_tensor(xf, ps[:, 3, 0:T], xf, ALU.add))

            layer_norm(2)
            z, ez, r, eq, onehot = (rt[:, i, :, :] for i in range(5))
            dve.wait_ge(rt_psum, 1)
            v.tensor_tensor(z, ps[:, 4, 0:B * E0].rearrange("p (b e) -> p b e", b=B),
                            bc(br_sb[:], 1, B), ALU.add).then_inc(rt_z, 1)
            dve.wait_ge(rt_e, 1)
            link(v.tensor_scalar(ez, ez, 1.0, None, ALU.add))
            link(v.reciprocal(r, ez))
            link(v.tensor_reduce(rtm[:, 0, :], r, AX.X, ALU.max))
            link(v.tensor_tensor(eq, r, bc(rtm[:, 0, :], 2, E0), ALU.is_equal))
            link(v.tensor_tensor(eq, eq, bc(rank_sb[:], 1, B), ALU.mult))
            link(v.tensor_reduce(rtm[:, 1, :], eq, AX.X, ALU.max))
            link(v.tensor_tensor(onehot, eq, bc(rtm[:, 1, :], 2, E0), ALU.is_equal))
            for b in range(B):
                s = v.tensor_tensor(diag[:, b, :, :], bc(ident[:], 1, E0), bc(onehot[:, b, :], 2, S), ALU.mult)
            s.then_inc(diag_done, 1)
            link(v.tensor_tensor(eq, onehot, bc(rtm[:, 0, :], 2, E0), ALU.mult))
            dve.wait_ge(load["mask"], 16)
            dve.wait_ge(zeroed, 1)
            v.tensor_scalar(cap[:], mask_sb[:], 0.0, BIG, ALU.is_equal, ALU.mult).then_inc(cap_big, 1)
            for i in range(2):
                dve.wait_ge(xm_psum, 3 + i)
                v.tensor_copy(xm[:, 1, 4 * i:4 * i + 4, :].rearrange("p e s -> p (e s)"), ps[:, 2 + i, :])\
                    .then_inc(xm_dve, 1)
            dve.wait_ge(cap_big, 1)
            v.tensor_scalar(cap[:], cap[:], neg_nbias[:], None, ALU.add).then_inc(cap_done, 1)
            for b in range(B):
                dve.wait_ge(y0_psum, 2 * b + 2)
                link(v.tensor_tensor(yw[:], ps[:, 2 * b:2 * b + 2, :].rearrange("p a (e d) -> p (a e) d", d=D),
                                     bc(eq[:, b, :], 2, D), ALU.mult))
                link(v.tensor_reduce(xb[:, b, :], yw[:].rearrange("p e d -> p d e"), AX.X, ALU.add))
            link(v.tensor_tensor(x[:], x[:], xb[:], ALU.add))

            layer_norm(3)
            dve.wait_ge(q1_done, 1)
            link(v.tensor_copy(q1s[:], q1[:]))
            v.tensor_tensor(q1s[64:128], q1[64:128], q1s[64:128], ALU.subtract).then_inc(q1s_done, 1)
            dve.wait_ge(q1s_done, 1)
            spread_q(v, 0).then_inc(qbd_done, 1)
            v.memset(ps[:, 6:8, :], 0.0).then_inc(acc_zero, 1)
            dve.wait_ge(cap_done, 1)
            v.tensor_scalar(keep[:], cap[:].rearrange("p (b k) s -> p b (k s)", b=B)[:, :, 0:2 * S], neg_nbias[:],
                            None, ALU.is_gt).then_inc(keep_done, 1)
            dve.wait_ge(load["kstack"], 256)
            for m in range(NU):
                if is_first(m):
                    continue
                c, u, at = m // UNITS, m % UNITS, nth(m)
                dve.wait_ge(s1_psum, m + 1)
                if at > 3:
                    dve.wait_ge(sq_done, at - 3)
                k = (c // 4) * NBLK + 2 * u
                bank = 2 * (m % 3)
                v.scalar_tensor_tensor(
                    w_ring[:, (at - 1) % 3, :].rearrange("p (h n) -> p h n", h=4),
                    ps[:, bank:bank + 2, :].rearrange("p a (h n) -> p (a h) n", h=2), neg_nbias[:],
                    bc(cap[:, k:k + 2, :].rearrange("p i s -> p (i s)"), 1, 4), ALU.max, ALU.min)\
                    .then_inc(w1_done, 1)
            dve.wait_ge(o1_turned, 1)
            for b in range(B):
                o4 = ps[:, b, :].rearrange("p (h d) -> p h d", d=HR)
                r4 = rl1[:, 4 * b:4 * b + 4, :].rearrange("p g j -> p (g j)")
                link(v.tensor_scalar(r4, o4[:, :, DA], TINY, None, ALU.add))
                link(v.reciprocal(r4, r4))
                s = v.tensor_tensor(attn1[:, b, :, :], o4[:, :, 0:DA], bc(r4, 2, DA), ALU.mult)
            s.then_inc(o1_norm, 1)
            dve.wait_ge(o1_proj, 1)
            link(v.tensor_tensor(xf, ps[:, 3, 0:T], xf, ALU.add))

            layer_norm(4)
            dve.wait_ge(sa_psum, 1)
            v.tensor_tensor(v_sa[:], ps[:, 1, 0:T].rearrange("p (b d) -> p b d", b=B),
                            bc(bias_rows[:, D:2 * D], 1, B), ALU.add).then_inc(sa_v, 1)
            dve.wait_ge(sa_score, 1)
            link(v.tensor_reduce(mx_sa[:, 0, :], ps[:, 2, 0:T].rearrange("p (b s) -> p b s", b=B), AX.X, ALU.max))
            v.tensor_scalar(mx_sa[:, 1, :], mx_sa[:, 0, :], -SCALE_SA, None, ALU.mult).then_inc(sa_max, 1)
            dve.wait_ge(sa_exp, B)
            link(v.reciprocal(mx_sa[:, 3, :], mx_sa[:, 2, :]))
            dve.wait_ge(sa_out, 1)
            for b in range(B):
                s = v.scalar_tensor_tensor(x[:, b, :], ps[:, 4, b * D:(b + 1) * D], mx_sa[:, 3, b:b + 1],
                                           x[:, b, :], ALU.mult, ALU.add)
            link(s)

            layer_norm(5)
            z, ez, score, sel = (sc1[:, i, :, :] for i in range(4))
            dve.wait_ge(gt_psum, 1)
            v.tensor_copy(z, ps[:, 6, 0:B * E1].rearrange("p (b e) -> p b e", b=B)).then_inc(gt_z, 1)
            dve.wait_ge(gt_e, 1)
            link(v.tensor_scalar(ez, ez, 1.0, None, ALU.add))
            link(v.reciprocal(score, ez))
            link(v.tensor_tensor(sel, score, bc(gate_b[:], 1, B), ALU.add))
            for b in range(B):
                ge, gt = cmp1[:, 0, b, :, :], cmp1[:, 1, b, :, :]
                mine, other = bc(sel[:, b, :], 2, E1), bc(sel[:, b, :], 1, E1)
                v.tensor_tensor(gt, other, mine, ALU.is_gt)
                link(v.tensor_tensor(ge, other, mine, ALU.is_ge))
                link(v.tensor_tensor(ge, ge, below[:], ALU.mult))
                link(v.tensor_tensor(gt, gt, ge, ALU.max))
                link(v.tensor_reduce(comb[:, b, :], gt, AX.X, ALU.add))
            link(v.scalar_tensor_tensor(comb[:], comb[:], TOPK - 0.5, score, ALU.is_lt, ALU.mult))
            link(v.tensor_reduce(csum[:, 0, :], comb[:], AX.X, ALU.add))
            link(v.reciprocal(csum[:, 1, :], csum[:, 0, :]))
            for b in range(B):
                s = v.tensor_scalar(comb[:, b, :], comb[:, b, :], csum[:, 1, b:b + 1], ROUTE_SCALE,
                                    ALU.mult, ALU.mult)
            link(s)
            for i in range(EP):
                n = T * (2 if 2 * i + 1 <= E1 else 1)
                dve.wait_ge(silu_done, i + 1)
                v.tensor_tensor(hT1[:, 2 * i:2 * i + n // T, :].rearrange("p e t -> p (e t)"),
                                ps[:, 2 * (i % 2) + 1, 0:n], silu_g[:, i % 2, 0:n], ALU.mult).then_inc(h1_done, 1)
            for i in range(E1 + 1):
                dve.wait_ge(y1_psum, i + 1)
                for b in range(B):
                    y = ps[:, (4, 5, 7)[i % 3], b * D:(b + 1) * D]
                    if i == 0:
                        s = v.tensor_tensor(x[:, b, :], y, x[:, b, :], ALU.add)
                    else:
                        s = v.scalar_tensor_tensor(x[:, b, :], y, comb[:, b, i - 1:i], x[:, b, :],
                                                   ALU.mult, ALU.add)
                s.then_inc(y1_added, 1)
                dve.wait_ge(y1_added, i + 1)


N_SMALL = 11


def _rope_tables():
    inv = np.float32(10000.0) ** (-np.arange(0, DR, 2, dtype=np.float32) / np.float32(DR))
    ang = np.arange(S, dtype=np.float32)[:, None] * inv
    table = np.zeros((4, HR, 2, S), np.float32)
    table[:, :DC, 0] = 1.0
    for r in range(DR):
        table[:, DC + r, 0] = np.cos(ang[:, r // 2])
        table[:, DC + r, 1] = np.sin(ang[:, r // 2]) * (-1.0 if r % 2 == 0 else 1.0)
    return table.reshape(P, 2, S)


def _layout(a):
    ctx = a["ctx_1024"]
    swap = [1, 0, 3, 2]
    wk0_t = np.zeros((2, DH, H // 2, 2, D), np.float32)
    keys = a["L0_xattn_Wkv"][:, :H * DH].T.reshape(H // 2, 2, DH, D)
    for e in range(2):
        wk0_t[e, :, :, e] = keys[:, e].transpose(1, 0, 2)
    w_lat = np.zeros((D, P), np.float32)
    w_lat[:, 0:LAT], w_lat[:, LAT:2 * LAT] = a["L0_attn_W_DQ"], a["L0_attn_W_DKV"]
    w_lat[:, 2 * LAT:2 * LAT + DR] = a["L0_attn_W_KR"]
    w_lat[:, 2 * LAT + DR:2 * LAT + 2 * DR] = a["L0_attn_W_KR"][:, swap]
    uq = a["L0_attn_W_UQ"].reshape(LAT, 4, 4, DC)
    qr = a["L0_attn_W_QR"].reshape(LAT, 4, 4, DR)
    wq_mla = np.zeros((P, 2, 4, 4, HR), np.float32)
    wq_mla[:LAT, 0, :, :, :DC] = uq
    wq_mla[:LAT, 0, :, :, DC:DC + DR] = qr
    wq_mla[:LAT, 1, :, :, DC:DC + DR] = qr[..., swap]
    wk_mla = np.zeros((P, 5, 4, HR), np.float32)
    wk_mla[LAT:2 * LAT, :4, :, :DC] = a["L0_attn_W_UK"].reshape(LAT, 4, 4, DC)
    for r in range(DR):
        wk_mla[2 * LAT + r, :4, :, DC + r] = 1.0
        wk_mla[2 * LAT + DR + r, 4, :, DC + r] = 1.0
    wuv = np.zeros((P, D), np.float32)
    wuv[LAT:2 * LAT] = a["L0_attn_W_UV"]
    wq1 = a["L1_xattn_Wq"].T.reshape(D, 4, 1, 4 * DA)
    e = np.arange(E1)
    rows = lambda v, n: np.broadcast_to(v[None, :], (P, n))
    return {
        "x_tok": a["x"].transpose(1, 0, 2),
        "ctx_nat": ctx.reshape(B * NBLK, P, D).transpose(1, 0, 2),
        "ctx_t": ctx.reshape(B * CTX, D).T,
        "mask_t": a["mask_BxSxS2_bk0"].reshape(B, S, NBLK, P).transpose(3, 0, 2, 1).reshape(P, B * NBLK, S),
        "wq0": a["L0_xattn_Wq"],
        "wk0_t": wk0_t.reshape(P, H, D),
        "wv0": a["L0_xattn_Wkv"][:, H * DH:],
        "wo0": a["L0_xattn_Wo"].reshape(H // 2, P, D).transpose(1, 0, 2),
        "bo0": rows(a["L0_xattn_bo"], D),
        "w_lat": w_lat, "wq_mla": wq_mla.reshape(P, 2, 4, P), "wk_mla": wk_mla.reshape(P, 5, P),
        "wuv": wuv, "wo_mla": a["L0_attn_W_O"], "rope": _rope_tables(),
        "wr": a["L0_ffn_Wr"], "br": rows(a["L0_ffn_br"], E0),
        "w1": a["L0_ffn_W1"].transpose(1, 0, 2),
        "w2": a["L0_ffn_W2"].reshape(E0, NF, P, D).transpose(2, 1, 0, 3),
        "rank": rows(np.arange(E0, 0, -1, dtype=np.float32), E0),
        "wq1": np.broadcast_to(wq1, (D, 4, 4, 4 * DA)).reshape(D, 4, P),
        "wkvo1": np.stack([a["L1_xattn_Wkv"][:D].T, a["L1_xattn_Wkv"][D:].T, a["L1_xattn_Wo"].T], 1),
        "nbias": np.broadcast_to(a["L1_xattn_nbias"][None, :], (P, 1)),
        "headsel": ((np.arange(P)[:, None] % HR) // DA == np.arange(4)).astype(np.float32),
        "wqkv_sa": np.stack([a["L1_attn_W_q"], a["L1_attn_W_k"], a["L1_attn_W_v"]], 1),
        "bqk_sa": np.stack([a["L1_attn_b_q"], a["L1_attn_b_k"]], 1),
        "bv_sa": rows(a["L1_attn_b_v"], D),
        "gate_w": a["L1_ffn_gate_w"].T, "gate_b": rows(a["L1_ffn_expert_bias"], E1),
        "below": np.broadcast_to((e[None, :] < e[:, None]).astype(np.float32), (P, E1, E1)),
        "wg": np.concatenate([a["L1_ffn_w_gate"], a["L1_ffn_shared_gate_w"][None]]).transpose(2, 0, 1),
        "wu": np.concatenate([a["L1_ffn_w_up"], a["L1_ffn_shared_up_w"][None]]).transpose(2, 0, 1),
        "wd": np.concatenate([a["L1_ffn_w_down"], a["L1_ffn_shared_down_w"][None]]).transpose(2, 0, 1),
        "ident": np.eye(P, dtype=np.float32),
    }


def kernel(**inputs):
    import concourse.bacc as bacc
    from concourse.bass_utils import run_bass_kernel_spmd

    nc = bacc.Bacc("TRN2", target_bir_lowering=False, num_devices=1)
    arrays = {k: np.ascontiguousarray(v) for k, v in
              _layout({k: np.asarray(v) for k, v in inputs.items()}).items()}
    ins = {}
    for name, shape in INPUTS.items():
        a = arrays[name]
        assert a.shape == shape, (name, a.shape, shape)
        ins[name] = nc.dram_tensor(f"in_{name}", shape, mybir.dt.from_np(a.dtype), kind="ExternalInput").ap()
    out = nc.dram_tensor("out_x", (B, S, D), F32, kind="ExternalOutput").ap()
    build(nc, ins, out)
    r = run_bass_kernel_spmd(nc, [{f"in_{k}": arrays[k] for k in INPUTS}], core_ids=[0])
    return r.results[0]["out_x"]
```

```python
from contextlib import ExitStack
import math

import numpy as np
import concourse.bass as bass
from concourse import mybir

F32 = mybir.dt.float32
F32R = mybir.dt.float32r
I32 = mybir.dt.int32
U8 = mybir.dt.uint8
ALU = mybir.AluOpType
ACT = mybir.ActivationFunctionType
AX = mybir.AxisListType

P = 128
B = 2
S = 128
T = B * S
D = 128
CTX = 2048
NBLK = CTX // P
H = 16
DH = 64
QUAD = 4
NQ = B * H // QUAD
CH = CTX // 512
SCALE0 = DH ** -0.5
LAT = 32
DC = D // H
DR = DC // 2
HR = 32
CLIP = 80.0
SCALE_MLA = 1.0 / math.sqrt(DC + DR)
E0 = 8
FF = 512
NF = FF // P
DA = D // H
SCALE1 = 1.0 / math.sqrt(DA)
BIG = 1.0e38
TINY = 1e-32
SCALE_SA = 1.0 / math.sqrt(D)
E1 = 16
TOPK = 8
ROUTE_SCALE = 2.826
EPS = 1e-5
RSQRT_SEED = 0x5F3759DF

WARM = 7

INPUTS = {
    "x_tok": (S, B, D), "ctx_nat": (P, B * NBLK, D), "ctx_t": (D, B * CTX),
    "mask_t": (P, B * NBLK, S),
    "wq0": (D, H * DH), "wk0_t": (P, H, D), "wv0": (D, H * DH), "wo0": (P, H // 2, D), "bo0": (P, D),
    "w_lat": (D, P), "wq_mla": (P, 2, 4, P), "wk_mla": (P, 5, P), "wuv": (P, D), "wo_mla": (D, D), "rope": (P, 2, S),
    "wr": (D, E0), "br": (P, E0), "w1": (D, E0, FF), "w2": (P, NF, E0, D), "rank": (P, E0),
    "wq1": (D, 4, P), "wkvo1": (D, 3, D), "nbias": (P, 1), "headsel": (P, 4),
    "wqkv_sa": (D, 3, D), "bqk_sa": (D, 2), "bv_sa": (P, D),
    "gate_w": (D, E1), "gate_b": (P, E1), "below": (P, E1, E1),
    "wg": (D, E1 + 1, P), "wu": (D, E1 + 1, P), "wd": (P, E1 + 1, D),
    "ident": (P, P),
}


class Arena:

    def __init__(self, nc, start, end):
        self.nc, self.at, self.end = nc, start, end

    def take(self, name, shape, dt=F32):
        size = int(np.prod(shape[1:])) * (1 if dt == U8 else 4)
        t = self.nc.alloc_sbuf_tensor_at(name, list(shape), dt, offset=self.at)
        self.at += -(-size // 32) * 32
        assert self.at <= self.end, (name, self.at - self.end)
        return t


def build(nc, ins, out):
    with ExitStack() as ctx:
        def sem(name):
            return ctx.enter_context(nc.semaphore(name))

        def bc(ap, axis, n):
            ap = ap.unsqueeze(axis)
            shape = list(ap.shape)
            shape[axis] = n
            return ap.to_broadcast(shape)

        start = -(-nc.sbuf_base // 32) * 32
        end = nc.sbuf_usable_end
        A = Arena(nc, start, end)
        x = A.take("x", (P, B, D))
        xn = A.take("xn", (P, B, D))
        xnT = A.take("xnT", (P, T))
        ident = A.take("ident_sb", (P, P))
        headsel = A.take("headsel_sb", (P, 4))
        nbias = A.take("nbias_sb", (P, 1))
        neg_nbias = A.take("neg_nbias", (P, 1))
        bias_rows = A.take("bias_rows", (P, 2 * D))
        br_sb = A.take("br_sb", (P, E0))
        rank_sb = A.take("rank_sb", (P, E0))
        wr_sb = A.take("wr_sb", (P, E0))
        w_lat = A.take("w_lat_sb", (P, P))
        wuv = A.take("wuv_sb", (P, D))
        wo_mla = A.take("wo_mla_sb", (P, D))
        rope = A.take("rope_sb", (P, 2, S))
        stats = A.take("stats", (P, B, 6))
        mv = A.take("mv", (P, B, 2))
        nwt = A.take("nwt", (P, 4, B))
        seed = A.take("seed", (P, 2, B), I32)
        max2 = A.take("max2", (P, 2 * 2))
        nmax = A.take("nmax", (P, 2))
        rowsum = A.take("rowsum", (P, B * H, 2))
        rden = A.take("rden", (P, 2, QUAD))
        xb = A.take("xb", (P, B, D))
        zeros = A.take("zeros", (P, T))
        attn0 = A.take("attn0", (P, B, H * DH))
        attn0_at = A.at - B * H * DH * 4
        wv0 = A.take("wv0_sb", (P, H * DH))
        wo0 = A.take("wo0_sb", (P, H // 2, D))
        wo0_at = A.at - H // 2 * D * 4
        stage = A.at

        A = Arena(nc, stage, end)
        ctxT_hi = A.take("ctxT_hi", (P, B * CTX), F32R)
        ctxT_lo = A.take("ctxT_lo", (P, B * CTX), F32R)
        probs_at = A.at
        probs = A.take("probs", (P, 2, QUAD, CTX))
        qk_at = A.at
        qk_hi = A.take("qk_hi", (P, H, B, S), F32R)
        qk_lo = A.take("qk_lo", (P, H, B, S), F32R)
        ctx_at = A.at
        ctx_hi = A.take("ctx_hi", (P, B * NBLK, D), F32R)
        ctx_lo = A.take("ctx_lo", (P, B * NBLK, D), F32R)
        pT_at = A.at
        pT_hi = A.take("pT_hi", (P, 3, 512), F32R)
        pT_lo = A.take("pT_lo", (P, 3, 512), F32R)
        u_sb = A.take("u_sb", (P, 512))
        A = Arena(nc, probs_at + QUAD * CTX * 4, qk_at)
        ctx_raw1 = A.take("ctx_raw1", (P, 2, CTX))
        wq0 = A.take("wq0_sb", (P, H * DH))
        wk0_t = A.take("wk0_t_sb", (P, H, D))
        q0T = A.take("q0T", (P, 2, 2, T))
        ctxT_raw0 = Arena(nc, pT_at, end).take("ctxT_raw0", (P, CTX))
        ctx_raw0 = Arena(nc, attn0_at, stage).take("ctx_raw0", (P, CTX))

        A = Arena(nc, stage, probs_at)
        w1 = A.take("w1_sb", (P, E0, FF))
        w2 = A.take("w2_sb", (P, NF, E0, D))
        A = Arena(nc, stage, probs_at)
        wg = A.take("wg_sb", (P, E1 + 1, P))
        wu = A.take("wu_sb", (P, E1 + 1, P))
        wd = A.take("wd_sb", (P, E1 + 1, D))
        oT1 = A.take("oT1", (P, 2 * 4, S))
        keep = A.take("keep", (P, B, 2 * S))
        A = Arena(nc, probs_at, qk_at)
        attn0T = A.take("attn0T", (P, B, H // 2, S))
        lat_at = A.at
        lat_sb = A.take("lat_sb", (P, T))
        qr_at = A.at
        qr = A.take("qr", (P, 4, T))
        kr_at = A.at
        kr = A.take("kr", (P, 4, T))
        ropet_at = A.at
        ropet = A.take("ropet", (P, 4, T))
        ropek = A.take("ropek", (P, T))
        vx = A.take("vx", (P, B, H, HR))
        qbd_m = A.take("qbd_m", (P, B, 4, 4, S))
        pm = A.take("pm", (P, B, 4, 4, S))
        rl_m = A.take("rl_m", (P, B, H))
        wq_mla = A.take("wq_mla_sb", (P, 2, 4, P))
        clipped = Arena(nc, probs_at, lat_at).take("clipped", (P, 2, 1024))
        A = Arena(nc, qr_at, kr_at)
        oTm = A.take("oTm", (P, B, 4, S))
        A = Arena(nc, ropet_at, qk_at)
        attn_m = A.take("attn_m", (P, B, H, DC))
        attn_mT = A.take("attn_mT", (P, T))
        A = Arena(nc, probs_at, qk_at)
        kstack = A.take("kstack", (P, 4, B * CTX), F32R)
        A = Arena(nc, probs_at, qk_at)
        qk_sa = A.take("qk_sa", (P, 2, T))
        v_sa = A.take("v_sa", (P, B, D))
        p_sa = A.take("p_sa", (P, B, S))
        pT_sa = A.take("pT_sa", (P, T))
        mx_sa = A.take("mx_sa", (P, 4, B))
        wqkv = A.take("wqkv_sb", (P, 3, D))
        bqk = A.take("bqk_sb", (P, 2))
        gate_w = A.take("gate_w_sb", (P, E1))
        gate_b = A.take("gate_b_sb", (P, E1))
        below = A.take("below_sb", (P, E1, E1))
        sc1 = A.take("sc1", (P, 4, B, E1))
        cmp1 = A.take("cmp1", (P, 3, B, E1, E1))
        comb = A.take("comb", (P, B, E1))
        csum = A.take("csum", (P, 2, B))
        silu_g = A.take("silu_g", (P, 2, 512))
        hT1 = A.take("hT1", (P, E1 + 1, T))
        y_scaled = A.take("y_scaled", (P, 3, D))
        A = Arena(nc, qk_at, ctx_at)
        ctxT_raw2 = A.take("ctxT_raw2", (P, B * CTX))
        k1_raw = Arena(nc, A.at, ctx_at).take("k1_raw", (P, B * CTX))
        cap = A.take("cap", (P, B * NBLK, S))
        A = Arena(nc, qk_at, ctx_at)
        xm = A.take("xm", (P, B, E0, S))
        g0 = A.take("g0", (P, NF, T))
        yw = A.take("yw", (P, E0, D))
        A = Arena(nc, qk_at, ctx_at)
        qbd = A.take("qbd", (P, B, 4, 4, S), F32R)
        A = Arena(nc, ctx_at, end)
        k1_hi = A.take("k1_hi", (P, B * CTX), F32R)
        k1_lo = A.take("k1_lo", (P, B * CTX), F32R)
        v1 = A.take("v1", (P, B * NBLK, H, DA + 1))
        A = Arena(nc, ctx_at, end)
        w_ring = A.take("w_ring", (P, 3, 1024))
        p_ring = A.take("p_ring", (P, 3, 1024))
        w_first = A.take("w_first", (P, 1024))
        attn1 = A.take("attn1", (P, B, H, DA))
        attn1T = A.take("attn1T", (P, T))
        rl1 = A.take("rl1", (P, 2 * 4, 4))
        A = Arena(nc, attn0_at, attn0_at + B * H * DH * 4)
        wk_mla = A.take("wk_mla_sb", (P, 5, P))
        A2 = Arena(nc, attn0_at, attn0_at + B * H * DH * 4)
        diag = A2.take("diag", (P, B, E0, S))
        A2 = Arena(nc, attn0_at, attn0_at + B * H * DH * 4)
        q1 = A2.take("q1", (P, 4, T))
        q1s = A2.take("q1s", (P, 4, T), F32R)
        p_first = Arena(nc, attn0_at, stage).take("p_first", (P, 1024))
        A = Arena(nc, attn0_at + B * H * DH * 4, wo0_at)
        rt = A.take("rt", (P, 5, B, E0))
        rtm = A.take("rtm", (P, 2, B))
        wq1 = A.take("wq1_sb", (P, 4, P))
        wkvo1 = A.take("wkvo1_sb", (P, 3, D))
        mask_sb = Arena(nc, wo0_at, stage).take("mask_sb", (P, B * NBLK, S), U8)

        ps = ctx.enter_context(nc.psum_tensor("ps", [P, 8, 512], F32))

        load = {n: sem("ld_" + n) for n in (
            "x", "wqk0", "wqk1", "ctxT0", "ctxT1", "ctx0", "ctx1", "vo0", "small", "mla",
            "w1", "w2", "ctxT2", "mask", "l1w", "kstack", "exp1", "sa")}
        xn_ready, xnT_psum, xnT_ready = sem("xn_ready"), sem("xnT_psum"), sem("xnT_ready")
        chain = sem("dve_chain")
        q0_psum, q0_sb = sem("q0_psum"), sem("q0_sb")
        qk_psum, qk_hi_done, qk_lo_done = sem("qk_psum"), sem("qk_hi_done"), sem("qk_lo_done")
        splitT_hi, splitT_lo = sem("splitT_hi"), sem("splitT_lo")
        split_hi, split_lo = sem("split_hi"), sem("split_lo")
        scored, maxed, exped = sem("scored"), sem("maxed"), sem("exped")
        turned, hi_done, lo_done, pv_done = sem("turned"), sem("hi_done"), sem("lo_done"), sem("pv_done")
        u_copied, o_psum, o_copied = sem("u_copied"), sem("o_psum"), sem("o_copied")
        a0_turned, a0T_act, a0T_dve, proj0 = sem("a0_turned"), sem("a0T_act"), sem("a0T_dve"), sem("proj0")
        xb_done = sem("xb_done")
        lat_psum, lat_copied = sem("lat_psum"), sem("lat_copied")
        k_psum, vm_psum, q_psum, qsw_psum = sem("k_psum"), sem("vm_psum"), sem("q_psum"), sem("qsw_psum")
        kc_read, kr_done, q_terms, qbd_m_dve, qbd_m_pool = (
            sem("kc_read"), sem("kr_done"), sem("q_terms"), sem("qbd_m_dve"), sem("qbd_m_pool"))
        vm_done, zeroed = sem("vm_done"), sem("zeroed")
        ms_psum, ms_clip, ms_exp, ms_masked = sem("ms_psum"), sem("ms_clip"), sem("ms_exp"), sem("ms_masked")
        mo_psum, mo_T, mo_turned, mo_norm, mo_turned2, mo_T2, mo_proj = (
            sem("mo_psum"), sem("mo_T"), sem("mo_turned"), sem("mo_norm"), sem("mo_turned2"), sem("mo_T2"),
            sem("mo_proj"))
        rt_psum, rt_z, rt_e, diag_done = sem("rt_psum"), sem("rt_z"), sem("rt_e"), sem("diag_done")
        xm_psum, xm_act, xm_dve = sem("xm_psum"), sem("xm_act"), sem("xm_dve")
        h0_psum, g0_done, y0_psum = sem("h0_psum"), sem("g0_done"), sem("y0_psum")
        kv_psum, kv_act, k1_split = sem("kv_psum"), sem("kv_act"), sem("k1_split")
        q1s_done, qbd_pool = sem("q1s_done"), sem("qbd_pool")
        cap_big, cap_done = sem("cap_big"), sem("cap_done")
        q1_psum, q1_done, qbd_done = sem("q1_psum"), sem("q1_done"), sem("qbd_done")
        s1_psum, w1_done, sq_done, pv1_done = sem("s1_psum"), sem("w1_done"), sem("sq_done"), sem("pv1_done")
        keep_done, relu_done, kept, sq_pool = sem("keep_done"), sem("relu_done"), sem("kept"), sem("sq_pool")
        warm, acc_zero, o1_copied = sem("warm"), sem("acc_zero"), sem("o1_copied")
        o1_turned, o1_norm, o1_turned2, o1_T, o1_proj = (sem("o1_turned"), sem("o1_norm"), sem("o1_turned2"),
                                                         sem("o1_T"), sem("o1_proj"))
        sa_psum, sa_qk, sa_v, sa_score, sa_max, sa_exp, sa_turned, sa_T, sa_out = (
            sem("sa_psum"), sem("sa_qk"), sem("sa_v"), sem("sa_score"), sem("sa_max"), sem("sa_exp"),
            sem("sa_turned"), sem("sa_T"), sem("sa_out"))
        gt_psum, gt_z, gt_e = sem("gt_psum"), sem("gt_z"), sem("gt_e")
        gu_psum, silu_done, h1_done, y1_psum = sem("gu_psum"), sem("silu_done"), sem("h1_done"), sem("y1_psum")
        routed, y1_added, y1_scaled, y1_pool, stored = (sem("routed"), sem("y1_added"), sem("y1_scaled"),
                                                        sem("y1_pool"), sem("stored"))

        def down_bank(e, b):
            if e < DOWN_LAST:
                return 4 + 2 * b + e % 2
            return ((4, 6), (5, 7), (2, 3), (0, 1))[(e - DOWN_LAST) % 4][b]

        def turn_bank(n):
            return 4 + n % 2 if n < TAIL else (n - TAIL) % 4

        def qk_pair(t, n):
            return t[:, 2 * n:2 * n + 2, :, :].rearrange("p h b s -> p (h b s)")

        def ctx_chunk(i):
            part, c = i // 4, i % 4
            b, nat = part // 2, part % 2
            cols = slice(c * 512, (c + 1) * 512)
            raw = (ctxT_raw0, ctx_raw0)[nat][:, cols] if b == 0 else ctx_raw1[:, nat, cols]
            if nat:
                rows = slice(b * NBLK + 4 * c, b * NBLK + 4 * c + 4)
                hi_t, lo_t = (t[:, rows, :].rearrange("p k d -> p (k d)") for t in (ctx_hi, ctx_lo))
            else:
                hi_t, lo_t = (t[:, b * CTX + c * 512:b * CTX + (c + 1) * 512] for t in (ctxT_hi, ctxT_lo))
            return hi_t, lo_t, raw, load[("ctxT0", "ctx0", "ctxT1", "ctx1")[part]]

        def place_q(engine, b, j):
            rows, cols = slice(HR * j, HR * j + HR), slice(b * S, (b + 1) * S)
            return engine.tensor_tensor(qbd_m[rows, b, :, j, :], qr[rows, :, cols], ropet[rows, :, cols], ALU.add)

        def spread_q(engine, c):
            b, g = c // 4, c % 4
            return engine.tensor_tensor(qbd[:, b, g, :, :], bc(q1s[:, g, b * S:(b + 1) * S], 1, 4),
                                        bc(headsel[:], 2, S), ALU.mult)

        NHS = B * H
        NB0 = NQ * NBLK
        LAG = 3
        TAIL = NB0 - NBLK
        UNITS = NBLK // 2
        COMBOS = B * 4
        NU = COMBOS * UNITS
        WEIGH_LAG = 5
        NKV = B * CTX // 512
        FILL = [[("v", i) for i in range(4)],
                [("k", i) for i in range(3)],
                [("k", 3), ("v", 4)],
                [("k", i) for i in range(4, 7)] + [("v", 5)],
                [("k", 7)] + [("v", i) for i in range(6, NKV)]]
        EP = (E1 + 2) // 2
        DOWN_LAG = 2
        DOWN_LAST = 2 * (EP - DOWN_LAG - 1)

        def c_of(m):
            return m // UNITS

        def is_first(m):
            return m % UNITS == 0

        def nth(m):
            return m - m // UNITS

        block = ctx.enter_context(nc.Block())

        @block.sync
        def _(sp):
            def get(dst, name, s, src=None):
                sp.dma_start(dst, ins[name] if src is None else src).then_inc(load[s], 16)

            get(x[:], "x_tok", "x")
            get(ident[:], "ident", "x")
            get(wq0[:, 0:2 * P], "wq0", "wqk0", ins["wq0"][:, 0:2 * P])
            get(wk0_t[:, 0:QUAD, :], "wk0_t", "wqk0", ins["wk0_t"][:, 0:QUAD, :])
            get(ctxT_raw0[:], "ctx_t", "ctxT0", ins["ctx_t"][:, 0:CTX])
            get(wq0[:, 2 * P:], "wq0", "wqk1", ins["wq0"][:, 2 * P:])
            get(wk0_t[:, QUAD:, :], "wk0_t", "wqk1", ins["wk0_t"][:, QUAD:, :])
            get(ctx_raw0[:], "ctx_nat", "ctx0", ins["ctx_nat"][:, 0:NBLK, :].rearrange("p k d -> p (k d)"))
            get(ctx_raw1[:, 0, :], "ctx_t", "ctxT1", ins["ctx_t"][:, CTX:])
            get(ctx_raw1[:, 1, :], "ctx_nat", "ctx1", ins["ctx_nat"][:, NBLK:, :].rearrange("p k d -> p (k d)"))
            get(wv0[:], "wv0", "vo0")
            get(wo0[:], "wo0", "vo0")
            small = [(bias_rows[:, 0:D], "bo0"), (bias_rows[:, D:2 * D], "bv_sa"), (w_lat[:], "w_lat"),
                     (wuv[:], "wuv"), (wo_mla[:], "wo_mla"), (rope[:], "rope"), (wr_sb[:], "wr"),
                     (br_sb[:], "br"), (rank_sb[:], "rank"), (headsel[:], "headsel"), (nbias[:], "nbias")]
            assert len(small) == N_SMALL
            for dst, name in small:
                get(dst, name, "small")
            sp.wait_ge(scored, 2 * NHS)
            get(ctxT_raw2[:], "ctx_t", "ctxT2")
            get(w1[:], "w1", "w1")
            get(w2[:], "w2", "w2")
            sp.wait_ge(turned, NB0)
            get(wq_mla[:], "wq_mla", "mla")
            sp.wait_ge(o_psum, NQ)
            get(wkvo1[:], "wkvo1", "l1w")
            get(wq1[:], "wq1", "l1w")
            sp.wait_ge(a0_turned, B)
            get(wk_mla[:], "wk_mla", "mla")
            sp.wait_ge(proj0, B)
            get(mask_sb[:], "mask_t", "mask")
            sp.wait_ge(mo_proj, 1)
            sp.wait_ge(kv_act, 2 * NKV)
            sp.wait_ge(k1_split, NKV)
            for t in range(4):
                part = k1_lo if t % 2 else k1_hi
                for g in range(4):
                    sp.dma_start(kstack[32 * t:32 * t + 32, g, :].bitcast(F32),
                                 part[32 * g:32 * g + 32, :].bitcast(F32)).then_inc(load["kstack"], 16)
            sp.wait_ge(y0_psum, 2 * B)
            get(wg[:], "wg", "exp1")
            get(wu[:], "wu", "exp1")
            get(wd[:], "wd", "exp1")
            sp.wait_ge(s1_psum, NU)
            get(wqkv[:], "wqkv_sa", "sa")
            get(bqk[:], "bqk_sa", "sa")
            get(gate_w[:], "gate_w", "sa")
            get(gate_b[:], "gate_b", "sa")
            get(below[:], "below", "sa")
            sp.wait_ge(y1_added, E1 + 1)
            sp.wait_ge(y1_pool, E1 + 1)
            sp.dma_start(out.rearrange("b s d -> s b d"), x[:]).then_inc(stored, 16)
            sp.wait_ge(stored, 16)

        @block.tensor
        def _(pe):
            mm = nc.tensor.matmul

            def turn_xn(layer):
                pe.wait_ge(xn_ready, layer + 1)
                for b in range(B):
                    last = nc.tensor.transpose(ps[:, 5, b * S:(b + 1) * S], xn[:, b, :], ident[:])
                last.then_inc(xnT_psum, 1)
                pe.wait_ge(xnT_ready, layer + 1)

            def keep_warm(bank, count):
                for _ in range(count):
                    mm(ps[:, bank, 0:T], zeros[:, 0:P], zeros[:], start=True, stop=True)

            pe.wait_ge(warm, 1)
            keep_warm(0, WARM)
            pe.wait_ge(load["x"], 32)
            turn_xn(0)

            def make_q(i):
                pe.wait_ge(load[f"wqk{min(i, 1)}"], 32)
                for t in range(2):
                    last = mm(ps[:, 4, t * T:(t + 1) * T], wq0[:, (2 * i + t) * P:(2 * i + t + 1) * P], xnT[:],
                              start=True, stop=True)
                last.then_inc(q0_psum, 1)

            def make_qk(n):
                pe.wait_ge(q0_sb, n // 2 + 1)
                if n >= 2:
                    pe.wait_ge(qk_lo_done, n - 1)
                for j in range(2):
                    last = mm(ps[:, 6 + n % 2, j * T:(j + 1) * T], wk0_t[:, 2 * n + j, :],
                              q0T[:, n // 2 % 2, n % 2, :], start=True, stop=True)
                last.then_inc(qk_psum, 1)

            def scores(hs, c):
                b, h = hs // H, hs % H
                if hs >= 1:
                    pe.wait_ge(exped, 2 * (hs - 1) + c // 2 + 1)
                if hs == 0:
                    pe.wait_ge(splitT_lo, c + 1)
                if hs == H:
                    pe.wait_ge(split_lo, 4 + c + 1)
                cols = slice(b * CTX + c * 512, b * CTX + (c + 1) * 512)
                mm(ps[:, c, :], qk_hi[:, h, b, :], ctxT_hi[:, cols], start=True, stop=False)
                mm(ps[:, c, :], qk_lo[:, h, b, :], ctxT_hi[:, cols], start=False, stop=False)
                last = mm(ps[:, c, :], qk_hi[:, h, b, :], ctxT_lo[:, cols], start=False, stop=True)
                if c % 2:
                    last.then_inc(scored, 1)

            def turn_probs(n):
                q, k = n // NBLK, n % NBLK
                if k == 0:
                    pe.wait_ge(exped, 2 * QUAD * (q + 1))
                if n == 0:
                    pe.wait_ge(q0_sb, QUAD)
                if n >= TAIL + 4:
                    pe.wait_ge(lo_done, n - 3)
                elif 2 <= n < TAIL:
                    pe.wait_ge(lo_done, n - 1)
                for j in range(QUAD):
                    last = nc.tensor.transpose(ps[:, turn_bank(n), j * S:(j + 1) * S],
                                               probs[:, q % 2, j, k * P:(k + 1) * P], ident[:])
                last.then_inc(turned, 1)

            def weigh_ctx(n):
                q, k = n // NBLK, n % NBLK
                row = (q // QUAD) * NBLK + k
                if k == 0 and q < 2:
                    pe.wait_ge(qk_lo_done, H // 2 - 1 + q)
                if k == 0 and q >= 2:
                    pe.wait_ge(o_copied, q - 1)
                if q % QUAD == 0 and k % 4 == 0:
                    pe.wait_ge(split_lo, (0, 8)[q // QUAD] + k // 4 + 1)
                pe.wait_ge(lo_done, n + 1)
                acc = ps[:, 6 + q % 2, :]
                mm(acc, ctx_hi[:, row, :], pT_hi[:, n % 3, :], start=(k == 0), stop=False)
                mm(acc, ctx_hi[:, row, :], pT_lo[:, n % 3, :], start=False, stop=False)
                mm(acc, ctx_lo[:, row, :], pT_hi[:, n % 3, :], start=False,
                   stop=(k == NBLK - 1)).then_inc(pv_done, 1)
                if n >= NBLK and k == 2:
                    project_v(q - 1)

            def project_v(q):
                pe.wait_ge(u_copied, q + 1)
                if q == 0:
                    pe.wait_ge(load["vo0"], 32)
                for j in range(QUAD):
                    h = (q % QUAD) * QUAD + j // 2 * 2
                    last = mm(ps[:, 6 + q % 2, j * P:(j + 1) * P], u_sb[:, j * S:(j + 1) * S],
                              wv0[:, h * DH:(h + 2) * DH], start=True, stop=True)
                last.then_inc(o_psum, 1)

            make_q(0)
            make_qk(0)
            for step in range(NHS + QUAD):
                n0 = (step - QUAD) * QUAD
                if step < H and step % 2 == 0:
                    pe.wait_ge(qk_lo_done, step // 2 + 1)
                for slot in range(4):
                    if step < NHS and slot < 2:
                        scores(step, 2 * slot)
                        scores(step, 2 * slot + 1)
                    n = n0 + slot
                    if n >= LAG:
                        weigh_ctx(n - LAG)
                    if n >= 0:
                        turn_probs(n)
                if step < 4:
                    if step:
                        make_qk(2 * step)
                    make_qk(2 * step + 1)
                    if step < 3:
                        make_q(step + 1)
            for n in range(NB0 - LAG, NB0):
                weigh_ctx(n)

            def turn_o(b):
                for t in range(H // 2):
                    last = nc.tensor.transpose(ps[:, 2 * b + t // 4, (t % 4) * S:(t % 4 + 1) * S],
                                               attn0[:, b, t * P:(t + 1) * P], ident[:])
                last.then_inc(a0_turned, 1)

            def project_o(b):
                pe.wait_ge(a0T_act, b + 1)
                for t in range(H // 2):
                    if b and t == H // 4:
                        pe.wait_ge(a0T_dve, 1)
                    last = mm(ps[:, 4 + b, 0:D], attn0T[:, b, t, :], wo0[:, t, :],
                              start=(t == 0), stop=(t == H // 2 - 1))
                last.then_inc(proj0, 1)

            pe.wait_ge(o_copied, NQ // 2)
            turn_o(0)
            project_v(NQ - 1)
            project_o(0)
            pe.wait_ge(o_copied, NQ)
            turn_o(1)
            project_o(1)

            made = [0]

            def fill(gap):
                for kind, i in FILL[gap]:
                    n = made[0]
                    if n >= 2:
                        pe.wait_ge(kv_act, n - 1)
                    if kind == "k":
                        last = mm(ps[:, 6 + n % 2, :], wkvo1[:, 0, :], ctxT_raw2[:, i * 512:(i + 1) * 512],
                                  start=True, stop=True)
                    else:
                        for r in range(4):
                            at = (4 * i + r) * P
                            last = mm(ps[:, 6 + n % 2, r * P:(r + 1) * P], ctxT_raw2[:, at:at + P],
                                      wkvo1[:, 1, :], start=True, stop=True)
                    last.then_inc(kv_psum, 1)
                    made[0] += 1

            pe.wait_ge(load["ctxT2"], 16)
            pe.wait_ge(load["l1w"], 32)
            fill(0)
            turn_xn(1)
            pe.wait_ge(load["small"], 16 * N_SMALL)
            mm(ps[:, 5, T:2 * T], w_lat[:], xnT[:], start=True, stop=True).then_inc(lat_psum, 1)
            pe.wait_ge(lat_copied, 1)
            pe.wait_ge(load["mla"], 32)
            mm(ps[:, 4, 0:T], wk_mla[:, 4, :], lat_sb[:], start=True, stop=True)
            for g in range(4):
                last = mm(ps[:, g // 2, (g % 2) * T:(g % 2 + 1) * T], wk_mla[:, g, :], lat_sb[:],
                          start=True, stop=True)
            last.then_inc(k_psum, 1)
            for g in range(4):
                last = mm(ps[:, 2 + g // 2, (g % 2) * T:(g % 2 + 1) * T], wq_mla[:, 0, g, :], lat_sb[:],
                          start=True, stop=True)
            last.then_inc(q_psum, 1)
            pe.wait_ge(kc_read, 1)
            for g in range(4):
                last = mm(ps[:, g // 2, (g % 2) * T:(g % 2 + 1) * T], wq_mla[:, 1, g, :], lat_sb[:],
                          start=True, stop=True)
            last.then_inc(qsw_psum, 1)
            for b in range(B):
                last = mm(ps[:, 5, b * D:(b + 1) * D], lat_sb[:, b * S:(b + 1) * S], wuv[:],
                          start=True, stop=True)
            last.then_inc(vm_psum, 1)
            fill(1)
            pe.wait_ge(kr_done, 1)
            for b in range(B):
                pe.wait_ge(qbd_m_dve, b + 1)
                pe.wait_ge(qbd_m_pool, b + 1)
                for g in range(4):
                    if b and g % 2 == 0:
                        pe.wait_ge(ms_clip, g // 2 + 1)
                    last = mm(ps[:, g, :], kr[:, g, b * S:(b + 1) * S],
                              qbd_m[:, b, g, :, :].rearrange("p j s -> p (j s)"), start=True, stop=True)
                    if g % 2:
                        last.then_inc(ms_psum, 1)
            fill(2)
            pe.wait_ge(vm_done, 1)
            for b in range(B):
                for g in range(4):
                    if g % 2 == 0:
                        pe.wait_ge(ms_masked, 2 * b + g // 2 + 1)
                    for j in range(4):
                        last = mm(ps[HR * j:HR * j + HR, 4 + b, g * S:(g + 1) * S], vx[:, b, 4 * g + j, :],
                                  pm[:, b, g, j, :], start=True, stop=True)
                last.then_inc(mo_psum, 1)
            for b in range(B):
                pe.wait_ge(mo_T, b + 1)
                if b == 0:
                    pe.wait_ge(ms_clip, 2 * B)
                for g in range(4):
                    last = nc.tensor.transpose(ps[:, b, g * P:(g + 1) * P], oTm[:, b, g, :], ident[:])
                last.then_inc(mo_turned, 1)
            for b in range(B):
                pe.wait_ge(mo_norm, b + 1)
                last = nc.tensor.transpose(ps[:, 2, b * S:(b + 1) * S],
                                           attn_m[:, b, :, :].rearrange("p h d -> p (h d)"), ident[:])
            last.then_inc(mo_turned2, 1)
            pe.wait_ge(mo_T2, 1)
            for b in range(B):
                last = mm(ps[:, 3, b * D:(b + 1) * D], attn_mT[:, b * S:(b + 1) * S], wo_mla[:],
                          start=True, stop=True)
            last.then_inc(mo_proj, 1)

            fill(3)
            turn_xn(2)
            for b in range(B):
                last = mm(ps[:, 4, b * E0:(b + 1) * E0], xnT[:, b * S:(b + 1) * S], wr_sb[:],
                          start=True, stop=True)
            last.then_inc(rt_psum, 1)
            fill(4)
            for b in range(B):
                pe.wait_ge(diag_done, b + 1)
                for eh in range(2):
                    mm(ps[:, 2 * b + eh, :], xn[:, b, :],
                       diag[:, b, 4 * eh:4 * eh + 4, :].rearrange("p e s -> p (e s)"),
                       start=True, stop=True).then_inc(xm_psum, 1)
            pe.wait_ge(load["w1"], 16)
            pe.wait_ge(xm_act, 2)
            pe.wait_ge(xm_dve, 2)
            pe.wait_ge(kv_act, 2 * NKV)
            for f in range(NF):
                for e in range(E0):
                    last = mm(ps[:, 6 + f // 2, (f % 2) * T:(f % 2 + 1) * T], w1[:, e, f * P:(f + 1) * P],
                              xm[:, :, e, :], start=(e == 0), stop=(e == E0 - 1))
                last.then_inc(h0_psum, 1)
            pe.wait_ge(load["w2"], 16)
            pe.wait_ge(g0_done, NF)
            for b in range(B):
                for eh in range(2):
                    for f in range(NF):
                        last = mm(ps[:, 2 * b + eh, :], g0[:, f, b * S:(b + 1) * S],
                                  w2[:, f, 4 * eh:4 * eh + 4, :].rearrange("p e d -> p (e d)"),
                                  start=(f == 0), stop=(f == NF - 1))
                    last.then_inc(y0_psum, 1)

            keep_warm(4, 13)
            turn_xn(3)
            for g in range(4):
                last = mm(ps[:, g // 2, (g % 2) * T:(g % 2 + 1) * T], wq1[:, g, :], xnT[:], start=True, stop=True)
                if g % 2:
                    last.then_inc(q1_psum, 1)
            pe.wait_ge(load["kstack"], 16 * 16)

            def scores1(m):
                c, u = m // UNITS, m % UNITS
                b, g = c // 4, c % 4
                if m >= 3:
                    if is_first(m - 3):
                        pe.wait_ge(relu_done, c_of(m - 3) + 1)
                    else:
                        pe.wait_ge(w1_done, nth(m - 3))
                if m == 0:
                    pe.wait_ge(qbd_done, 1)
                    pe.wait_ge(q1_done, 2)
                elif u == 0:
                    pe.wait_ge(qbd_pool, c)
                for i in range(2):
                    at = b * CTX + (2 * u + i) * P
                    for a in range(2):
                        dst = ps[:, 2 * (m % 3) + a, :].rearrange("p (h i s) -> p h i s", h=2, i=2)[:, :, i, :]
                        last = mm(dst, kstack[:, g, at:at + P], qbd[:, b, g, 2 * a:2 * a + 2, :],
                                  start=True, stop=True)
                last.then_inc(s1_psum, 1)

            def weigh_v(n):
                c, u = n // UNITS, (n + 1) % UNITS
                b, g = c // 4, c % 4
                if u == 1 and c >= 2:
                    pe.wait_ge(o1_copied, c - 1)
                if u == 0:
                    pe.wait_ge(sq_pool, c + 1)
                    p = p_first[:]
                else:
                    at = nth(c * UNITS + u)
                    pe.wait_ge(sq_done, at)
                    p = p_ring[:, (at - 1) % 3, :]
                for i in range(2):
                    k = 2 * u + i
                    for j in range(4):
                        last = mm(ps[HR * j:HR * j + DA + 1, 6 + c % 2, 0:S], v1[:, b * NBLK + k, 4 * g + j, :],
                                  p[:, (2 * j + i) * S:(2 * j + i + 1) * S],
                                  start=(k == 2), stop=(k == 1))
                last.then_inc(pv1_done, 1)

            pe.wait_ge(acc_zero, 1)
            pe.wait_ge(zeroed, 4)
            for m in range(NU + WEIGH_LAG):
                if m < NU:
                    scores1(m)
                if m >= WEIGH_LAG:
                    weigh_v(m - WEIGH_LAG)
            for c in range(COMBOS):
                if c % 4 == 0:
                    pe.wait_ge(o1_copied, c + 4)
                last = nc.tensor.transpose(ps[:, c // 4, (c % 4) * P:(c % 4 + 1) * P], oT1[:, c, :], ident[:])
            last.then_inc(o1_turned, 1)
            pe.wait_ge(o1_norm, 1)
            for b in range(B):
                last = nc.tensor.transpose(ps[:, 2, b * S:(b + 1) * S],
                                           attn1[:, b, :, :].rearrange("p h d -> p (h d)"), ident[:])
            last.then_inc(o1_turned2, 1)
            pe.wait_ge(o1_T, 1)
            for b in range(B):
                last = mm(ps[:, 3, b * D:(b + 1) * D], attn1T[:, b * S:(b + 1) * S], wkvo1[:, 2, :],
                          start=True, stop=True)
            last.then_inc(o1_proj, 1)

            keep_warm(4, 6)
            turn_xn(4)
            pe.wait_ge(load["sa"], 16 * 5)
            for i in range(2):
                mm(ps[:, 0, i * T:(i + 1) * T], wqkv[:, i, :], xnT[:], start=True, stop=True)
            for b in range(B):
                last = mm(ps[:, 1, b * D:(b + 1) * D], xnT[:, b * S:(b + 1) * S], wqkv[:, 2, :],
                          start=True, stop=True)
            last.then_inc(sa_psum, 1)
            pe.wait_ge(sa_qk, 2)
            for b in range(B):
                last = mm(ps[:, 2, b * S:(b + 1) * S], qk_sa[:, 0, b * S:(b + 1) * S],
                          qk_sa[:, 1, b * S:(b + 1) * S], start=True, stop=True)
            last.then_inc(sa_score, 1)
            pe.wait_ge(sa_exp, B)
            for b in range(B):
                last = nc.tensor.transpose(ps[:, 3, b * S:(b + 1) * S], p_sa[:, b, :], ident[:])
            last.then_inc(sa_turned, 1)
            pe.wait_ge(sa_T, 1)
            pe.wait_ge(sa_v, 1)
            for b in range(B):
                last = mm(ps[:, 4, b * D:(b + 1) * D], pT_sa[:, b * S:(b + 1) * S], v_sa[:, b, :],
                          start=True, stop=True)
            last.then_inc(sa_out, 1)

            keep_warm(7, 8)
            turn_xn(5)
            for b in range(B):
                last = mm(ps[:, 6, b * E1:(b + 1) * E1], xnT[:, b * S:(b + 1) * S], gate_w[:],
                          start=True, stop=True)
            last.then_inc(gt_psum, 1)
            pe.wait_ge(load["exp1"], 48)

            def gate_up(i):
                if i >= 2:
                    pe.wait_ge(h1_done, i - 1)
                for w, weights in enumerate((wg, wu)):
                    for r in range(2):
                        e = 2 * i + r
                        if e <= E1:
                            last = mm(ps[:, 2 * (i % 2) + w, r * T:(r + 1) * T], weights[:, e, :], xnT[:],
                                      start=True, stop=True)
                last.then_inc(gu_psum, 1)

            def down(e):
                before = e - 2 if e < DOWN_LAST + 2 else e - 4
                if DOWN_LAST + 2 <= e < DOWN_LAST + 4:
                    pe.wait_ge(h1_done, EP)
                elif before >= 0:
                    pe.wait_ge(y1_added, before + 1)
                    pe.wait_ge(y1_scaled, before + 1)
                pe.wait_ge(h1_done, e // 2 + 1)
                for b in range(B):
                    last = mm(ps[:, down_bank(e, b), 0:D], hT1[:, e, b * S:(b + 1) * S], wd[:, e, :],
                              start=True, stop=True)
                last.then_inc(y1_psum, 1)

            for i in range(EP):
                gate_up(i)
                if i > DOWN_LAG:
                    down(2 * (i - DOWN_LAG - 1))
                    down(2 * (i - DOWN_LAG - 1) + 1)
            for e in range(DOWN_LAST, E1 + 1):
                down(e)

        @block.scalar
        def _(act):
            def copy(dst, src):
                return nc.scalar.activation(dst, src, ACT.Copy)

            def copy_xnT(layer):
                act.wait_ge(xnT_psum, layer + 1)
                copy(xnT[:], ps[:, 5, 0:T]).then_inc(xnT_ready, 1)


            def split(i):
                hi_t, _, raw, loaded = ctx_chunk(i)
                act.wait_ge(loaded, 16)
                copy(hi_t, raw).then_inc(splitT_hi, 1)

            def copy_q(i):
                act.wait_ge(q0_psum, i + 1)
                copy(q0T[:, i % 2, :, :].rearrange("p a t -> p (a t)"), ps[:, 4, :]).then_inc(q0_sb, 1)

            def make_qk(n):
                act.wait_ge(qk_psum, n + 1)
                copy(qk_pair(qk_hi, n), ps[:, 6 + n % 2, :]).then_inc(qk_hi_done, 1)

            copy_xnT(0)
            split(0)
            split(1)
            copy_q(0)
            split(2)
            split(3)
            make_qk(0)

            def hi(n):
                act.wait_ge(turned, n + 1)
                if n >= 3:
                    act.wait_ge(pv_done, n - 2)
                copy(pT_hi[:, n % 3, :], ps[:, turn_bank(n), :]).then_inc(hi_done, 1)

            def exp_half(hs, p):
                q, j = hs // QUAD, hs % QUAD
                act.wait_ge(maxed, hs + 1)
                if hs == QUAD and p == 0:
                    act.wait_ge(split_lo, 12)
                if q >= 2 and j == 0 and p == 0:
                    act.wait_ge(turned, NBLK * (q - 1))
                nc.scalar.activation(
                    probs[:, q % 2, j, p * 1024:(p + 1) * 1024].rearrange("p (a n) -> p a n", a=2),
                    ps[:, 2 * p:2 * p + 2, :], ACT.Exp, bias=nmax[:, hs % 2:hs % 2 + 1], scale=SCALE0,
                    accum_out=rowsum[:, hs, p:p + 1]).then_inc(exped, 1)

            def copy_u(q):
                act.wait_ge(pv_done, NBLK * (q + 1))
                if q >= 1:
                    act.wait_ge(o_psum, q)
                copy(u_sb[:], ps[:, 6 + q % 2, :]).then_inc(u_copied, 1)

            for step in range(NHS + QUAD):
                n0 = (step - QUAD) * QUAD
                if n0 >= 1:
                    hi(n0 - 1)
                if n0 >= 0:
                    hi(n0)
                    hi(n0 + 1)
                if step < NHS:
                    exp_half(step, 0)
                if n0 >= 0:
                    hi(n0 + 2)
                    if n0 >= NBLK and n0 % NBLK == 0:
                        copy_u(n0 // NBLK - 1)
                if 1 <= step < 4:
                    make_qk(2 * step)
                if step < NHS:
                    exp_half(step, 1)
                if step < 4:
                    make_qk(2 * step + 1)
                if step < 3:
                    copy_q(step + 1)
            hi(NB0 - 1)
            copy_u(NQ - 1)
            act.wait_ge(a0_turned, 1)
            copy(attn0T[:, 0, :, :].rearrange("p (a t) s -> p a (t s)", a=2), ps[:, 0:2, :]).then_inc(a0T_act, 1)
            act.wait_ge(a0_turned, 2)
            copy(attn0T[:, 1, 0:H // 4, :].rearrange("p t s -> p (t s)"), ps[:, 2, :]).then_inc(a0T_act, 1)

            made = [0]

            def fill(gap):
                for kind, i in FILL[gap]:
                    n = made[0]
                    act.wait_ge(kv_psum, n + 1)
                    bank = ps[:, 6 + n % 2, :]
                    if kind == "k":
                        cols = slice(i * 512, (i + 1) * 512)
                        copy(k1_raw[:, cols], bank)
                        copy(k1_hi[:, cols], bank).then_inc(kv_act, 1)
                    else:
                        copy(v1[:, 4 * i:4 * i + 4, :, 0:DA],
                             bank.rearrange("p (k h d) -> p k h d", k=4, h=H)).then_inc(kv_act, 1)
                    made[0] += 1

            fill(0)
            copy_xnT(1)
            act.wait_ge(lat_psum, 1)
            copy(lat_sb[:], ps[:, 5, T:2 * T]).then_inc(lat_copied, 1)
            act.wait_ge(vm_psum, 1)
            act.wait_ge(zeroed, 2)
            copy(vx[:, :, :, 0:DC], ps[:, 5, 0:T].rearrange("p (b h d) -> p b h d", b=B, h=H)).then_inc(vm_done, 1)
            fill(1)
            for i in range(2 * B):
                act.wait_ge(ms_clip, i + 1)
                nc.scalar.activation(pm[:, i // 2, 2 * (i % 2):2 * (i % 2) + 2, :, :].rearrange("p g j s -> p (g j s)"),
                                     clipped[:, i % 2, :], ACT.Exp, scale=SCALE_MLA).then_inc(ms_exp, 1)
            fill(2)
            for b in range(B):
                act.wait_ge(mo_psum, b + 1)
                copy(oTm[:, b, :, :].rearrange("p g s -> p (g s)"), ps[:, 4 + b, :]).then_inc(mo_T, 1)
            act.wait_ge(mo_turned2, 1)
            copy(attn_mT[:], ps[:, 2, 0:T]).then_inc(mo_T2, 1)

            fill(3)
            copy_xnT(2)
            act.wait_ge(rt_z, 1)
            nc.scalar.activation(rt[:, 1, :, :], rt[:, 0, :, :], ACT.Exp, scale=-1.0).then_inc(rt_e, 1)
            fill(4)
            for i in range(2):
                act.wait_ge(xm_psum, i + 1)
                copy(xm[:, 0, 4 * i:4 * i + 4, :].rearrange("p e s -> p (e s)"), ps[:, i, :]).then_inc(xm_act, 1)
            for f in range(NF):
                act.wait_ge(h0_psum, 2 * (f // 2) + 2)
                nc.scalar.activation(g0[:, f, :], ps[:, 6 + f // 2, (f % 2) * T:(f % 2 + 1) * T],
                                     ACT.Gelu).then_inc(g0_done, 1)

            copy_xnT(3)
            for i in range(2):
                act.wait_ge(q1_psum, i + 1)
                nc.scalar.activation(q1[:, 2 * i:2 * i + 2, :].rearrange("p g t -> p (g t)"), ps[:, i, :],
                                     ACT.Copy, scale=SCALE1).then_inc(q1_done, 1)

            def copy_o1(c):
                act.wait_ge(pv1_done, UNITS * (c + 1))
                copy(oT1[:, c, :], ps[:, 6 + c % 2, 0:S]).then_inc(o1_copied, 1)

            def relu_first(c):
                m = c * UNITS
                act.wait_ge(s1_psum, m + 1)
                if c:
                    act.wait_ge(sq_pool, c)
                at = 2 * (m % 3)
                nc.scalar.activation(w_first[:].rearrange("p (a n) -> p a n", a=2), ps[:, at:at + 2, :], ACT.Relu,
                                     bias=nbias[:]).then_inc(relu_done, 1)

            def weighed_at(at):
                return (at - 1) // (UNITS - 1) * UNITS + (at - 1) % (UNITS - 1) + 1

            for m in range(NU):
                if m % UNITS == 3 and m >= UNITS:
                    copy_o1(c_of(m) - 1)
                if m == 0:
                    relu_first(0)
                elif m % UNITS == UNITS - 1 and c_of(m) + 1 < COMBOS:
                    relu_first(c_of(m) + 1)
                if is_first(m):
                    continue
                at = nth(m)
                act.wait_ge(w1_done, at)
                if at > 3:
                    act.wait_ge(pv1_done, weighed_at(at - 3))
                nc.scalar.activation(p_ring[:, (at - 1) % 3, :], w_ring[:, (at - 1) % 3, :], ACT.Square,
                                     bias=nbias[:]).then_inc(sq_done, 1)
            copy_o1(COMBOS - 1)
            act.wait_ge(o1_turned2, 1)
            copy(attn1T[:], ps[:, 2, 0:T]).then_inc(o1_T, 1)

            copy_xnT(4)
            act.wait_ge(sa_psum, 1)
            for i in range(2):
                nc.scalar.activation(qk_sa[:, i, :], ps[:, 0, i * T:(i + 1) * T], ACT.Identity,
                                     bias=bqk[:, i:i + 1]).then_inc(sa_qk, 1)
            act.wait_ge(sa_max, 1)
            for b in range(B):
                nc.scalar.activation(p_sa[:, b, :], ps[:, 2, b * S:(b + 1) * S], ACT.Exp,
                                     bias=mx_sa[:, 1, b:b + 1], scale=SCALE_SA,
                                     accum_out=mx_sa[:, 2, b:b + 1]).then_inc(sa_exp, 1)
            act.wait_ge(sa_turned, 1)
            copy(pT_sa[:], ps[:, 3, 0:T]).then_inc(sa_T, 1)

            copy_xnT(5)
            act.wait_ge(gt_z, 1)
            nc.scalar.activation(sc1[:, 1, :, :], sc1[:, 0, :, :], ACT.Exp, scale=-1.0).then_inc(gt_e, 1)

            def scale_expert(e):
                act.wait_ge(y1_psum, e + 1)
                if e == 0:
                    act.wait_ge(routed, 1)
                if e >= 3:
                    act.wait_ge(y1_pool, e - 2)
                nc.scalar.activation(y_scaled[:, e % 3, :], ps[:, down_bank(e, 1), 0:D], ACT.Copy,
                                     scale=comb[:, 1, e:e + 1] if e < E1 else 1.0).then_inc(y1_scaled, 1)

            for i in range(EP):
                n = T * (2 if 2 * i + 1 <= E1 else 1)
                act.wait_ge(gu_psum, i + 1)
                if i >= 2:
                    act.wait_ge(h1_done, i - 1)
                nc.scalar.activation(silu_g[:, i % 2, 0:n], ps[:, 2 * (i % 2), 0:n], ACT.Silu)\
                    .then_inc(silu_done, 1)
                if i > DOWN_LAG:
                    scale_expert(2 * (i - DOWN_LAG - 1))
                    scale_expert(2 * (i - DOWN_LAG - 1) + 1)
            for e in range(DOWN_LAST, E1 + 1):
                scale_expert(e)

        @block.gpsimd
        def _(pool):
            nc.gpsimd.memset(zeros[:], 0.0).then_inc(warm, 1)
            for i in range(4, 16):
                hi_t, lo_t, raw, _ = ctx_chunk(i)
                pool.wait_ge(split_hi, i - 3)
                nc.gpsimd.tensor_tensor(lo_t, raw, hi_t, ALU.subtract).then_inc(split_lo, 1)
            pool.wait_ge(load["small"], 16 * N_SMALL)
            nc.gpsimd.tensor_tensor(xb[:], x[:], bc(bias_rows[:, 0:D], 1, B), ALU.add).then_inc(xb_done, 1)
            nc.gpsimd.tensor_scalar(neg_nbias[:], nbias[:], -1.0, None, ALU.mult).then_inc(zeroed, 1)
            pool.wait_ge(turned, NB0)
            nc.gpsimd.memset(vx[:, :, :, DC:DC + 1], 1.0)
            nc.gpsimd.memset(vx[:, :, :, DC + 1:HR], 0.0).then_inc(zeroed, 1)
            nc.gpsimd.memset(qbd_m[:], 0.0).then_inc(zeroed, 1)
            pool.wait_ge(o_psum, NQ)
            nc.gpsimd.memset(v1[:, :, :, DA:DA + 1], 1.0).then_inc(zeroed, 1)
            pool.wait_ge(kc_read, 1)
            nc.gpsimd.tensor_tensor(kr[:], kr[:], bc(ropek[:], 1, 4), ALU.add).then_inc(kr_done, 1)
            pool.wait_ge(kr_done, 1)
            pool.wait_ge(q_terms, 1)
            pool.wait_ge(zeroed, 4)
            for b in range(B):
                place_q(nc.gpsimd, b, 3).then_inc(qbd_m_pool, 1)
                pool.wait_ge(qbd_m_pool, b + 1)
            for i in range(2 * B):
                pool.wait_ge(ms_exp, i + 1)
                part = pm[:, i // 2, 2 * (i % 2):2 * (i % 2) + 2, :, :].rearrange("p g j s -> p (g j) s")
                nc.gpsimd.affine_select(out=part, in_=part, compare_op=ALU.is_ge, fill=0.0, base=0,
                                        pattern=[[0, 8], [1, S]], channel_multiplier=-1).then_inc(ms_masked, 1)
            items = [item for gap in FILL for item in gap]
            for n, (kind, i) in enumerate(items):
                if kind == "k":
                    cols = slice(i * 512, (i + 1) * 512)
                    pool.wait_ge(kv_act, n + 1)
                    nc.gpsimd.tensor_tensor(k1_lo[:, cols], k1_raw[:, cols], k1_hi[:, cols],
                                            ALU.subtract).then_inc(k1_split, 1)
            pool.wait_ge(q1s_done, 2)
            pool.wait_ge(keep_done, 1)
            for c in range(COMBOS):
                if c + 1 < COMBOS:
                    spread_q(nc.gpsimd, c + 1).then_inc(qbd_pool, 1)
                pool.wait_ge(relu_done, c + 1)
                heads = w_first[:].rearrange("p (h n) -> p h n", h=4)
                nc.gpsimd.tensor_tensor(heads, heads, bc(keep[:, c // 4, :], 1, 4), ALU.mult).then_inc(kept, 1)
                pool.wait_ge(kept, c + 1)
                if c:
                    pool.wait_ge(pv1_done, UNITS * c)
                nc.gpsimd.tensor_tensor(p_first[:], w_first[:], w_first[:], ALU.mult).then_inc(sq_pool, 1)
            for e in range(E1 + 1):
                pool.wait_ge(y1_scaled, e + 1)
                if e:
                    pool.wait_ge(y1_pool, e)
                nc.gpsimd.tensor_tensor(x[:, 1, :], x[:, 1, :], y_scaled[:, e % 3, :], ALU.add).then_inc(y1_pool, 1)

        @block.vector
        def _(dve):
            v = nc.vector
            links = [0]

            def link(ins_):
                links[0] += 1
                ins_.then_inc(chain, 1)
                dve.wait_ge(chain, links[0])

            def layer_norm(layer):
                for b in range(B):
                    s = v.bn_stats(stats[:, b, :], x[:, b, :])
                link(s)
                for b in range(B):
                    s = v.bn_aggr(mv[:, b, :], stats[:, b, :])
                link(s)
                var, y, t, half = (nwt[:, i, :] for i in range(4))
                v.tensor_scalar(half, mv[:, :, 1], EPS, -0.5, ALU.add, ALU.mult)
                link(v.tensor_scalar(var, mv[:, :, 1], EPS, None, ALU.add))
                link(v.tensor_scalar(seed[:, 0, :], var.bitcast(I32), 1, None, ALU.logical_shift_right))
                link(v.tensor_scalar(y.bitcast(I32), seed[:, 0, :], -1.0, float(RSQRT_SEED), ALU.mult, ALU.add))
                for _ in range(3):
                    for b in range(B):
                        s = v.scalar_tensor_tensor(t[:, b:b + 1], y[:, b:b + 1], half[:, b:b + 1],
                                                   y[:, b:b + 1], ALU.mult, ALU.mult)
                    link(s)
                    link(v.scalar_tensor_tensor(y, t, 1.5, y, ALU.add, ALU.mult))
                for b in range(B):
                    s = v.tensor_scalar(xn[:, b, :], x[:, b, :], mv[:, b, 0:1], nwt[:, 1, b:b + 1],
                                        ALU.subtract, ALU.mult)
                s.then_inc(xn_ready, 1)

            dve.wait_ge(load["x"], 32)
            layer_norm(0)


            def qk_rest(n):
                dve.wait_ge(qk_hi_done, n + 1)
                v.tensor_tensor(qk_pair(qk_lo, n), ps[:, 6 + n % 2, :], qk_pair(qk_hi, n),
                                ALU.subtract).then_inc(qk_lo_done, 1)

            def split_rest(i):
                hi_t, lo_t, raw, _ = ctx_chunk(i)
                dve.wait_ge(splitT_hi, i + 1)
                v.tensor_tensor(lo_t, raw, hi_t, ALU.subtract).then_inc(splitT_lo, 1)

            def split(i):
                hi_t, _, raw, loaded = ctx_chunk(i)
                dve.wait_ge(loaded, 16)
                v.tensor_copy(hi_t, raw).then_inc(split_hi, 1)

            for i in range(4):
                split_rest(i)
            qk_rest(0)

            def lo(n):
                dve.wait_ge(hi_done, n + 1)
                v.tensor_tensor(pT_lo[:, n % 3, :], ps[:, turn_bank(n), :], pT_hi[:, n % 3, :],
                                ALU.subtract).then_inc(lo_done, 1)

            def half_max(hs, p):
                dve.wait_ge(scored, 2 * hs + p + 1)
                return v.tensor_reduce(max2[:, p:p + 1], ps[:, 2 * p:2 * p + 2, :], AX.XY, ALU.max)

            def copy_o(q):
                hs = q * QUAD
                b, h = hs // H, hs % H
                r = rden[:, q % 2, :]
                dve.wait_ge(exped, 2 * QUAD * (q + 1))
                link(v.tensor_tensor(r, rowsum[:, hs:hs + QUAD, 0], rowsum[:, hs:hs + QUAD, 1], ALU.add))
                link(v.reciprocal(r, r))
                dve.wait_ge(o_psum, q + 1)
                for e in range(2):
                    s = v.tensor_tensor(
                        attn0[:, b, h * DH:(h + QUAD) * DH].rearrange("p (a f) -> p a f", a=2)[:, :, e * DH:(e + 1) * DH],
                        ps[:, 6 + q % 2, :].rearrange("p (a f) -> p a f", a=2)[:, :, e * (P + DH):e * (P + DH) + DH],
                        bc(r[:, e::2], 2, DH), ALU.mult)
                s.then_inc(o_copied, 1)

            for step in range(NHS + QUAD):
                n0 = (step - QUAD) * QUAD
                if 2 <= step <= 4:
                    qk_rest(2 * step - 2)
                if step < NHS:
                    half_max(step, 0)
                if 1 <= step <= 4:
                    qk_rest(2 * step - 1)
                if n0 >= 1:
                    lo(n0 - 1)
                if n0 >= 0:
                    lo(n0)
                if step < NHS:
                    link(half_max(step, 1))
                    v.tensor_scalar(nmax[:, step % 2:step % 2 + 1], max2[:, 0:1], max2[:, 1:2], -SCALE0,
                                    ALU.max, ALU.mult).then_inc(maxed, 1)
                if step < 3:
                    for i in range(4 * step + 4, 4 * step + 8):
                        split(i)
                if n0 >= 0:
                    lo(n0 + 1)
                    if n0 > NBLK and n0 % NBLK == QUAD:
                        copy_o(n0 // NBLK - 1)
                    lo(n0 + 2)
            lo(NB0 - 1)
            copy_o(NQ - 1)
            dve.wait_ge(a0_turned, B)
            v.tensor_copy(attn0T[:, 1, H // 4:, :].rearrange("p t s -> p (t s)"), ps[:, 3, :]).then_inc(a0T_dve, 1)
            dve.wait_ge(proj0, B)
            dve.wait_ge(xb_done, 1)
            link(v.tensor_tensor(x[:], ps[:, 4:6, 0:D], xb[:], ALU.add))

            layer_norm(1)
            cos, sin = rope[:, 0, :], rope[:, 1, :]
            rows_gb = "p g (b s) -> p (g b) s"

            def banks(a):
                return ps[:, a:a + 2, :].rearrange("p a (g s) -> p (a g) s", s=S)

            dve.wait_ge(k_psum, 1)
            v.tensor_tensor(ropek[:].rearrange("p (b s) -> p b s", b=B),
                            ps[:, 4, 0:T].rearrange("p (b s) -> p b s", b=B), bc(sin, 1, B), ALU.mult)
            v.tensor_tensor(kr[:].rearrange(rows_gb, b=B), banks(0), bc(cos, 1, 8), ALU.mult).then_inc(kc_read, 1)
            dve.wait_ge(q_psum, 1)
            v.tensor_tensor(qr[:].rearrange(rows_gb, b=B), banks(2), bc(cos, 1, 8), ALU.mult)
            dve.wait_ge(qsw_psum, 1)
            v.tensor_tensor(ropet[:].rearrange(rows_gb, b=B), banks(0), bc(sin, 1, 8), ALU.mult)\
                .then_inc(q_terms, 1)
            dve.wait_ge(q_terms, 1)
            dve.wait_ge(zeroed, 3)
            for b in range(B):
                for j in range(3):
                    s = place_q(v, b, j)
                s.then_inc(qbd_m_dve, 1)
            for i in range(2 * B):
                dve.wait_ge(ms_psum, i + 1)
                if i >= 2:
                    dve.wait_ge(ms_exp, i - 1)
                at = 2 * (i % 2)
                v.tensor_scalar(clipped[:, i % 2, :].rearrange("p (a n) -> p a n", a=2), ps[:, at:at + 2, :],
                                CLIP, -CLIP, ALU.min, ALU.max).then_inc(ms_clip, 1)
            for b in range(B):
                dve.wait_ge(mo_turned, b + 1)
                heads = ps[:, b, :].rearrange("p (h d) -> p h d", d=HR)
                link(v.reciprocal(rl_m[:, b, :], heads[:, :, DC]))
                v.tensor_tensor(attn_m[:, b, :, :], heads[:, :, 0:DC], bc(rl_m[:, b, :], 2, DC), ALU.mult)\
                    .then_inc(mo_norm, 1)
            dve.wait_ge(mo_proj, 1)
            xf = x[:].rearrange("p b d -> p (b d)")
            link(v.tensor_tensor(xf, ps[:, 3, 0:T], xf, ALU.add))

            layer_norm(2)
            z, ez, r, eq, onehot = (rt[:, i, :, :] for i in range(5))
            dve.wait_ge(rt_psum, 1)
            v.tensor_tensor(z, ps[:, 4, 0:B * E0].rearrange("p (b e) -> p b e", b=B),
                            bc(br_sb[:], 1, B), ALU.add).then_inc(rt_z, 1)
            dve.wait_ge(rt_e, 1)
            link(v.tensor_scalar(ez, ez, 1.0, None, ALU.add))
            link(v.reciprocal(r, ez))
            link(v.tensor_reduce(rtm[:, 0, :], r, AX.X, ALU.max))
            link(v.tensor_tensor(eq, r, bc(rtm[:, 0, :], 2, E0), ALU.is_equal))
            link(v.tensor_tensor(eq, eq, bc(rank_sb[:], 1, B), ALU.mult))
            link(v.tensor_reduce(rtm[:, 1, :], eq, AX.X, ALU.max))
            link(v.tensor_tensor(onehot, eq, bc(rtm[:, 1, :], 2, E0), ALU.is_equal))
            for b in range(B):
                v.tensor_tensor(diag[:, b, :, :], bc(ident[:], 1, E0), bc(onehot[:, b, :], 2, S), ALU.mult)\
                    .then_inc(diag_done, 1)
            link(v.tensor_tensor(eq, onehot, bc(rtm[:, 0, :], 2, E0), ALU.mult))
            for i in range(2):
                dve.wait_ge(xm_psum, 3 + i)
                v.tensor_copy(xm[:, 1, 4 * i:4 * i + 4, :].rearrange("p e s -> p (e s)"), ps[:, 2 + i, :])\
                    .then_inc(xm_dve, 1)
            dve.wait_ge(load["mask"], 16)
            dve.wait_ge(zeroed, 1)
            dve.wait_ge(k1_split, NKV)
            v.tensor_scalar(cap[:], mask_sb[:], 0.0, BIG, ALU.is_equal, ALU.mult).then_inc(cap_big, 1)
            dve.wait_ge(cap_big, 1)
            v.tensor_scalar(cap[:], cap[:], neg_nbias[:], None, ALU.add).then_inc(cap_done, 1)
            for b in range(B):
                for eh in range(2):
                    dve.wait_ge(y0_psum, 2 * b + eh + 1)
                    part = yw[:, 4 * eh:4 * eh + 4, :]
                    link(v.tensor_tensor(part, ps[:, 2 * b + eh, :].rearrange("p (e d) -> p e d", d=D),
                                         bc(eq[:, b, 4 * eh:4 * eh + 4], 2, D), ALU.mult))
                    link(v.tensor_reduce(xb[:, b, :], part.rearrange("p e d -> p d e"), AX.X, ALU.add))
                    link(v.tensor_tensor(x[:, b, :], x[:, b, :], xb[:, b, :], ALU.add))

            layer_norm(3)
            v.memset(ps[:, 6:8, :], 0.0).then_inc(acc_zero, 1)
            dve.wait_ge(cap_done, 1)
            v.tensor_scalar(keep[:], cap[:].rearrange("p (b k) s -> p b (k s)", b=B)[:, :, 0:2 * S], neg_nbias[:],
                            None, ALU.is_gt).then_inc(keep_done, 1)
            for part, ready in ((slice(0, 1), 1), (slice(1, 4), 2)):
                dve.wait_ge(q1_done, ready)
                link(v.tensor_copy(q1s[:, part, :], q1[:, part, :]))
                v.tensor_tensor(q1s[64:128, part, :], q1[64:128, part, :], q1s[64:128, part, :],
                                ALU.subtract).then_inc(q1s_done, 1)
                dve.wait_ge(q1s_done, ready)
                if ready == 1:
                    spread_q(v, 0).then_inc(qbd_done, 1)
            dve.wait_ge(load["kstack"], 256)
            for m in range(NU):
                if is_first(m):
                    continue
                c, u, at = m // UNITS, m % UNITS, nth(m)
                dve.wait_ge(s1_psum, m + 1)
                if at > 3:
                    dve.wait_ge(sq_done, at - 3)
                k = (c // 4) * NBLK + 2 * u
                bank = 2 * (m % 3)
                v.scalar_tensor_tensor(
                    w_ring[:, (at - 1) % 3, :].rearrange("p (h n) -> p h n", h=4),
                    ps[:, bank:bank + 2, :].rearrange("p a (h n) -> p (a h) n", h=2), neg_nbias[:],
                    bc(cap[:, k:k + 2, :].rearrange("p i s -> p (i s)"), 1, 4), ALU.max, ALU.min)\
                    .then_inc(w1_done, 1)
            dve.wait_ge(o1_turned, 1)
            for b in range(B):
                o4 = ps[:, b, :].rearrange("p (h d) -> p h d", d=HR)
                r4 = rl1[:, 4 * b:4 * b + 4, :].rearrange("p g j -> p (g j)")
                link(v.tensor_scalar(r4, o4[:, :, DA], TINY, None, ALU.add))
                link(v.reciprocal(r4, r4))
                s = v.tensor_tensor(attn1[:, b, :, :], o4[:, :, 0:DA], bc(r4, 2, DA), ALU.mult)
            s.then_inc(o1_norm, 1)
            dve.wait_ge(o1_proj, 1)
            link(v.tensor_tensor(xf, ps[:, 3, 0:T], xf, ALU.add))

            layer_norm(4)
            dve.wait_ge(sa_psum, 1)
            v.tensor_tensor(v_sa[:], ps[:, 1, 0:T].rearrange("p (b d) -> p b d", b=B),
                            bc(bias_rows[:, D:2 * D], 1, B), ALU.add).then_inc(sa_v, 1)
            dve.wait_ge(sa_score, 1)
            link(v.tensor_reduce(mx_sa[:, 0, :], ps[:, 2, 0:T].rearrange("p (b s) -> p b s", b=B), AX.X, ALU.max))
            v.tensor_scalar(mx_sa[:, 1, :], mx_sa[:, 0, :], -SCALE_SA, None, ALU.mult).then_inc(sa_max, 1)
            dve.wait_ge(sa_exp, B)
            link(v.reciprocal(mx_sa[:, 3, :], mx_sa[:, 2, :]))
            dve.wait_ge(sa_out, 1)
            for b in range(B):
                s = v.scalar_tensor_tensor(x[:, b, :], ps[:, 4, b * D:(b + 1) * D], mx_sa[:, 3, b:b + 1],
                                           x[:, b, :], ALU.mult, ALU.add)
            link(s)

            layer_norm(5)
            z, ez, score, sel = (sc1[:, i, :, :] for i in range(4))
            dve.wait_ge(gt_psum, 1)
            v.tensor_copy(z, ps[:, 6, 0:B * E1].rearrange("p (b e) -> p b e", b=B)).then_inc(gt_z, 1)
            dve.wait_ge(gt_e, 1)

            def gated(i):
                n = T * (2 if 2 * i + 1 <= E1 else 1)
                dve.wait_ge(silu_done, i + 1)
                v.tensor_tensor(hT1[:, 2 * i:2 * i + n // T, :].rearrange("p e t -> p (e t)"),
                                ps[:, 2 * (i % 2) + 1, 0:n], silu_g[:, i % 2, 0:n], ALU.mult).then_inc(h1_done, 1)

            def add_expert(e):
                dve.wait_ge(y1_psum, e + 1)
                y = ps[:, down_bank(e, 0), 0:D]
                if e == E1:
                    s = v.tensor_tensor(x[:, 0, :], y, x[:, 0, :], ALU.add)
                else:
                    s = v.scalar_tensor_tensor(x[:, 0, :], y, comb[:, 0, e:e + 1], x[:, 0, :], ALU.mult, ALU.add)
                s.then_inc(y1_added, 1)
                dve.wait_ge(y1_added, e + 1)

            link(v.tensor_scalar(ez, ez, 1.0, None, ALU.add))
            link(v.reciprocal(score, ez))
            link(v.tensor_tensor(sel, score, bc(gate_b[:], 1, B), ALU.add))
            ge, gt = cmp1[:, 0, :, :, :], cmp1[:, 1, :, :, :]
            mine, other = bc(sel, 3, E1), bc(sel, 2, E1)
            v.tensor_tensor(gt, other, mine, ALU.is_gt)
            link(v.tensor_tensor(ge, other, mine, ALU.is_ge))
            gated(0)
            link(v.tensor_tensor(ge, ge, bc(below[:], 1, B), ALU.mult))
            gated(1)
            link(v.tensor_tensor(gt, gt, ge, ALU.max))
            link(v.tensor_reduce(comb[:], gt, AX.X, ALU.add))
            gated(2)
            link(v.scalar_tensor_tensor(comb[:], comb[:], TOPK - 0.5, score, ALU.is_lt, ALU.mult))
            link(v.tensor_reduce(csum[:, 0, :], comb[:], AX.X, ALU.add))
            link(v.reciprocal(csum[:, 1, :], csum[:, 0, :]))
            for b in range(B):
                s = v.tensor_scalar(comb[:, b, :], comb[:, b, :], csum[:, 1, b:b + 1], ROUTE_SCALE,
                                    ALU.mult, ALU.mult)
            s.then_inc(routed, 1)
            dve.wait_ge(routed, 1)
            for i in range(3, EP):
                gated(i)
                if i > DOWN_LAG:
                    add_expert(2 * (i - DOWN_LAG - 1))
                    add_expert(2 * (i - DOWN_LAG - 1) + 1)
            for e in range(DOWN_LAST, E1 + 1):
                add_expert(e)


N_SMALL = 11


def _rope_tables():
    inv = np.float32(10000.0) ** (-np.arange(0, DR, 2, dtype=np.float32) / np.float32(DR))
    ang = np.arange(S, dtype=np.float32)[:, None] * inv
    table = np.zeros((4, HR, 2, S), np.float32)
    table[:, :DC, 0] = 1.0
    for r in range(DR):
        table[:, DC + r, 0] = np.cos(ang[:, r // 2])
        table[:, DC + r, 1] = np.sin(ang[:, r // 2]) * (-1.0 if r % 2 == 0 else 1.0)
    return table.reshape(P, 2, S)


def _layout(a):
    ctx = a["ctx_1024"]
    swap = [1, 0, 3, 2]
    wk0_t = np.zeros((2, DH, H // 2, 2, D), np.float32)
    keys = a["L0_xattn_Wkv"][:, :H * DH].T.reshape(H // 2, 2, DH, D)
    for e in range(2):
        wk0_t[e, :, :, e] = keys[:, e].transpose(1, 0, 2)
    w_lat = np.zeros((D, P), np.float32)
    w_lat[:, 0:LAT], w_lat[:, LAT:2 * LAT] = a["L0_attn_W_DQ"], a["L0_attn_W_DKV"]
    w_lat[:, 2 * LAT:2 * LAT + DR] = a["L0_attn_W_KR"]
    w_lat[:, 2 * LAT + DR:2 * LAT + 2 * DR] = a["L0_attn_W_KR"][:, swap]
    uq = a["L0_attn_W_UQ"].reshape(LAT, 4, 4, DC)
    qr = a["L0_attn_W_QR"].reshape(LAT, 4, 4, DR)
    wq_mla = np.zeros((P, 2, 4, 4, HR), np.float32)
    wq_mla[:LAT, 0, :, :, :DC] = uq
    wq_mla[:LAT, 0, :, :, DC:DC + DR] = qr
    wq_mla[:LAT, 1, :, :, DC:DC + DR] = qr[..., swap]
    wk_mla = np.zeros((P, 5, 4, HR), np.float32)
    wk_mla[LAT:2 * LAT, :4, :, :DC] = a["L0_attn_W_UK"].reshape(LAT, 4, 4, DC)
    for r in range(DR):
        wk_mla[2 * LAT + r, :4, :, DC + r] = 1.0
        wk_mla[2 * LAT + DR + r, 4, :, DC + r] = 1.0
    wuv = np.zeros((P, D), np.float32)
    wuv[LAT:2 * LAT] = a["L0_attn_W_UV"]
    wq1 = a["L1_xattn_Wq"].T.reshape(D, 4, 1, 4 * DA)
    e = np.arange(E1)
    rows = lambda v, n: np.broadcast_to(v[None, :], (P, n))
    return {
        "x_tok": a["x"].transpose(1, 0, 2),
        "ctx_nat": ctx.reshape(B * NBLK, P, D).transpose(1, 0, 2),
        "ctx_t": ctx.reshape(B * CTX, D).T,
        "mask_t": a["mask_BxSxS2_bk0"].reshape(B, S, NBLK, P).transpose(3, 0, 2, 1).reshape(P, B * NBLK, S),
        "wq0": a["L0_xattn_Wq"],
        "wk0_t": wk0_t.reshape(P, H, D),
        "wv0": a["L0_xattn_Wkv"][:, H * DH:],
        "wo0": a["L0_xattn_Wo"].reshape(H // 2, P, D).transpose(1, 0, 2),
        "bo0": rows(a["L0_xattn_bo"], D),
        "w_lat": w_lat, "wq_mla": wq_mla.reshape(P, 2, 4, P), "wk_mla": wk_mla.reshape(P, 5, P),
        "wuv": wuv, "wo_mla": a["L0_attn_W_O"], "rope": _rope_tables(),
        "wr": a["L0_ffn_Wr"], "br": rows(a["L0_ffn_br"], E0),
        "w1": a["L0_ffn_W1"].transpose(1, 0, 2),
        "w2": a["L0_ffn_W2"].reshape(E0, NF, P, D).transpose(2, 1, 0, 3),
        "rank": rows(np.arange(E0, 0, -1, dtype=np.float32), E0),
        "wq1": np.broadcast_to(wq1, (D, 4, 4, 4 * DA)).reshape(D, 4, P),
        "wkvo1": np.stack([a["L1_xattn_Wkv"][:D].T, a["L1_xattn_Wkv"][D:].T, a["L1_xattn_Wo"].T], 1),
        "nbias": np.broadcast_to(a["L1_xattn_nbias"][None, :], (P, 1)),
        "headsel": ((np.arange(P)[:, None] % HR) // DA == np.arange(4)).astype(np.float32),
        "wqkv_sa": np.stack([a["L1_attn_W_q"], a["L1_attn_W_k"], a["L1_attn_W_v"]], 1),
        "bqk_sa": np.stack([a["L1_attn_b_q"], a["L1_attn_b_k"]], 1),
        "bv_sa": rows(a["L1_attn_b_v"], D),
        "gate_w": a["L1_ffn_gate_w"].T, "gate_b": rows(a["L1_ffn_expert_bias"], E1),
        "below": np.broadcast_to((e[None, :] < e[:, None]).astype(np.float32), (P, E1, E1)),
        "wg": np.concatenate([a["L1_ffn_w_gate"], a["L1_ffn_shared_gate_w"][None]]).transpose(2, 0, 1),
        "wu": np.concatenate([a["L1_ffn_w_up"], a["L1_ffn_shared_up_w"][None]]).transpose(2, 0, 1),
        "wd": np.concatenate([a["L1_ffn_w_down"], a["L1_ffn_shared_down_w"][None]]).transpose(2, 0, 1),
        "ident": np.eye(P, dtype=np.float32),
    }


def kernel(**inputs):
    import concourse.bacc as bacc
    from concourse.bass_utils import run_bass_kernel_spmd

    nc = bacc.Bacc("TRN2", target_bir_lowering=False, num_devices=1)
    arrays = {k: np.ascontiguousarray(v) for k, v in
              _layout({k: np.asarray(v) for k, v in inputs.items()}).items()}
    ins = {}
    for name, shape in INPUTS.items():
        a = arrays[name]
        assert a.shape == shape, (name, a.shape, shape)
        ins[name] = nc.dram_tensor(f"in_{name}", shape, mybir.dt.from_np(a.dtype), kind="ExternalInput").ap()
    out = nc.dram_tensor("out_x", (B, S, D), F32, kind="ExternalOutput").ap()
    build(nc, ins, out)
    r = run_bass_kernel_spmd(nc, [{f"in_{k}": arrays[k] for k in INPUTS}], core_ids=[0])
    return r.results[0]["out_x"]
```
